# Optimizing a Trainium2 kernel written in Bass

```python
import numpy as np
import jax
import jax.numpy as jnp

def _softmax(x, axis=-1):
    return jax.nn.softmax(x, axis=axis)

def _gelu(x):
    return jax.nn.gelu(x, approximate=True)

def _silu(x):
    return jax.nn.silu(x)

def _sigmoid(x):
    return jax.nn.sigmoid(x)

def _layernorm(x, axis=-1, eps=1e-05):
    m = jnp.mean(x, axis=axis, keepdims=True)
    v = jnp.var(x, axis=axis, keepdims=True)
    return (x - m) / jnp.sqrt(v + eps)

def _scatter_add(tgt, idx, src, axis=0):
    return tgt.at[idx].add(src)

def _segment_sum(src, seg, n):
    return jax.ops.segment_sum(src, seg, n)
kernel_name = 'mk_macaron_d2_jaxref_r8_d88f5c'

def setup_inputs(seed: int=0):
    np.random.seed(seed)
    _w = jnp.asarray

    def _L0_attn_setup():
        import jax, jax.numpy as jnp
        import numpy as np
        H, P, N, G, K, CH, E = (32, 128, 128, 8, 4, 32, 256)
        I = H * P
        CD = I + 2 * G * N
        PROJ = I + CD + H
        EPS = 1e-06

        def segsum(x):
            L = x.shape[-1]
            cs = jnp.cumsum(x, axis=-1)
            ss = cs[..., :, None] - cs[..., None, :]
            mask = jnp.tril(jnp.ones((L, L), dtype=bool))
            return jnp.where(mask, ss, -jnp.inf)
        key = jax.random.key(seed)
        ks = jax.random.split(key, 6)
        b, s = (2, 256)
        return {'x': jax.random.normal(ks[0], (b, s, E), jnp.float32), 'in_proj_w': jax.random.normal(ks[1], (PROJ, E), jnp.float32) / np.sqrt(E), 'conv_w': jax.random.normal(ks[2], (CD, 1, K), jnp.float32) / np.sqrt(K), 'conv_b': jax.random.normal(ks[3], (CD,), jnp.float32) * 0.02, 'dt_bias': jax.random.normal(ks[4], (H,), jnp.float32) * 0.1 + 1.0, 'A_log': jnp.log(jnp.arange(1, H + 1, dtype=jnp.float32)), 'D': jnp.ones((H,), jnp.float32), 'norm_w': jnp.ones((I,), jnp.float32), 'out_proj_w': jax.random.normal(ks[5], (E, I), jnp.float32) / np.sqrt(I)}
    _L0_attn_in = _L0_attn_setup()

    def _L0_ffn_setup():
        import jax, jax.numpy as jnp
        import numpy as np
        B, S, D = (4, 512, 256)
        DFF = 4 * D
        SKIP = 0.125
        key = jax.random.key(seed)
        ks = jax.random.split(key, 4)
        s_in = 1.0 / np.sqrt(D).astype(np.float32)
        s_ff = 1.0 / np.sqrt(DFF).astype(np.float32)
        return {'x': jax.random.normal(ks[0], (B, S, D), jnp.float32), 'Wr': jax.random.normal(ks[1], (D, 1), jnp.float32) * s_in, 'br': jnp.zeros((1,), jnp.float32), 'W1': jax.random.normal(ks[2], (D, DFF), jnp.float32) * s_in, 'b1': jnp.zeros((DFF,), jnp.float32), 'W2': jax.random.normal(ks[3], (DFF, D), jnp.float32) * s_ff, 'b2': jnp.zeros((D,), jnp.float32)}
    _L0_ffn_in = _L0_ffn_setup()

    def _L1_attn_setup():
        import jax, jax.numpy as jnp
        import numpy as np
        INFTY_APPROX = 1e+30
        ROTARY_BASE = 10000.0
        ATTN_SCALE = 1.0 / 128.0

        def rope(x):
            T, D = (x.shape[-2], x.shape[-1])
            half = D // 2
            pos = jnp.arange(T, dtype=jnp.float32)[:, None]
            freqs = jnp.power(ROTARY_BASE, -jnp.arange(half, dtype=jnp.float32) / half)[None, :]
            rad = pos * freqs
            cos = jnp.cos(rad).astype(x.dtype)
            sin = jnp.sin(rad).astype(x.dtype)
            even, odd = jnp.split(x, 2, axis=-1)
            r_even = even * cos - odd * sin
            r_odd = even * sin + odd * cos
            return jnp.concatenate([r_even, r_odd], axis=-1)
        key = jax.random.key(seed)
        ks = jax.random.split(key, 5)
        B, T, M, H, D = (2, 256, 256, 16, 128)
        stddev = M ** (-0.5)
        return {'x': jax.random.normal(ks[0], (B, T, M), dtype=jnp.float32), 'wq': stddev * jax.random.normal(ks[1], (M, H, D), dtype=jnp.float32), 'wk': stddev * jax.random.normal(ks[2], (M, H, D), dtype=jnp.float32), 'wv': stddev * jax.random.normal(ks[3], (M, H, D), dtype=jnp.float32), 'wo': stddev * jax.random.normal(ks[4], (H, D, M), dtype=jnp.float32)}
    _L1_attn_in = _L1_attn_setup()

    def _L1_ffn_setup():
        import jax, jax.numpy as jnp
        import numpy as np
        EPS = 1e-06
        K_STEPS = 4
        USE_GATING = True

        def layer_norm(x, gamma, beta):
            mu = jnp.mean(x, axis=-1, keepdims=True)
            var = jnp.mean(jnp.square(x - mu), axis=-1, keepdims=True)
            return (x - mu) * jax.lax.rsqrt(var + EPS) * gamma + beta
        key = jax.random.key(seed)
        B, L, D, H = (4, 512, 256, 1024)
        ks = jax.random.split(key, 16)
        s = 0.02
        return {'x': jax.random.normal(ks[0], (B, L, D), dtype=jnp.float32), 'in_gamma': jnp.ones((D,), jnp.float32), 'in_beta': jnp.zeros((D,), jnp.float32), 'agg_w': jax.random.normal(ks[1], (D, D), jnp.float32) * s, 'agg_b': jnp.zeros((D,), jnp.float32), 'pn_gamma': jnp.ones((D,), jnp.float32), 'pn_beta': jnp.zeros((D,), jnp.float32), 'd1_w': jax.random.normal(ks[2], (D, H), jnp.float32) * s, 'd1_b': jnp.zeros((H,), jnp.float32), 'd2_w': jax.random.normal(ks[3], (H, D), jnp.float32) * s, 'd2_b': jnp.zeros((D,), jnp.float32), 'bc_w': jax.random.normal(ks[4], (D, D), jnp.float32) * s, 'bc_b': jnp.zeros((D,), jnp.float32), 'gate_w': jax.random.normal(ks[5], (D, D), jnp.float32) * s, 'gate_b': jnp.zeros((D,), jnp.float32), 'out_gamma': jnp.ones((D,), jnp.float32), 'out_beta': jnp.zeros((D,), jnp.float32)}
    _L1_ffn_in = _L1_ffn_setup()
    _d = {'L0_attn_x': _L0_attn_in['x'], 'L0_attn_in_proj_w': _L0_attn_in['in_proj_w'], 'L0_attn_conv_w': _L0_attn_in['conv_w'], 'L0_attn_conv_b': _L0_attn_in['conv_b'], 'L0_attn_dt_bias': _L0_attn_in['dt_bias'], 'L0_attn_A_log': _L0_attn_in['A_log'], 'L0_attn_D': _L0_attn_in['D'], 'L0_attn_norm_w': _L0_attn_in['norm_w'], 'L0_attn_out_proj_w': _L0_attn_in['out_proj_w'], 'L0_ffn_Wr': _L0_ffn_in['Wr'], 'L0_ffn_br': _L0_ffn_in['br'], 'L0_ffn_W1': _L0_ffn_in['W1'], 'L0_ffn_b1': _L0_ffn_in['b1'], 'L0_ffn_W2': _L0_ffn_in['W2'], 'L0_ffn_b2': _L0_ffn_in['b2'], 'L1_attn_wq': _L1_attn_in['wq'], 'L1_attn_wk': _L1_attn_in['wk'], 'L1_attn_wv': _L1_attn_in['wv'], 'L1_attn_wo': _L1_attn_in['wo'], 'L1_ffn_in_gamma': _L1_ffn_in['in_gamma'], 'L1_ffn_in_beta': _L1_ffn_in['in_beta'], 'L1_ffn_agg_w': _L1_ffn_in['agg_w'], 'L1_ffn_agg_b': _L1_ffn_in['agg_b'], 'L1_ffn_pn_gamma': _L1_ffn_in['pn_gamma'], 'L1_ffn_pn_beta': _L1_ffn_in['pn_beta'], 'L1_ffn_d1_w': _L1_ffn_in['d1_w'], 'L1_ffn_d1_b': _L1_ffn_in['d1_b'], 'L1_ffn_d2_w': _L1_ffn_in['d2_w'], 'L1_ffn_d2_b': _L1_ffn_in['d2_b'], 'L1_ffn_bc_w': _L1_ffn_in['bc_w'], 'L1_ffn_bc_b': _L1_ffn_in['bc_b'], 'L1_ffn_gate_w': _L1_ffn_in['gate_w'], 'L1_ffn_gate_b': _L1_ffn_in['gate_b'], 'L1_ffn_out_gamma': _L1_ffn_in['out_gamma'], 'L1_ffn_out_beta': _L1_ffn_in['out_beta']}
    _x0 = _d['L0_attn_x']
    _d['L0_attn_x'] = jax.random.normal(jax.random.fold_in(jax.random.key(seed), 1), (1, 1024, 256), dtype=_x0.dtype)
    del _x0
    return _d

def reference(L0_attn_x, L0_attn_in_proj_w, L0_attn_conv_w, L0_attn_conv_b, L0_attn_dt_bias, L0_attn_A_log, L0_attn_D, L0_attn_norm_w, L0_attn_out_proj_w, L0_ffn_Wr, L0_ffn_br, L0_ffn_W1, L0_ffn_b1, L0_ffn_W2, L0_ffn_b2, L1_attn_wq, L1_attn_wk, L1_attn_wv, L1_attn_wo, L1_ffn_in_gamma, L1_ffn_in_beta, L1_ffn_agg_w, L1_ffn_agg_b, L1_ffn_pn_gamma, L1_ffn_pn_beta, L1_ffn_d1_w, L1_ffn_d1_b, L1_ffn_d2_w, L1_ffn_d2_b, L1_ffn_bc_w, L1_ffn_bc_b, L1_ffn_gate_w, L1_ffn_gate_b, L1_ffn_out_gamma, L1_ffn_out_beta):

    def _L0_attn_ref(x, in_proj_w, conv_w, conv_b, dt_bias, A_log, D, norm_w, out_proj_w):
        import jax, jax.numpy as jnp
        import numpy as np
        H, P, N, G, K, CH, E = (32, 128, 128, 8, 4, 32, 256)
        I = H * P
        CD = I + 2 * G * N
        PROJ = I + CD + H
        EPS = 1e-06

        def segsum(x):
            L = x.shape[-1]
            cs = jnp.cumsum(x, axis=-1)
            ss = cs[..., :, None] - cs[..., None, :]
            mask = jnp.tril(jnp.ones((L, L), dtype=bool))
            return jnp.where(mask, ss, -jnp.inf)
        b, s, _ = x.shape
        proj = x @ in_proj_w.T
        gate, hbc, dt = jnp.split(proj, [I, I + CD], axis=-1)
        hbc_t = jnp.transpose(hbc, (0, 2, 1))
        conv = jax.lax.conv_general_dilated(hbc_t, conv_w, window_strides=(1,), padding=[(K - 1, 0)], feature_group_count=CD, dimension_numbers=('NCH', 'OIH', 'NCH'))
        hbc = jax.nn.silu(jnp.transpose(conv + conv_b[None, :, None], (0, 2, 1)))
        hs, B, C = jnp.split(hbc, [I, I + G * N], axis=-1)
        A = -jnp.exp(A_log.astype(jnp.float32))
        dt = jax.nn.softplus(dt.astype(jnp.float32) + dt_bias)
        dt = jnp.clip(dt, 0.0, None)
        X = hs.reshape(b, s, H, P).astype(jnp.float32)
        B = jnp.tile(B.reshape(b, s, G, N).astype(jnp.float32), (1, 1, H // G, 1))
        C = jnp.tile(C.reshape(b, s, G, N).astype(jnp.float32), (1, 1, H // G, 1))
        D_res = D[:, None] * X
        X = X * dt[..., None]
        A_bt = A * dt
        nc = s // CH
        Xc = X.reshape(b, nc, CH, H, P)
        Bc = B.reshape(b, nc, CH, H, N)
        Cc = C.reshape(b, nc, CH, H, N)
        Ac = jnp.transpose(A_bt.reshape(b, nc, CH, H), (0, 3, 1, 2))
        A_cum = jnp.cumsum(Ac, axis=-1)
        Lmat = jnp.exp(segsum(Ac))
        Y_diag = jnp.einsum('bclhn,bcshn,bhcls,bcshd->bclhd', Cc, Bc, Lmat, Xc)
        decay_states = jnp.exp(A_cum[..., -1:] - A_cum)
        states = jnp.einsum('bclhn,bhcl,bclhd->bchdn', Bc, decay_states, Xc)
        states = jnp.concatenate([jnp.zeros_like(states[:, :1]), states], axis=1)
        A_last = jnp.pad(A_cum[..., -1], ((0, 0), (0, 0), (1, 0)))
        decay_chunk = jnp.exp(segsum(A_last))
        new_states = jnp.einsum('bhij,bjhdn->bihdn', decay_chunk, states)
        states_prev = new_states[:, :-1]
        state_decay = jnp.exp(A_cum)
        Y_off = jnp.einsum('bclhn,bchdn,bhcl->bclhd', Cc, states_prev, state_decay)
        y = (Y_diag + Y_off).reshape(b, s, H, P) + D_res
        y = y.reshape(b, s, I)
        gs = I // G
        h32 = y * jax.nn.silu(gate.astype(jnp.float32))
        g = h32.reshape(b, s, I // gs, gs)
        var = jnp.mean(g * g, axis=-1, keepdims=True)
        h32 = (g * jax.lax.rsqrt(var + EPS)).reshape(b, s, I)
        return norm_w * h32 @ out_proj_w.T

    def _L0_ffn_ref(x, Wr, br, W1, b1, W2, b2):
        import jax, jax.numpy as jnp
        import numpy as np
        B, S, D = (4, 512, 256)
        DFF = 4 * D
        SKIP = 0.125
        Bs, Ss, Ds = x.shape
        k = max(int(Ss * SKIP), 1)
        logits = (x @ Wr + br)[..., 0]
        weights, idx = jax.lax.top_k(logits, k)
        perm = jnp.argsort(idx, axis=1)
        tokens = jnp.take_along_axis(idx, perm, axis=1)
        fx = jnp.take_along_axis(x, tokens[..., None], axis=1)
        h = jax.nn.gelu(fx @ W1 + b1, approximate=False)
        out_l = h @ W2 + b2
        tw = jax.nn.softmax(weights, axis=1)
        rw = jnp.take_along_axis(tw, perm, axis=1)
        xw = rw[..., None] * out_l
        bidx = jnp.arange(Bs)[:, None]
        return x.at[bidx, tokens].add(xw)

    def _L1_attn_ref(x, wq, wk, wv, wo):
        import jax, jax.numpy as jnp
        import numpy as np
        INFTY_APPROX = 1e+30
        ROTARY_BASE = 10000.0
        ATTN_SCALE = 1.0 / 128.0

        def rope(x):
            T, D = (x.shape[-2], x.shape[-1])
            half = D // 2
            pos = jnp.arange(T, dtype=jnp.float32)[:, None]
            freqs = jnp.power(ROTARY_BASE, -jnp.arange(half, dtype=jnp.float32) / half)[None, :]
            rad = pos * freqs
            cos = jnp.cos(rad).astype(x.dtype)
            sin = jnp.sin(rad).astype(x.dtype)
            even, odd = jnp.split(x, 2, axis=-1)
            r_even = even * cos - odd * sin
            r_odd = even * sin + odd * cos
            return jnp.concatenate([r_even, r_odd], axis=-1)
        T = x.shape[1]
        q = jnp.einsum('bim,mhd->bhid', x, wq)
        k = jnp.einsum('bim,mhd->bhid', x, wk)
        v = jnp.einsum('bim,mhd->bhid', x, wv)
        q = rope(q)
        k = rope(k)
        mult = jnp.asarray(ATTN_SCALE ** 0.5, dtype=x.dtype)
        s = jnp.einsum('bhid,bhjd->bhij', q * mult, k * mult)
        i = jnp.arange(T)[:, None]
        j = jnp.arange(T)[None, :]
        mask = jnp.less(i, j).astype(s.dtype)[None, None, :, :]
        s = s - jnp.asarray(INFTY_APPROX, dtype=s.dtype) * mask
        p = jax.nn.softmax(s, axis=-1)
        o = jnp.einsum('bhij,bhjd->bhid', p, v)
        r = jnp.einsum('bhid,hdm->bim', o, wo)
        return r

    def _L1_ffn_ref(x, in_gamma, in_beta, agg_w, agg_b, pn_gamma, pn_beta, d1_w, d1_b, d2_w, d2_b, bc_w, bc_b, gate_w, gate_b, out_gamma, out_beta):
        import jax, jax.numpy as jnp
        import numpy as np
        EPS = 1e-06
        K_STEPS = 4
        USE_GATING = True

        def layer_norm(x, gamma, beta):
            mu = jnp.mean(x, axis=-1, keepdims=True)
            var = jnp.mean(jnp.square(x - mu), axis=-1, keepdims=True)
            return (x - mu) * jax.lax.rsqrt(var + EPS) * gamma + beta
        x_norm = layer_norm(x, in_gamma, in_beta)
        thought = x_norm[:, -1, :] @ agg_w + agg_b
        for _ in range(K_STEPS):
            t = layer_norm(thought, pn_gamma, pn_beta)
            t = jax.nn.gelu(t @ d1_w + d1_b, approximate=False)
            thought = thought + (t @ d2_w + d2_b)
        broadcast = (thought @ bc_w + bc_b)[:, None, :]
        if USE_GATING:
            gate = jax.nn.sigmoid(x @ gate_w + gate_b)
            out = x + gate * broadcast
        else:
            out = x + broadcast
        return layer_norm(out, out_gamma, out_beta)
    x = L0_attn_x
    x = x + 0.5 * _L0_ffn_ref(_layernorm(x, axis=-1), L0_ffn_Wr, L0_ffn_br, L0_ffn_W1, L0_ffn_b1, L0_ffn_W2, L0_ffn_b2)
    x = x + _L0_attn_ref(_layernorm(x, axis=-1), L0_attn_in_proj_w, L0_attn_conv_w, L0_attn_conv_b, L0_attn_dt_bias, L0_attn_A_log, L0_attn_D, L0_attn_norm_w, L0_attn_out_proj_w)
    x = x + 0.5 * _L0_ffn_ref(_layernorm(x, axis=-1), L0_ffn_Wr, L0_ffn_br, L0_ffn_W1, L0_ffn_b1, L0_ffn_W2, L0_ffn_b2)
    x = x + 0.5 * _L1_ffn_ref(_layernorm(x, axis=-1), L1_ffn_in_gamma, L1_ffn_in_beta, L1_ffn_agg_w, L1_ffn_agg_b, L1_ffn_pn_gamma, L1_ffn_pn_beta, L1_ffn_d1_w, L1_ffn_d1_b, L1_ffn_d2_w, L1_ffn_d2_b, L1_ffn_bc_w, L1_ffn_bc_b, L1_ffn_gate_w, L1_ffn_gate_b, L1_ffn_out_gamma, L1_ffn_out_beta)
    x = x + _L1_attn_ref(_layernorm(x, axis=-1), L1_attn_wq, L1_attn_wk, L1_attn_wv, L1_attn_wo)
    x = x + 0.5 * _L1_ffn_ref(_layernorm(x, axis=-1), L1_ffn_in_gamma, L1_ffn_in_beta, L1_ffn_agg_w, L1_ffn_agg_b, L1_ffn_pn_gamma, L1_ffn_pn_beta, L1_ffn_d1_w, L1_ffn_d1_b, L1_ffn_d2_w, L1_ffn_d2_b, L1_ffn_bc_w, L1_ffn_bc_b, L1_ffn_gate_w, L1_ffn_gate_b, L1_ffn_out_gamma, L1_ffn_out_beta)
    return x

_drawn_inputs = setup_inputs


def setup_inputs(seed=0):
    import zlib

    import numpy as np

    out = dict(_drawn_inputs(seed))
    spreads = {'L0_attn_D': (1.0, 0.6),
     'L0_attn_norm_w': (1.0, 0.2),
     'L0_ffn_b1': (0.0, 0.8),
     'L0_ffn_b2': (0.0, 2.0),
     'L1_ffn_in_gamma': (1.0, 0.6),
     'L1_ffn_in_beta': (0.0, 2.0),
     'L1_ffn_agg_b': (0.0, 0.645),
     'L1_ffn_pn_gamma': (1.0, 0.6),
     'L1_ffn_pn_beta': (0.0, 0.8),
     'L1_ffn_d1_b': (0.0, 0.8),
     'L1_ffn_d2_b': (0.0, 0.316),
     'L1_ffn_bc_b': (0.0, 0.424),
     'L1_ffn_gate_b': (0.0, 0.8),
     'L1_ffn_out_gamma': (1.0, 0.2),
     'L1_ffn_out_beta': (0.0, 0.1)}
    factors = {'L0_attn_conv_b': 3.519,
     'L0_attn_dt_bias': 2.983,
     'L0_ffn_Wr': 4.312,
     'L0_ffn_W1': 3.357,
     'L0_ffn_W2': 3.171,
     'L1_attn_wq': 7.407,
     'L1_attn_wk': 7.344,
     'L1_ffn_gate_w': 8.0}
    for name, (base, spread) in spreads.items():
        noise = np.random.default_rng([zlib.crc32(name.encode()), seed]).standard_normal(out[name].shape)
        drawn = base * np.exp(spread * noise) if base else spread * noise
        out[name] = jnp.asarray(drawn.astype(out[name].dtype))
    for name, factor in factors.items():
        out[name] = (out[name] * factor).astype(out[name].dtype)
    return out
```

```python
from contextlib import ExitStack

import concourse.bass as bass
from concourse import mybir

F32 = mybir.dt.float32
ALU = mybir.AluOpType
ACT = mybir.ActivationFunctionType
AX = mybir.AxisListType

P = 128
T = 1024
E = 256
NT = T // P
KT = E // P
TOPK = P
DFF = 1024
FT = DFF // P
HM, GM = 32, 8
CONV = 4
XTILE, BTILE, CTILE = HM, 2 * HM, 2 * HM + GM
CW = CONV + 1
NH = 16
HALF = T // 2
BANK = 512
ATTN_SCALE = 1.0 / 128.0
NEG = -1e30


def build(nc, A, out):
    with ExitStack() as ctx:
        open_sems = []

        def sems(phase, names):
            S = {n: nc.alloc_semaphore(phase + "_" + n) for n in names.split()}
            open_sems.extend(S.values())
            return S

        def end_phase():
            nc.clear_and_free_semaphores(list(open_sems))
            open_sems.clear()
            nc.all_engine_barrier()

        def sb(name, cols):
            return ctx.enter_context(nc.sbuf_tensor(name, [P, cols], F32))

        x_sb = sb("x_sb", NT * E)
        xn_sb = sb("xn_sb", NT * E)
        xnT_sb = sb("xnT_sb", KT * T)
        X = x_sb[:, :].rearrange("p (t e) -> p t e", t=NT)
        XN = xn_sb[:, :].rearrange("p (t e) -> p t e", t=NT)
        XNT = xnT_sb[:, :].rearrange("p (k t) -> p k t", k=KT)
        ident = sb("ident", P)
        ones = sb("ones", P)
        upto = sb("upto", P)
        after = sb("after", P)
        slots = sb("slots", P)
        causal = sb("causal", P)
        ARENA = 46200
        arena = sb("arena", ARENA)
        psum = ctx.enter_context(nc.psum_tensor("psum", [P, 8 * BANK], F32))

        class Region:

            def __init__(self):
                self.at = 0

            def __call__(self, cols):
                self.at += cols
                assert self.at <= ARENA, self.at
                return arena[:, self.at - cols:self.at]

        def bank(b, n=1):
            return psum[:, b * BANK:(b + n) * BANK]

        def row(ap):
            return ap.rearrange("(a d) -> a d", a=1).to_broadcast([P, ap.shape[0]])

        def proj(pe, dst, lhs, rhs, n):
            for k in range(n):
                last = pe.matmul(dst, lhs(k), rhs(k), start=(k == 0), stop=(k == n - 1))
            return last

        def credit(g, spare, pairs):
            for i, (s, n) in enumerate(pairs):
                g.memset(spare[:, i:i + 1], 0.0).then_inc(s, n)

        LN = "stats aggr ve sd rstd xn tr xnT"

        def ln_region(take):
            return {"st": take(NT * 6).rearrange("p (t s) -> p t s", t=NT),
                    "mv": take(NT * 2).rearrange("p (t s) -> p t s", t=NT),
                    "ve": take(NT), "sd": take(NT), "rstd": take(NT)}

        def ln_dve(v, S, M, src, dst, eps, tiles=NT):
            for t in range(tiles):
                v.bn_stats(M["st"][:, t, :], src[:, t, :]).then_inc(S["stats"], 1)
            v.wait_ge(S["stats"], tiles)
            for t in range(tiles):
                v.bn_aggr(M["mv"][:, t, :], M["st"][:, t, :]).then_inc(S["aggr"], 1)
            v.wait_ge(S["aggr"], tiles)
            v.tensor_scalar(M["ve"], M["mv"][:, :, 1], eps, None, ALU.add).then_inc(S["ve"], 1)
            v.wait_ge(S["sd"], 1)
            v.reciprocal(M["rstd"], M["sd"]).then_inc(S["rstd"], 1)
            v.wait_ge(S["rstd"], 1)
            for t in range(tiles):
                v.tensor_scalar(dst[:, t, :], src[:, t, :], M["mv"][:, t, 0:1], M["rstd"][:, t:t + 1],
                                ALU.subtract, ALU.mult).then_inc(S["xn"], 1)

        def ln_sqrt(act, S, M):
            act.wait_ge(S["ve"], 1)
            nc.scalar.activation(M["sd"], M["ve"], ACT.Sqrt).then_inc(S["sd"], 1)

        def ln_pe(pe, S):
            for g in range(NT // 2):
                pe.wait_ge(S["xn"], 2 * g + 2)
                if g >= 2:
                    pe.wait_ge(S["xnT"], g - 1)
                for k in range(KT):
                    for h in range(2):
                        last = pe.transpose(bank(g % 2)[:, (2 * k + h) * P:(2 * k + h + 1) * P],
                                            XN[:, 2 * g + h, k * P:(k + 1) * P], ident[:, :])
                last.then_inc(S["tr"], 1)

        def ln_copy(act, S):
            for g in range(NT // 2):
                act.wait_ge(S["tr"], g + 1)
                nc.scalar.copy(XNT[:, :, 2 * g * P:(2 * g + 2) * P],
                               bank(g % 2).rearrange("p (k t) -> p k t", k=KT)).then_inc(S["xnT"], 1)

        def topk_ffn(name, first):
            take = Region()
            S = sems(name, LN + " w r x const wr lcol lb ltr lmax rank rk sel selT seltr selTev wexp wz zs z rz cw"
                     " g gc up hT dn ol sc res half prod")
            M = ln_region(take)
            w1 = take(KT * DFF).rearrange("p (k f) -> p k f", k=KT)
            w2 = take(FT * E).rearrange("p (k e) -> p k e", k=FT)
            b1 = take(FT)
            b2, wr, br = take(E), take(E), take(1)
            lcol, lbc = take(NT), take(T).rearrange("p (t q) -> p t q", t=NT)
            junk = take(T)
            parts = take(3 * NT).rearrange("p (a t) -> p a t", a=3)
            rank, rank2, mask = take(NT), take(NT), take(NT)
            sel = take(NT * TOPK).rearrange("p (t s) -> p t s", t=NT)
            selT = take(NT * TOPK).rearrange("p (t s) -> p t s", t=NT)
            nmax, wexp, wz, zz, rz, cw = take(1), take(NT), take(NT), take(1), take(1), take(NT)
            fxT = take(KT * TOPK).rearrange("p (k s) -> p k s", k=KT)
            hT = take(FT * TOPK).rearrange("p (k s) -> p k s", k=FT)
            outl = take(E)
            prod2 = take(E * NT)
            prod = prod2.rearrange("p (t e) -> p t e", t=NT)

            with nc.Block() as block:
                @block.sync
                def _(sp):
                    if first:
                        for t in range(NT):
                            sp.dma_start(X[:, t, :], A["x"][t * P:(t + 1) * P, :]).then_inc(S["x"], 16)
                    sp.dma_start(wr, row(A["Wr"])).then_inc(S["r"], 16)
                    sp.dma_start(br, row(A["br"])).then_inc(S["r"], 16)
                    sp.dma_start(b2, row(A["b2"])).then_inc(S["r"], 16)
                    sp.dma_start(b1, A["b1"]).then_inc(S["r"], 16)
                    sp.dma_start(w1, A["W1"].rearrange("(k p) f -> p k f", p=P)).then_inc(S["w"], 16)
                    sp.dma_start(w2, A["W2"].rearrange("(k p) e -> p k e", p=P)).then_inc(S["w"], 16)

                if first:
                    @block.gpsimd
                    def _(g):
                        g.memset(ones[:, :], 1.0).then_inc(S["const"], 1)
                        g.memset(causal[:, :], 0.0).then_inc(S["const"], 1)
                        g.iota(slots[:, :], pattern=[[1, P]], base=0, channel_multiplier=0,
                               allow_small_or_imprecise_dtypes=True).then_inc(S["const"], 1)
                        g.wait_ge(S["const"], 3)
                        g.affine_select(out=ident[:, :], in_=ones[:, :], compare_op=ALU.is_equal, fill=0.0, base=0,
                                        pattern=[[-1, P]], channel_multiplier=1).then_inc(S["const"], 1)
                        g.affine_select(out=upto[:, :], in_=ones[:, :], compare_op=ALU.is_ge, fill=0.0, base=0,
                                        pattern=[[1, P]], channel_multiplier=-1).then_inc(S["const"], 1)
                        g.affine_select(out=after[:, :], in_=ones[:, :], compare_op=ALU.is_gt, fill=0.0, base=0,
                                        pattern=[[-1, P]], channel_multiplier=1).then_inc(S["const"], 1)
                        g.affine_select(out=causal[:, :], in_=causal[:, :], compare_op=ALU.is_ge, fill=NEG, base=0,
                                        pattern=[[-1, P]], channel_multiplier=1).then_inc(S["const"], 1)

                @block.vector
                def _(v):
                    if first:
                        v.wait_ge(S["x"], 16 * NT)
                    ln_dve(v, S, M, X, XN, 1e-5)
                    v.wait_ge(S["r"], 64)
                    v.wait_ge(S["xn"], NT)
                    for t in range(NT):
                        v.tensor_tensor(prod[:, t, :], XN[:, t, :], wr, ALU.mult).then_inc(S["prod"], 1)
                    v.wait_ge(S["prod"], NT)
                    v.tensor_reduce(lcol, prod, AX.X, ALU.add).then_inc(S["wr"], 1)
                    v.wait_ge(S["wr"], 1)
                    v.tensor_scalar(lcol, lcol, br[:, 0:1], None, ALU.add).then_inc(S["lcol"], 1)
                    v.wait_ge(S["lcol"], 1)
                    v.tensor_copy(lbc, lcol.unsqueeze(2).to_broadcast([P, NT, P])).then_inc(S["lb"], 1)
                    v.wait_ge(S["ltr"], 1)
                    lrow = bank(2, 2)
                    v.tensor_reduce(nmax, lrow, AX.X, ALU.max, negate=True).then_inc(S["lmax"], 1)
                    v.memset(parts[:, 0, 0:1], 0.0).then_inc(S["rank"], 1)
                    for t in range(NT):
                        v.wait_ge(S["rank"], 3 * t if t else 1)
                        if t:
                            v.tensor_scalar(junk[:, 0:t * P], lrow[:, 0:t * P], lcol[:, t:t + 1], 0.0, ALU.is_ge,
                                            ALU.add, accum_out=parts[:, 0, t:t + 1]).then_inc(S["rank"], 1)
                        v.tensor_scalar(prod2[:, 0:T - t * P], lrow[:, t * P:T], lcol[:, t:t + 1], 0.0, ALU.is_gt,
                                        ALU.add, accum_out=parts[:, 1, t:t + 1]).then_inc(S["rank"], 1)
                        v.scalar_tensor_tensor(prod2[:, T:T + P], lrow[:, t * P:(t + 1) * P], lcol[:, t:t + 1],
                                               after[:, :], ALU.is_equal, ALU.mult,
                                               accum_out=parts[:, 2, t:t + 1]).then_inc(S["rank"], 1)
                    v.wait_ge(S["rank"], 3 * NT)
                    v.tensor_tensor(rank2, parts[:, 0, :], parts[:, 1, :], ALU.add).then_inc(S["rk"], 1)
                    v.wait_ge(S["rk"], 1)
                    v.tensor_tensor(rank, rank2, parts[:, 2, :], ALU.add).then_inc(S["rk"], 1)
                    v.wait_ge(S["rk"], 2)
                    for t in range(NT):
                        v.tensor_scalar(sel[:, t, :], slots[:, :], rank[:, t:t + 1], None,
                                        ALU.is_equal).then_inc(S["sel"], 1)
                    v.tensor_scalar(mask, rank, float(TOPK), None, ALU.is_lt).then_inc(S["rk"], 1)
                    v.wait_ge(S["wexp"], 1)
                    v.wait_ge(S["rk"], 3)
                    v.tensor_tensor(wz, wexp, mask, ALU.mult).then_inc(S["wz"], 1)
                    v.wait_ge(S["zs"], 1)
                    v.tensor_reduce(zz, bank(4)[:, 0:NT], AX.X, ALU.add).then_inc(S["z"], 1)
                    v.wait_ge(S["z"], 1)
                    v.reciprocal(rz, zz).then_inc(S["rz"], 1)
                    v.wait_ge(S["rz"], 1)
                    v.tensor_scalar(cw, wexp, rz[:, 0:1], 0.5, ALU.mult, ALU.mult).then_inc(S["cw"], 1)
                    v.wait_ge(S["g"], 1)
                    v.tensor_copy(fxT, bank(5)[:, 0:KT * TOPK].rearrange("p (k s) -> p k s", k=KT)).then_inc(S["gc"], 1)
                    for g in range(2):
                        v.wait_ge(S["seltr"], g + 1)
                        v.tensor_copy(selT[:, 4 * g:4 * g + 4, :],
                                      bank(6 + g).rearrange("p (t s) -> p t s", t=4)).then_inc(S["selTev"], 1)
                    for t in range(NT):
                        v.scalar_tensor_tensor(X[:, t, :], XN[:, t, :], 0.5, X[:, t, :], ALU.mult,
                                               ALU.add).then_inc(S["half"], 1)
                    v.wait_ge(S["dn"], 1)
                    v.tensor_tensor(outl, bank(2)[:, 0:E], b2, ALU.add).then_inc(S["ol"], 1)
                    v.wait_ge(S["half"], NT)
                    v.wait_ge(S["cw"], 1)
                    for t in range(NT):
                        v.wait_ge(S["sc"], t + 1)
                        v.scalar_tensor_tensor(X[:, t, :], bank(4 + t % 2)[:, 0:E], cw[:, t:t + 1], X[:, t, :],
                                               ALU.mult, ALU.add).then_inc(S["res"], 1)

                @block.scalar
                def _(act):
                    ln_sqrt(act, S, M)
                    act.wait_ge(S["lmax"], 1)
                    nc.scalar.activation(wexp, lcol, ACT.Exp, bias=nmax[:, 0:1]).then_inc(S["wexp"], 1)
                    for f in range(FT):
                        act.wait_ge(S["up"], f + 1)
                        nc.scalar.activation(hT[:, f, :], bank(2 + f % 2)[:, 0:TOPK], ACT.Gelu,
                                             bias=b1[:, f:f + 1]).then_inc(S["hT"], 1)

                @block.tensor
                def _(pe):
                    if first:
                        pe.wait_ge(S["const"], 7)
                    pe.wait_ge(S["lb"], 1)
                    for t in range(NT):
                        last = pe.transpose(bank(2, 2)[:, t * P:(t + 1) * P], lbc[:, t, :], ident[:, :])
                    last.then_inc(S["ltr"], 1)
                    pe.wait_ge(S["sel"], NT)
                    for k in range(KT):
                        last = proj(pe, bank(5)[:, k * TOPK:(k + 1) * TOPK],
                                    lambda t: XN[:, t, k * P:(k + 1) * P], lambda t: sel[:, t, :], NT)
                    last.then_inc(S["g"], 1)
                    for t in range(NT):
                        last = pe.transpose(bank(6 + t // 4)[:, t % 4 * P:(t % 4 + 1) * P], sel[:, t, :], ident[:, :])
                        if t % 4 == 3:
                            last.then_inc(S["seltr"], 1)
                    pe.wait_ge(S["wz"], 1)
                    pe.matmul(bank(4)[:, 0:NT], ones[:, :], wz, start=True, stop=True).then_inc(S["zs"], 1)
                    pe.wait_ge(S["gc"], 1)
                    pe.wait_ge(S["w"], 32)
                    pe.wait_ge(S["rank"], 3 * NT)
                    for f in range(FT):
                        if f >= 2:
                            pe.wait_ge(S["hT"], f - 1)
                        proj(pe, bank(2 + f % 2)[:, 0:TOPK], lambda k: w1[:, k, f * P:(f + 1) * P],
                             lambda k: fxT[:, k, :], KT).then_inc(S["up"], 1)
                    pe.wait_ge(S["hT"], FT)
                    proj(pe, bank(2)[:, 0:E], lambda k: hT[:, k, :], lambda k: w2[:, k, :], FT).then_inc(S["dn"], 1)
                    pe.wait_ge(S["selTev"], 2)
                    pe.wait_ge(S["ol"], 1)
                    pe.wait_ge(S["z"], 1)
                    for t in range(NT):
                        if t >= 2:
                            pe.wait_ge(S["res"], t - 1)
                        pe.matmul(bank(4 + t % 2)[:, 0:E], selT[:, t, :], outl, start=True, stop=True).then_inc(S["sc"], 1)

        def mamba():
            take = Region()
            BTOK = take(GM * T).rearrange("p (g c n) -> p g c n", g=GM, c=NT)
            CT = take(GM * T).rearrange("p (g t) -> p g t", g=GM)
            CB = take(GM * T).rearrange("p (g t) -> p g t", g=GM)
            cwt = take((HM + 2 * GM) * CW).rearrange("p (n w) -> p n w", w=CW)
            dt, cum, dend, etot = (take(HM * NT) for _ in range(4))
            nw = take(HM)
            dskip = take(HM)
            spare = take(32)
            wx = take(2 * E).rearrange("p (b k c) -> p b k c", b=2, k=KT)
            raw = take(T + CONV - 1)
            xT = take(2 * T).rearrange("p (b t) -> p b t", b=2)
            common = take.at

            def col(ap, i):
                return ap[:, bass.ds(i, 1)]

            def tap_of(tile, w):
                return cwt[:, bass.ds(tile, 1), w:w + 1].rearrange("p o w -> p (o w)")

            def conv_taps(v, S, b, n, tile):
                v.wait_ge(S["c"], n + 2)
                for w in range(CONV - 1):
                    if w:
                        v.wait_ge(S["tap"], n * (CONV - 2) + w)
                    v.scalar_tensor_tensor(xT[:, b, :], raw[:, w:w + T], tap_of(tile, w), xT[:, b, :], ALU.mult,
                                           ALU.add).then_inc(S["tap"] if w < CONV - 2 else S["conv"], 1)

            def conv_newest(act, S, b, tile):
                nc.scalar.copy(raw[:, CONV - 1:], bank(0, 2)).then_inc(S["raw"], 1)
                nc.scalar.activation(xT[:, b, :], bank(0, 2), ACT.Identity, bias=tap_of(tile, CONV),
                                     scale=tap_of(tile, CONV - 1)).then_inc(S["c"], 1)

            def channels(pe, w):
                for h in range(2):
                    last = proj(pe, bank(h), lambda k: w[:, k, :], lambda k: XNT[:, k, h * HALF:(h + 1) * HALF], KT)
                return last

            S2 = sems("mb", "w0 w1 pj raw c tap conv xt bt btok cbp cb")
            S3 = sems("mm", "wx0 wx1 wg0 wg1 cr0 cr1 wo px pg raw c tap conv xt tx xd xs ds rc st ec cs df lm mm"
                      " y yd sg u sqs ad vr vv sd rr wos op oc")

            M = ln_region(take)
            wdt = take(KT * HM).rearrange("p (k h) -> p k h", k=KT)
            dtb, alog, aneg = take(HM), take(HM), take(HM)
            z, za, ze, zl, a = (take(HM * NT) for _ in range(5))
            cumT = take(2 * P).rearrange("p (b l) -> p b l", b=2)
            S = sems("mp", LN + " r dtp z za ze zl dt alog a cs sfx tot cum dend etot ctr cT scr pad")
            with nc.Block() as block:
                @block.sync
                def _(sp):
                    sp.dma_start(wdt, A["w_dt"].rearrange("(k p) h -> p k h", p=P)).then_inc(S["r"], 16)
                    sp.dma_start(dtb, row(A["dt_bias"])).then_inc(S["r"], 16)
                    sp.dma_start(alog, row(A["A_log"])).then_inc(S["r"], 16)
                    sp.dma_start(cwt, A["conv"].rearrange("(n p) w -> p n w", p=P)).then_inc(S["r"], 16)
                    sp.dma_start(nw, A["norm_w"]).then_inc(S["r"], 16)
                    sp.dma_start(dskip, row(A["D"])).then_inc(S["r"], 16)
                    sp.wait_ge(S["cT"], 1)
                    for b in range(2):
                        sp.dma_start(A["cum_rows"][b * P:(b + 1) * P, :], cumT[:, b, :]).then_inc(S["scr"], 16)
                    sp.wait_ge(S["r"], 96)
                    sp.wait_ge(S["scr"], 32)

                @block.gpsimd
                def _(g):
                    g.memset(raw[:, 0:CONV - 1], 0.0).then_inc(S["pad"], 1)
                    credit(g, spare, [(S2["pj"], 2), (S2["c"], 1), (S2["cbp"], 1), (S2["btok"], 1), (S2["cb"], 1)]
                           + [(S3[n], 1) for n in "c st y yd xs ds sg u ad vr vv op oc".split()]
                           + [(S3[n], 2) for n in "px pg ec df".split()])

                @block.vector
                def _(v):
                    ln_dve(v, S, M, X, XN, 1e-5)
                    v.wait_ge(S["r"], 96)
                    v.wait_ge(S["dtp"], 1)
                    pd = bank(2)[:, 0:HM * NT].rearrange("p (c h) -> p c h", c=NT)
                    for t in range(NT):
                        v.tensor_tensor(z.rearrange("p (h c) -> p c h", c=NT)[:, t, :], pd[:, t, :], dtb,
                                        ALU.add).then_inc(S["z"], 1)
                    v.wait_ge(S["zl"], 1)
                    v.scalar_tensor_tensor(dt, z, 0.0, zl, ALU.max, ALU.add).then_inc(S["dt"], 1)
                    v.wait_ge(S["dt"], 1)
                    v.wait_ge(S["alog"], 1)
                    v.scalar_tensor_tensor(a.rearrange("p (h c) -> p h c", c=NT), dt.rearrange("p (h c) -> p h c", c=NT),
                                           -1.0, aneg.unsqueeze(2).to_broadcast([P, HM, NT]), ALU.mult,
                                           ALU.mult).then_inc(S["a"], 1)
                    v.wait_ge(S["cs"], 1)
                    v.tensor_copy(cum, bank(3)[:, 0:HM * NT]).then_inc(S["cum"], 1)
                    v.wait_ge(S["ctr"], 1)
                    v.tensor_copy(cumT, bank(6)[:, 0:2 * P].rearrange("p (b l) -> p b l", b=2)).then_inc(S["cT"], 1)

                @block.scalar
                def _(act):
                    ln_sqrt(act, S, M)
                    ln_copy(act, S)
                    act.wait_ge(S["r"], 96)
                    nc.scalar.activation(aneg, alog, ACT.Exp).then_inc(S["alog"], 1)
                    act.wait_ge(S["z"], NT)
                    nc.scalar.activation(za, z, ACT.Abs).then_inc(S["za"], 1)
                    act.wait_ge(S["za"], 1)
                    nc.scalar.activation(ze, za, ACT.Exp, scale=-1.0).then_inc(S["ze"], 1)
                    act.wait_ge(S["ze"], 1)
                    nc.scalar.activation(zl, ze, ACT.Ln, bias=1.0).then_inc(S["zl"], 1)
                    act.wait_ge(S["sfx"], 1)
                    nc.scalar.activation(dend, bank(4)[:, 0:HM * NT], ACT.Exp).then_inc(S["dend"], 1)
                    act.wait_ge(S["tot"], 1)
                    nc.scalar.activation(etot, bank(5)[:, 0:HM * NT], ACT.Exp).then_inc(S["etot"], 1)

                @block.tensor
                def _(pe):
                    ln_pe(pe, S)
                    pe.wait_ge(S["xnT"], NT // 2)
                    pe.wait_ge(S["r"], 96)
                    for t in range(NT):
                        last = proj(pe, bank(2)[:, t * HM:(t + 1) * HM], lambda k: XNT[:, k, t * P:(t + 1) * P],
                                    lambda k: wdt[:, k, :], KT)
                    last.then_inc(S["dtp"], 1)
                    pe.wait_ge(S["a"], 1)
                    pe.matmul(bank(3)[:, 0:HM * NT], upto[:, :], a, start=True, stop=True).then_inc(S["cs"], 1)
                    pe.matmul(bank(4)[:, 0:HM * NT], after[:, :], a, start=True, stop=True).then_inc(S["sfx"], 1)
                    pe.matmul(bank(5)[:, 0:HM * NT], ones[:, :], a, start=True, stop=True).then_inc(S["tot"], 1)
                    pe.wait_ge(S["cum"], 1)
                    for b in range(2):
                        last = pe.transpose(bank(6)[:, b * P:(b + 1) * P], cum[:, b * P:(b + 1) * P], ident[:, :])
                    last.then_inc(S["ctr"], 1)

            take.at = common
            bT = take(T)
            S = S2
            first_tile = [BTILE, CTILE]
            with nc.Block() as block:
                @block.sync
                def _(sp):
                    with sp.Fori(0, GM) as g:
                        for i in range(2):
                            sp.wait_ge(S["pj"], g * 2 + i + 1)
                            sp.dma_start(wx[:, i, :, :], A["w_in"][bass.ds(g + first_tile[i], 1), :, :, :]
                                         .rearrange("o p k c -> p (o k) c")).then_inc(S["w" + str(i)], 16)

                @block.tensor
                def _(pe):
                    with pe.Fori(0, GM) as g:
                        for i in range(2):
                            pe.wait_ge(S["w" + str(i)], g * 16 + 16)
                            pe.wait_ge(S["c"], g * 2 + i + 1)
                            channels(pe, wx[:, i, :, :]).then_inc(S["pj"], 1)
                        pe.wait_ge(S["xt"], g * 2 + 1)
                        pe.wait_ge(S["btok"], g + 1)
                        for c in range(NT):
                            last = pe.transpose(bank(4, 2)[:, c * P:(c + 1) * P], bT[:, c * P:(c + 1) * P], ident[:, :])
                        last.then_inc(S["bt"], 1)
                        pe.wait_ge(S["xt"], g * 2 + 2)
                        pe.wait_ge(S["cb"], g + 1)
                        for c in range(NT):
                            last = pe.matmul(bank(6, 2)[:, c * P:(c + 1) * P], bT[:, c * P:(c + 1) * P],
                                             CT[:, bass.ds(g, 1), c * P:(c + 1) * P].rearrange("p o t -> p (o t)"),
                                             start=True, stop=True)
                        last.then_inc(S["cbp"], 1)

                @block.scalar
                def _(act):
                    with act.Fori(0, GM) as g:
                        for i in range(2):
                            act.wait_ge(S["pj"], g * 2 + i + 3)
                            conv_newest(act, S, i, g + (first_tile[i] - HM))
                            act.wait_ge(S["conv"], g * 2 + i + 1)
                            if i == 0:
                                act.wait_ge(S["cbp"], g + 1)
                            dst = bT if i == 0 else CT[:, bass.ds(g, 1), :].rearrange("p o t -> p (o t)")
                            nc.scalar.activation(dst, xT[:, i, :], ACT.Silu).then_inc(S["xt"], 1)

                @block.vector
                def _(v):
                    with v.Fori(0, GM) as g:
                        for i in range(2):
                            conv_taps(v, S, i, g * 2 + i, g + (first_tile[i] - HM))
                        v.wait_ge(S["bt"], g + 1)
                        v.tensor_copy(BTOK[:, bass.ds(g, 1), :, :].rearrange("p o c n -> p (o c n)"),
                                      bank(4, 2)).then_inc(S["btok"], 1)
                        v.wait_ge(S["cbp"], g + 2)
                        v.tensor_tensor(CB[:, bass.ds(g, 1), :].rearrange("p o (c l) -> p (o c) l", c=NT),
                                        bank(6, 2).rearrange("p (c l) -> p c l", c=NT),
                                        upto[:, :].unsqueeze(1).to_broadcast([P, NT, P]), ALU.mult).then_inc(S["cb"], 1)

            take.at = common
            wg = take(2 * E).rearrange("p (b k c) -> p b k c", b=2, k=KT)
            lam = take(T)
            ecs = take(T)
            cumrow = take(2 * T).rearrange("p (b t) -> p b t", b=2)
            xdt, xst, states = take(T), take(T), take(T)
            U = take(4 * T).rearrange("p (j t) -> p j t", j=4)
            sumsq, sq = take(T), take(T)
            wo = take(4 * E).rearrange("p (j e) -> p j e", j=4)
            ve, sd, rr = take(NT), take(NT), take(NT)
            cum_rows = A["cum_rows"].rearrange("(h c) l -> h (c l)", c=NT)
            w_out = A["w_out"].rearrange("(n p) e -> p n e", p=P)
            S = S3
            OCT = GM
            PASSES = HM // OCT
            chunk3 = "p (c l) -> p c l"

            def w_tile(i):
                return A["w_in"][bass.ds(i, 1), :, :, :].rearrange("o p k c -> p (o k) c")

            with nc.Block() as block:
                @block.sync
                def _(sp):
                    sp.dma_start(wx[:, 0, :, :], A["w_in"][XTILE]).then_inc(S["wx0"], 16)
                    with sp.Fori(0, PASSES) as it:
                        for j in range(OCT):
                            K, b = it * OCT + j, j % 2
                            if j % 4 == 1:
                                G = it * 2 + j // 4
                                sp.wait_ge(S["op"], G * NT + 1)
                                sp.dma_start(wo, w_out[:, bass.ds(K - 1, 4), :]).then_inc(S["wo"], 16)
                            sp.wait_ge(S["px"], K + 2)
                            sp.dma_start(wx[:, 1 - b, :, :], w_tile(K + (XTILE + 1))).then_inc(S["wx" + str(1 - b)], 16)
                            sp.wait_ge(S["pg"], K + 1)
                            sp.dma_start(wg[:, b, :, :], w_tile(K)).then_inc(S["wg" + str(b)], 16)
                            sp.wait_ge(S["ec"], K + 1)
                            sp.wait_ge(S["df"], K + 1)
                            sp.dma_start(cumrow[:, b, :], cum_rows[bass.ds(K, 1), :].to_broadcast([P, T]))\
                              .then_inc(S["cr" + str(b)], 16)

                def out_proj(pe, G):
                    pe.wait_ge(S["ad"], G * 3 + 4)
                    pe.wait_ge(S["vv"], G + 1)
                    pe.wait_ge(S["oc"], G * NT + 1)
                    for t in range(NT):
                        last = pe.matmul(bank(6)[:, t:t + 1], sumsq[:, t * P:(t + 1) * P], ones[:, 0:1],
                                         start=True, stop=True)
                    last.then_inc(S["vr"], 1)
                    pe.wait_ge(S["wos"], G + 1)
                    for t in range(NT):
                        if t == 1:
                            pe.wait_ge(S["vv"], G + 2)
                        if t >= 2:
                            pe.wait_ge(S["oc"], G * NT + t)
                        proj(pe, bank(7 - t % 2)[:, 0:E], lambda i: U[:, i, t * P:(t + 1) * P],
                             lambda i: wo[:, i, :], 4).then_inc(S["op"], 1)

                @block.tensor
                def _(pe):
                    pe.wait_ge(S["wx0"], 16)
                    channels(pe, wx[:, 0, :, :]).then_inc(S["px"], 1)
                    with pe.Fori(0, PASSES) as it:
                        for j in range(OCT):
                            K, b, c0 = it * OCT + j, j % 2, it * (OCT // 2) + j // 2
                            pe.wait_ge(S["xt"], K + 1)
                            pe.wait_ge(S["st"], K + 1)
                            for c in range(NT):
                                last = pe.transpose(bank(2, 2)[:, c * P:(c + 1) * P], xT[:, b, c * P:(c + 1) * P],
                                                    ident[:, :])
                            last.then_inc(S["tx"], 1)
                            pe.wait_ge(S["wx" + str(1 - b)], (it * (OCT // 2) + (j + 1) // 2 + 1) * 16)
                            pe.wait_ge(S["sg"], K + 1)
                            channels(pe, wx[:, 1 - b, :, :]).then_inc(S["px"], 1)
                            pe.wait_ge(S["xs"], K + 2)
                            for c in range(NT - 1):
                                last = pe.matmul(bank(2, 2)[:, c * P:(c + 1) * P], BTOK[:, j, c, :],
                                                 xst[:, c * P:(c + 1) * P], start=True, stop=True)
                            last.then_inc(S["ds"], 1)
                            if j == 4:
                                out_proj(pe, it * 2)
                            pe.wait_ge(S["wg" + str(b)], (c0 + 1) * 16)
                            pe.wait_ge(S["c"], K + 3)
                            channels(pe, wg[:, b, :, :]).then_inc(S["pg"], 1)
                            pe.wait_ge(S["mm"], K + 1)
                            pe.wait_ge(S["cs"], K + 1)
                            pe.wait_ge(S["st"], K + 2)
                            pe.wait_ge(S["yd"], K + 1)
                            for c in range(NT):
                                r = slice(c * P, (c + 1) * P)
                                last = pe.matmul(bank(4, 2)[:, r], xdt[:, r], lam[:, r], start=True, stop=(c == 0))
                                if c:
                                    last = pe.matmul(bank(4, 2)[:, r], states[:, (c - 1) * P:c * P], ecs[:, r],
                                                     start=False, stop=True)
                            last.then_inc(S["y"], 1)
                        out_proj(pe, it * 2 + 1)

                @block.scalar
                def _(act):
                    act.wait_ge(S["px"], 3)
                    conv_newest(act, S, 0, 0)
                    act.wait_ge(S["conv"], 1)
                    nc.scalar.activation(xT[:, 0, :], xT[:, 0, :], ACT.Silu).then_inc(S["xt"], 1)

                    def root(G):
                        act.wait_ge(S["vv"], G + 2)
                        nc.scalar.activation(sd, ve, ACT.Sqrt).then_inc(S["sd"], 1)

                    with act.Fori(0, PASSES) as it:
                        for j in range(OCT):
                            K, b, G = it * OCT + j, j % 2, it * 2 + j // 4
                            act.wait_ge(S["px"], K + 4)
                            act.wait_ge(S["u"], K + 1)
                            conv_newest(act, S, 1 - b, K + 1)
                            act.wait_ge(S["cr" + str(b)], (it * (OCT // 2) + j // 2 + 1) * 16)
                            act.wait_ge(S["y"], K + 1)
                            nc.scalar.activation(ecs, cumrow[:, b, :], ACT.Exp).then_inc(S["ec"], 1)
                            act.wait_ge(S["df"], K + 3)
                            nc.scalar.activation(lam, lam, ACT.Exp).then_inc(S["lm"], 1)
                            act.wait_ge(S["conv"], K + 2)
                            nc.scalar.activation(xT[:, 1 - b, :], xT[:, 1 - b, :], ACT.Silu).then_inc(S["xt"], 1)
                            if j == 4:
                                root(it * 2)
                            act.wait_ge(S["pg"], K + 3)
                            act.wait_ge(S["op"], G * NT + 1)
                            nc.scalar.activation(U[:, j % 4, :], bank(0, 2), ACT.Silu).then_inc(S["sg"], 1)
                            act.wait_ge(S["u"], K + 2)
                            if j % 4 == 0:
                                act.wait_ge(S["vr"], G + 1)
                                nc.scalar.activation(sumsq, U[:, 0, :], ACT.Square).then_inc(S["sqs"], 1)
                            else:
                                act.wait_ge(S["ad"], G * 3 + j % 4)
                                nc.scalar.activation(sq, U[:, j % 4, :], ACT.Square).then_inc(S["sqs"], 1)
                        root(it * 2 + 1)

                @block.gpsimd
                def _(g):
                    with g.Fori(0, PASSES) as it:
                        for j in range(OCT):
                            K, b, G = it * OCT + j, j % 2, it * 2 + j // 4
                            if j % 4 == 2:
                                g.wait_ge(S["wo"], G * 16 + 16)
                                g.tensor_tensor(wo, wo, nw[:, bass.ds(K - 2, 4)].unsqueeze(2).to_broadcast([P, 4, E]),
                                                ALU.mult).then_inc(S["wos"], 1)
                            g.wait_ge(S["xd"], K + 1)
                            g.wait_ge(S["ds"], K + 1)
                            g.tensor_tensor(xst.rearrange(chunk3, c=NT), xdt.rearrange(chunk3, c=NT),
                                            dend[:, bass.ds(K * NT, NT)].unsqueeze(2).to_broadcast([P, NT, P]),
                                            ALU.mult).then_inc(S["xs"], 1)
                            g.wait_ge(S["ec"], K + 3)
                            g.tensor_tensor(ecs, ecs, CT[:, j, :], ALU.mult).then_inc(S["cs"], 1)
                            g.wait_ge(S["yd"], K + 2)
                            g.wait_ge(S["sg"], K + 2)
                            g.tensor_tensor(U[:, j % 4, :], U[:, j % 4, :], xT[:, b, :], ALU.mult).then_inc(S["u"], 1)
                            if j % 4:
                                g.wait_ge(S["sqs"], K + 1)
                                g.wait_ge(S["ad"], G * 3 + j % 4)
                                g.tensor_tensor(sumsq, sumsq, sq, ALU.add).then_inc(S["ad"], 1)

                @block.vector
                def _(v):
                    conv_taps(v, S, 0, 0, 0)

                    def normalise(G):
                        v.wait_ge(S["vr"], G + 2)
                        v.tensor_scalar(ve, bank(6)[:, 0:NT], 1.0 / (4 * P), 1e-6, ALU.mult, ALU.add).then_inc(S["vv"], 1)
                        v.wait_ge(S["sd"], G + 1)
                        v.reciprocal(rr, sd).then_inc(S["rr"], 1)
                        v.wait_ge(S["rr"], G + 1)
                        for t in range(NT):
                            v.wait_ge(S["op"], G * NT + (t + 2))
                            v.scalar_tensor_tensor(X[:, t, :], bank(7 - t % 2)[:, 0:E], rr[:, t:t + 1], X[:, t, :],
                                                   ALU.mult, ALU.add).then_inc(S["oc"], 1)

                    with v.Fori(0, PASSES) as it:
                        for j in range(OCT):
                            K, b = it * OCT + j, j % 2
                            v.wait_ge(S["tx"], K + 1)
                            v.wait_ge(S["y"], K + 1)
                            v.wait_ge(S["xs"], K + 1)
                            v.tensor_tensor(xdt.rearrange(chunk3, c=NT), bank(2, 2).rearrange(chunk3, c=NT),
                                            dt[:, bass.ds(K * NT, NT)].unsqueeze(2).to_broadcast([P, NT, P]),
                                            ALU.mult).then_inc(S["xd"], 1)
                            v.wait_ge(S["cr" + str(b)], (it * (OCT // 2) + j // 2 + 1) * 16)
                            for c in range(NT):
                                last = v.tensor_scalar(lam[:, c * P:(c + 1) * P], cumrow[:, b, c * P:(c + 1) * P],
                                                       col(cum, K * NT + c), 0.0, ALU.subtract, ALU.min)
                            last.then_inc(S["df"], 1)
                            conv_taps(v, S, 1 - b, K + 1, K + 1)
                            v.wait_ge(S["lm"], K + 1)
                            v.tensor_tensor(lam, lam, CB[:, j, :], ALU.mult).then_inc(S["mm"], 1)
                            v.wait_ge(S["ds"], K + 2)
                            v.tensor_copy(states[:, 0:P], bank(2, 2)[:, 0:P]).then_inc(S["rc"], 1)
                            for c in range(1, NT - 1):
                                v.wait_ge(S["rc"], K * (NT - 2) + c)
                                v.scalar_tensor_tensor(states[:, c * P:(c + 1) * P], states[:, (c - 1) * P:c * P],
                                                       col(etot, K * NT + c), bank(2, 2)[:, c * P:(c + 1) * P],
                                                       ALU.mult, ALU.add).then_inc(S["rc"] if c < NT - 2 else S["st"], 1)
                            if j == 4:
                                normalise(it * 2)
                            v.wait_ge(S["y"], K + 2)
                            v.scalar_tensor_tensor(xT[:, b, :], xT[:, b, :], col(dskip, K), bank(4, 2), ALU.mult,
                                                   ALU.add).then_inc(S["yd"], 1)
                        normalise(it * 2 + 1)

        def ponder_ffn(name, last_phase):
            take = Region()
            S = sems(name, LN + " w r c pad o_stats o_aggr o_ve o_sd o_rstd o_xn m d q vr ve2 sd2 rc n g t"
                     " ap th up hb h dn b1 bc bcr gp gs sg mul out og ob fin st")
            SO = {k: S["o_" + k] for k in "stats aggr ve sd rstd xn".split()}
            M, MO = ln_region(take), ln_region(take)
            cols = take(6 * KT).rearrange("p (n k) -> p n k", k=KT)
            in_g, in_b, agg_b, pn_g, pn_b, d2_b = (cols[:, i, :] for i in range(6))
            d1_b = take(FT)
            agg = take(KT * E).rearrange("p (k e) -> p k e", k=KT)
            bcw = take(KT * E).rearrange("p (k e) -> p k e", k=KT)
            gw = take(KT * E).rearrange("p (k e) -> p k e", k=KT)
            d1 = take(KT * DFF).rearrange("p (k f) -> p k f", k=KT)
            d2 = take(FT * E).rearrange("p (k e) -> p k e", k=FT)
            gb, bcb, out_g, out_b, bcrow = (take(E) for _ in range(5))
            mean_w, negmean_w = take(P), take(P)
            dev, dsq, tn, tt, th, th2 = (take(KT) for _ in range(6))
            hb, hh = take(FT), take(FT)
            var, vsd, vrs = take(1), take(1), take(1)
            SG = take(NT * E).rearrange("p (t e) -> p t e", t=NT)

            def wide(r):
                return r.unsqueeze(1).to_broadcast([P, NT, E])

            with nc.Block() as block:
                @block.sync
                def _(sp):
                    for dst, src in ((gb, "gate_b"), (bcb, "bc_b"), (out_g, "out_g"), (out_b, "out_b")):
                        sp.dma_start(dst, row(A[src])).then_inc(S["r"], 16)
                    sp.dma_start(cols, A["cols"]).then_inc(S["r"], 16)
                    sp.dma_start(d1_b, A["d1_b"]).then_inc(S["r"], 16)
                    for dst, src in ((agg, "agg_w"), (gw, "gate_w"), (d1, "d1_w"), (d2, "d2_w"), (bcw, "bc_w")):
                        sp.dma_start(dst, A[src].rearrange("(k p) f -> p k f", p=P)).then_inc(S["w"], 16)
                    if last_phase:
                        for t in range(NT):
                            sp.wait_ge(S["fin"], t + 1)
                            sp.dma_start(out[t * P:(t + 1) * P, :], X[:, t, :]).then_inc(S["st"], 16)
                        sp.wait_ge(S["st"], 16 * NT)

                @block.gpsimd
                def _(g):
                    g.memset(mean_w, 1.0 / E).then_inc(S["pad"], 1)
                    g.memset(negmean_w, -1.0 / E).then_inc(S["pad"], 1)

                def col_ln_dve(v, src, n, gamma, beta):
                    v.wait_ge(S["m"], n + 1)
                    v.tensor_scalar(dev, src, bank(2)[:, 0:1], None, ALU.add).then_inc(S["d"], 1)
                    v.wait_ge(S["d"], n + 1)
                    v.tensor_tensor(dsq, dev, dev, ALU.mult).then_inc(S["q"], 1)
                    v.wait_ge(S["vr"], n + 1)
                    v.tensor_scalar(var, bank(3)[:, 0:1], 1e-6, None, ALU.add).then_inc(S["ve2"], 1)
                    v.wait_ge(S["sd2"], n + 1)
                    v.reciprocal(vrs, vsd).then_inc(S["rc"], 1)
                    v.wait_ge(S["rc"], n + 1)
                    v.scalar_tensor_tensor(tn, dev, vrs[:, 0:1], gamma, ALU.mult, ALU.mult).then_inc(S["n"], 1)
                    v.wait_ge(S["n"], n + 1)
                    v.tensor_tensor(tt, tn, beta, ALU.add).then_inc(S["t"], 1)

                def col_ln_act(act, n):
                    act.wait_ge(S["ve2"], n + 1)
                    nc.scalar.activation(vsd, var, ACT.Sqrt).then_inc(S["sd2"], 1)

                def col_ln_pe(pe, src, n):
                    proj(pe, bank(2)[:, 0:1], lambda k: negmean_w, lambda k: src[:, k:k + 1], KT).then_inc(S["m"], 1)
                    pe.wait_ge(S["q"], n + 1)
                    proj(pe, bank(3)[:, 0:1], lambda k: mean_w, lambda k: dsq[:, k:k + 1], KT).then_inc(S["vr"], 1)

                newest = XNT[:, :, T - 1]

                @block.tensor
                def _(pe):
                    ln_pe(pe, S)
                    pe.wait_ge(S["xnT"], NT // 2)
                    pe.wait_ge(S["pad"], 2)
                    col_ln_pe(pe, newest, 0)
                    pe.wait_ge(S["w"], 16 * 5)
                    def gates(g):
                        if g >= 2:
                            pe.wait_ge(S["gs"], g - 1)
                        for h in range(2):
                            t = 2 * g + h
                            last = proj(pe, bank(6 + g % 2)[:, h * E:(h + 1) * E],
                                        lambda k: XNT[:, k, t * P:(t + 1) * P], lambda k: gw[:, k, :], KT)
                        last.then_inc(S["gp"], 1)
                    for g in range(NT // 2):
                        gates(g)
                    pe.wait_ge(S["t"], 1)
                    for m in range(KT):
                        last = proj(pe, bank(4)[:, m:m + 1], lambda k: agg[:, k, m * P:(m + 1) * P],
                                    lambda k: tt[:, k:k + 1], KT)
                    last.then_inc(S["ap"], 1)
                    with pe.Fori(0, 4) as i:
                        pe.wait_ge(S["th"], i + 1)
                        col_ln_pe(pe, th, i + 1)
                        pe.wait_ge(S["t"], i + 2)
                        for f in range(FT):
                            last = proj(pe, bank(5)[:, f:f + 1], lambda k: d1[:, k, f * P:(f + 1) * P],
                                        lambda k: tt[:, k:k + 1], KT)
                        last.then_inc(S["up"], 1)
                        pe.wait_ge(S["h"], i + 1)
                        for m in range(KT):
                            last = proj(pe, bank(4)[:, m:m + 1], lambda k: d2[:, k, m * P:(m + 1) * P],
                                        lambda k: hh[:, k:k + 1], FT)
                        last.then_inc(S["dn"], 1)
                    pe.wait_ge(S["th"], 5)
                    proj(pe, bank(3)[:, 0:E], lambda k: th[:, k:k + 1].to_broadcast([P, P]), lambda k: bcw[:, k, :],
                         KT).then_inc(S["bc"], 1)

                @block.scalar
                def _(act):
                    ln_sqrt(act, S, M)
                    ln_copy(act, S)
                    col_ln_act(act, 0)
                    act.wait_ge(S["gs"], NT // 2)
                    nc.scalar.activation(SG, SG, ACT.Sigmoid).then_inc(S["sg"], 1)
                    with act.Fori(0, 4) as i:
                        col_ln_act(act, i + 1)
                        act.wait_ge(S["hb"], i + 1)
                        nc.scalar.activation(hh, hb, ACT.Gelu).then_inc(S["h"], 1)
                    ln_sqrt(act, SO, MO)

                @block.vector
                def _(v):
                    ln_dve(v, S, M, X, XN, 1e-5)
                    v.wait_ge(S["r"], 16 * 6)
                    col_ln_dve(v, newest, 0, in_g, in_b)
                    for g in range(NT // 2):
                        v.wait_ge(S["gp"], g + 1)
                        v.tensor_tensor(SG[:, 2 * g:2 * g + 2, :], bank(6 + g % 2).rearrange("p (t e) -> p t e", t=2),
                                        gb.unsqueeze(1).to_broadcast([P, 2, E]), ALU.add).then_inc(S["gs"], 1)
                    v.wait_ge(S["ap"], 1)
                    v.tensor_tensor(th, bank(4)[:, 0:KT], agg_b, ALU.add).then_inc(S["th"], 1)
                    v.wait_ge(S["th"], 1)
                    with v.Fori(0, 4) as i:
                        v.tensor_tensor(th2, th, d2_b, ALU.add).then_inc(S["b1"], 1)
                        col_ln_dve(v, th, i + 1, pn_g, pn_b)
                        v.wait_ge(S["up"], i + 1)
                        v.tensor_tensor(hb, bank(5)[:, 0:FT], d1_b, ALU.add).then_inc(S["hb"], 1)
                        v.wait_ge(S["dn"], i + 1)
                        v.wait_ge(S["b1"], i + 1)
                        v.tensor_tensor(th, bank(4)[:, 0:KT], th2, ALU.add).then_inc(S["th"], 1)
                        v.wait_ge(S["th"], i + 2)
                    v.wait_ge(S["bc"], 1)
                    v.tensor_tensor(bcrow, bank(3)[:, 0:E], bcb, ALU.add).then_inc(S["bcr"], 1)
                    v.wait_ge(S["bcr"], 1)
                    v.wait_ge(S["sg"], 1)
                    v.tensor_tensor(SG, SG, wide(bcrow), ALU.mult).then_inc(S["mul"], 1)
                    v.wait_ge(S["mul"], 1)
                    v.tensor_tensor(SG, SG, XN, ALU.add).then_inc(S["out"], 1)
                    v.wait_ge(S["out"], 1)
                    ln_dve(v, SO, MO, SG, SG, 1e-6)
                    v.wait_ge(SO["xn"], NT)
                    v.tensor_tensor(SG, SG, wide(out_g), ALU.mult).then_inc(S["og"], 1)
                    v.wait_ge(S["og"], 1)
                    v.tensor_tensor(SG, SG, wide(out_b), ALU.add).then_inc(S["ob"], 1)
                    v.wait_ge(S["ob"], 1)
                    for t in range(NT):
                        v.scalar_tensor_tensor(X[:, t, :], SG[:, t, :], 0.5, X[:, t, :], ALU.mult,
                                               ALU.add).then_inc(S["fin"], 1)

        def attention():
            take = Region()
            V = take(NH * NT * P).rearrange("p (t n) -> p t n", t=NT)
            OT = take(NH * T).rearrange("p (h t) -> p h t", h=NH)
            common = take.at
            S = sems("av", LN + " w vp vc")
            SA = sems("ah", "w0 w1 tab pq t1 t2 rd sc msk mx nb ex rcp tr tev pv oe")
            SW = sems("ao", "w p a")
            M = ln_region(take)
            wv = take(KT * NH * P).rearrange("p (k n) -> p k n", k=KT)
            spare = take(8)
            NB = NH * P // BANK
            with nc.Block() as block:
                @block.sync
                def _(sp):
                    sp.dma_start(wv, A["wv"].rearrange("(k p) n -> p k n", p=P)).then_inc(S["w"], 16)

                @block.gpsimd
                def _(g):
                    credit(g, spare, [(SA[s], n) for s, n in (("pq", 1), ("t2", 2), ("rd", 2), ("ex", 2), ("tr", 1), ("tev", 1), ("pv", 2), ("oe", 2))])

                @block.vector
                def _(v):
                    ln_dve(v, S, M, X, XN, 1e-5)

                @block.scalar
                def _(act):
                    ln_sqrt(act, S, M)
                    ln_copy(act, S)
                    for n in range(NT * NB):
                        act.wait_ge(S["vp"], n + 1)
                        nc.scalar.copy(V[:, n // NB, n % NB * BANK:(n % NB + 1) * BANK], bank(4 + n % 4)).then_inc(S["vc"], 1)

                @block.tensor
                def _(pe):
                    ln_pe(pe, S)
                    pe.wait_ge(S["xnT"], NT // 2)
                    pe.wait_ge(S["w"], 16)
                    for n in range(NT * NB):
                        if n >= 4:
                            pe.wait_ge(S["vc"], n - 3)
                        t = n // NB
                        proj(pe, bank(4 + n % 4), lambda k: XNT[:, k, t * P:(t + 1) * P],
                             lambda k: wv[:, k, n % NB * BANK:(n % NB + 1) * BANK], KT).then_inc(S["vp"], 1)

            take.at = common
            S = SA
            cos_t, sin_t = take(T), take(T)
            wqk = take(4 * E).rearrange("p (b u k d) -> p b u k d", b=2, u=2, k=KT)
            qk = take(4 * T).rearrange("p (b u t) -> p b u t", b=2, u=2)
            turn = take(2 * HALF).rearrange("p (b t) -> p b t", b=2)
            pr = take(2 * T).rearrange("p (b t) -> p b t", b=2)
            PT = take(2 * T).rearrange("p (b t) -> p b t", b=2)
            oS = take(T)
            nmx, nb, rsum, rinv = take(2), take(2), take(2), take(2)
            NU = 4
            TG = 14
            groups, outs, m = {}, {}, 0
            for i in range(NT):
                groups[i] = []
                for lo in range(0, i + 1, 4):
                    groups[i].append((m, lo, min(lo + 4, i + 1)))
                    m += 1
                if i in (4, 7):
                    outs[i] = (m, 0 if i == 4 else 4)
                    m += 1
            assert m == TG
            HALFP = P // 2

            with nc.Block() as block:
                @block.sync
                def _(sp):
                    sp.dma_start(wqk[:, 0, :, :, :], A["w_qk"][0]).then_inc(S["w0"], 16)
                    sp.dma_start(cos_t, A["cos"]).then_inc(S["tab"], 16)
                    sp.dma_start(sin_t, A["sin"]).then_inc(S["tab"], 16)
                    with sp.Fori(0, NH // 2) as it:
                        for j in range(2):
                            h = it * 2 + j
                            sp.wait_ge(S["pq"], h * NU + 1)
                            sp.dma_start(wqk[:, 1 - j, :, :, :], A["w_qk"][bass.ds(h + 1, 1)]
                                         .rearrange("o p u k d -> p (o u) k d")).then_inc(S["w" + str(1 - j)], 16)

                def project(pe, f, b, u):
                    r = f * NU + u
                    pe.wait_ge(S["t2"], r + 1)
                    proj(pe, bank(u % 2), lambda k: wqk[:, b, u // 2, k, :],
                         lambda k: XNT[:, k, u % 2 * HALF:(u % 2 + 1) * HALF], KT).then_inc(S["pq"], 1)

                @block.tensor
                def _(pe):
                    pe.wait_ge(S["w0"], 16)
                    for u in range(NU):
                        project(pe, 0, 0, u)
                    with pe.Fori(0, NH // 2) as it:
                        for j in range(2):
                            h = it * 2 + j

                            def scores(i):
                                n = h * NT + i
                                pe.wait_ge(S["ex"], n + 1)
                                base = 2 + i % 2 * 2
                                for lo in range(0, (i + 1) * P, BANK):
                                    hi = min(lo + BANK, (i + 1) * P)
                                    last = pe.matmul(bank(base, 2)[:, lo:hi], qk[:, j, 0, i * P:(i + 1) * P],
                                                     qk[:, j, 1, lo:hi], start=True, stop=True)
                                last.then_inc(S["sc"], 1)

                            pe.wait_ge(S["rd"], (h + 1) * NU + 2)
                            scores(0)
                            for i in range(NT):
                                n = h * NT + i
                                if i + 1 < NT:
                                    scores(i + 1)
                                if i % 2:
                                    if i == 1:
                                        pe.wait_ge(S["w" + str(1 - j)], (it + 1 if j == 0 else it + 2) * 16)
                                    project(pe, h + 1, 1 - j, i // 2)
                                pe.wait_ge(S["ex"], n + 3)
                                for q, (m, lo, hi) in enumerate(groups[i]):
                                    pe.wait_ge(S["tev"], h * TG + (m + 1))
                                    for c in range(lo, hi):
                                        last = pe.transpose(bank(6)[:, (c - lo) * P:(c - lo + 1) * P],
                                                            pr[:, i % 2, c * P:(c + 1) * P], ident[:, :])
                                    last.then_inc(S["tr"], 1)
                                pe.wait_ge(S["oe"], n + 2)
                                for q, (m, lo, hi) in enumerate(groups[i]):
                                    pe.wait_ge(S["tev"], h * TG + (m + 2))
                                    for c in range(lo, hi):
                                        last = pe.matmul(bank(7)[:, 0:P], PT[:, i % 2, c * P:(c + 1) * P],
                                                         V[:, c, bass.ds(h * P, P)], start=(c == 0), stop=(c == i))
                                last.then_inc(S["pv"], 1)
                                if i in outs:
                                    m, lo = outs[i]
                                    pe.wait_ge(S["oe"], h * NT + (lo + 6))
                                    pe.wait_ge(S["tev"], h * TG + (m + 1))
                                    for c in range(lo, lo + 4):
                                        last = pe.transpose(bank(6)[:, (c - lo) * P:(c - lo + 1) * P],
                                                            oS[:, c * P:(c + 1) * P], ident[:, :])
                                    last.then_inc(S["tr"], 1)

                @block.scalar
                def _(act):
                    with act.Fori(0, NH // 2) as it:
                        for j in range(2):
                            h = it * 2 + j

                            def exps(i):
                                n = h * NT + i
                                b = i % 2
                                act.wait_ge(S["nb"], n + 1)
                                nc.scalar.activation(pr[:, b, 0:(i + 1) * P], bank(2 + 2 * b, 2)[:, 0:(i + 1) * P],
                                                     ACT.Exp, bias=nb[:, b:b + 1], scale=ATTN_SCALE,
                                                     accum_out=rsum[:, b:b + 1]).then_inc(S["ex"], 1)

                            for i in range(NT):
                                n = h * NT + i
                                b = i % 2
                                exps(i)
                                for m, lo, hi in groups[i]:
                                    act.wait_ge(S["tr"], h * TG + (m + 2))
                                    nc.scalar.copy(PT[:, b, lo * P:hi * P], bank(6)[:, 0:(hi - lo) * P])\
                                      .then_inc(S["tev"], 1)
                                act.wait_ge(S["pv"], n + 3)
                                act.wait_ge(S["rcp"], n + 1)
                                nc.scalar.activation(oS[:, i * P:(i + 1) * P], bank(7)[:, 0:P], ACT.Copy,
                                                     scale=rinv[:, b:b + 1]).then_inc(S["oe"], 1)
                                if i in outs:
                                    m, lo = outs[i]
                                    act.wait_ge(S["tr"], h * TG + (m + 2))
                                    nc.scalar.copy(OT[:, bass.ds(h, 1), lo * P:(lo + 4) * P]
                                                   .rearrange("p o t -> p (o t)"), bank(6)).then_inc(S["tev"], 1)

                @block.gpsimd
                def _(g):
                    def add(f, b, u):
                        r = f * NU + u
                        g.wait_ge(S["t2"], r + 3)
                        dst = qk[:, b, u // 2, u % 2 * HALF:(u % 2 + 1) * HALF]
                        g.tensor_tensor(dst, dst, turn[:, u % 2, :], ALU.add).then_inc(S["rd"], 1)

                    for u in range(NU):
                        add(0, 0, u)
                    with g.Fori(0, NH // 2) as it:
                        for j in range(2):
                            for u in range(NU):
                                add(it * 2 + j + 1, 1 - j, u)

                @block.vector
                def _(v):
                    def rotate(f, b, u):
                        r = f * NU + u
                        cols_ = slice(u % 2 * HALF, (u % 2 + 1) * HALF)
                        v.wait_ge(S["pq"], r + 2)
                        v.tensor_tensor(qk[:, b, u // 2, cols_], bank(u % 2), cos_t[:, cols_], ALU.mult).then_inc(S["t1"], 1)
                        v.wait_ge(S["rd"], r + 1)
                        v.tensor_tensor(turn[0:HALFP, u % 2, :], bank(u % 2)[HALFP:P, :], sin_t[HALFP:P, cols_],
                                        ALU.mult).then_inc(S["t1"], 1)
                        v.tensor_tensor(turn[HALFP:P, u % 2, :], bank(u % 2)[0:HALFP, :], sin_t[0:HALFP, cols_],
                                        ALU.mult).then_inc(S["t2"], 1)

                    v.wait_ge(S["tab"], 32)
                    for u in range(NU):
                        rotate(0, 0, u)
                    with v.Fori(0, NH // 2) as it:
                        for j in range(2):
                            h = it * 2 + j
                            for i in range(NT):
                                n = h * NT + i
                                b = i % 2
                                s = bank(2 + 2 * b, 2)
                                v.wait_ge(S["sc"], n + 1)
                                v.tensor_tensor(s[:, i * P:(i + 1) * P], s[:, i * P:(i + 1) * P], causal[:, :],
                                                ALU.add).then_inc(S["msk"], 1)
                                v.wait_ge(S["msk"], n + 1)
                                v.tensor_reduce(nmx[:, b:b + 1], s[:, 0:(i + 1) * P], AX.X, ALU.max,
                                                negate=True).then_inc(S["mx"], 1)
                                v.wait_ge(S["mx"], n + 1)
                                v.tensor_scalar(nb[:, b:b + 1], nmx[:, b:b + 1], ATTN_SCALE, None,
                                                ALU.mult).then_inc(S["nb"], 1)
                                if i % 2:
                                    rotate(h + 1, 1 - j, i // 2)
                                for q in ([i - 1] if i else []) + ([i] if i == NT - 1 else []):
                                    v.wait_ge(S["ex"], h * NT + (q + 3))
                                    v.wait_ge(S["oe"], h * NT + (q + 1))
                                    v.reciprocal(rinv[:, q % 2:q % 2 + 1], rsum[:, q % 2:q % 2 + 1])\
                                     .then_inc(S["rcp"], 1)

            take.at = common
            wo = take(NH * E).rearrange("p (h e) -> p h e", h=NH)
            S = SW
            with nc.Block() as block:
                @block.sync
                def _(sp):
                    sp.dma_start(wo, A["wo"].rearrange("(h p) e -> p h e", p=P)).then_inc(S["w"], 16)

                @block.tensor
                def _(pe):
                    pe.wait_ge(S["w"], 16)
                    for t in range(NT):
                        if t >= 2:
                            pe.wait_ge(S["a"], t - 1)
                        proj(pe, bank(t % 2)[:, 0:E], lambda h: OT[:, h, t * P:(t + 1) * P], lambda h: wo[:, h, :],
                             NH).then_inc(S["p"], 1)

                @block.vector
                def _(v):
                    for t in range(NT):
                        v.wait_ge(S["p"], t + 1)
                        v.tensor_tensor(X[:, t, :], X[:, t, :], bank(t % 2)[:, 0:E], ALU.add).then_inc(S["a"], 1)

        topk_ffn("fa", True)
        end_phase()
        mamba()
        end_phase()
        topk_ffn("fb", False)
        end_phase()
        ponder_ffn("pa", False)
        end_phase()
        attention()
        end_phase()
        ponder_ffn("pb", True)


def kernel(**inputs):
    import numpy as np
    import concourse.bacc as bacc
    from concourse.bass_utils import run_bass_kernel_spmd

    def f(name):
        return np.ascontiguousarray(inputs[name])

    def columns(name):
        return f(name).reshape(-1, P).T

    w_in = f("L0_attn_in_proj_w")
    tiles = w_in[:-HM].reshape(-1, P, KT, P).transpose(0, 3, 2, 1)
    wq, wk = (f(n).reshape(KT, P, NH, P).transpose(2, 1, 0, 3) for n in ("L1_attn_wq", "L1_attn_wk"))
    w_qk = np.stack([wq, wk], axis=2)
    half = P // 2
    freqs = np.power(np.float32(10000.0), -np.arange(half, dtype=np.float32) / np.float32(half))
    rad = (np.arange(T, dtype=np.float32)[:, None] * freqs[None, :]).astype(np.float32).T
    cos, sin = np.cos(rad).astype(np.float32), np.sin(rad).astype(np.float32)
    arrays = {
        "x": f("L0_attn_x").reshape(T, E),
        "Wr": f("L0_ffn_Wr").reshape(E), "br": f("L0_ffn_br"), "W1": f("L0_ffn_W1"), "b1": columns("L0_ffn_b1"),
        "W2": f("L0_ffn_W2"), "b2": f("L0_ffn_b2"),
        "w_in": tiles, "w_dt": w_in[-HM:].T,
        "conv": np.concatenate([f("L0_attn_conv_w")[:, 0, :], f("L0_attn_conv_b")[:, None]], axis=1),
        "dt_bias": f("L0_attn_dt_bias"), "A_log": f("L0_attn_A_log"), "D": f("L0_attn_D"),
        "norm_w": columns("L0_attn_norm_w"), "w_out": f("L0_attn_out_proj_w").T,
        "w_qk": np.concatenate([w_qk, w_qk[:1]]),
        "wv": f("L1_attn_wv").reshape(E, NH * P), "wo": f("L1_attn_wo").reshape(NH * P, E),
        "cos": np.concatenate([cos, cos]), "sin": np.concatenate([sin, -sin]),
        "cols": np.stack([columns(n) for n in ("L1_ffn_in_gamma", "L1_ffn_in_beta", "L1_ffn_agg_b", "L1_ffn_pn_gamma",
                                               "L1_ffn_pn_beta", "L1_ffn_d2_b")], axis=1),
        "d1_b": columns("L1_ffn_d1_b"), "gate_b": f("L1_ffn_gate_b"), "bc_b": f("L1_ffn_bc_b"),
        "out_g": f("L1_ffn_out_gamma"), "out_b": f("L1_ffn_out_beta"),
        "agg_w": f("L1_ffn_agg_w"), "gate_w": f("L1_ffn_gate_w"), "d1_w": f("L1_ffn_d1_w"), "d2_w": f("L1_ffn_d2_w"),
        "bc_w": f("L1_ffn_bc_w"),
    }
    arrays = {n: np.ascontiguousarray(a) for n, a in arrays.items()}
    nc = bacc.Bacc("TRN2", target_bir_lowering=False, num_devices=1)
    A = {n: nc.dram_tensor("in_" + n, a.shape, mybir.dt.from_np(a.dtype), kind="ExternalInput").ap()
         for n, a in arrays.items()}
    A["cum_rows"] = nc.dram_tensor("cum_rows", (HM * NT, P), F32, kind="Internal").ap()
    out = nc.dram_tensor("out_x", (T, E), F32, kind="ExternalOutput").ap()
    build(nc, A, out)
    r = run_bass_kernel_spmd(nc, [{"in_" + n: a for n, a in arrays.items()}], core_ids=[0])
    return r.results[0]["out_x"].reshape(1, T, E)
```

```python
from contextlib import ExitStack

import concourse.bass as bass
from concourse import mybir

F32 = mybir.dt.float32
ALU = mybir.AluOpType
ACT = mybir.ActivationFunctionType
AX = mybir.AxisListType

P = 128
T = 1024
E = 256
NT = T // P
KT = E // P
TOPK = P
DFF = 1024
FT = DFF // P
HM, GM = 32, 8
CONV = 4
XTILE, BTILE, CTILE = HM, 2 * HM, 2 * HM + GM
CW = CONV + 1
NH = 16
HALF = T // 2
BANK = 512
ATTN_SCALE = 1.0 / 128.0
NEG = -1e30


def build(nc, A, out):
    with ExitStack() as ctx:
        open_sems = []

        def sems(phase, names):
            S = {n: nc.alloc_semaphore(phase + "_" + n) for n in names.split()}
            open_sems.extend(S.values())
            return S

        def end_phase():
            nc.clear_and_free_semaphores(list(open_sems))
            open_sems.clear()
            nc.all_engine_barrier()

        def sb(name, cols):
            return ctx.enter_context(nc.sbuf_tensor(name, [P, cols], F32))

        x_sb = sb("x_sb", NT * E)
        xn_sb = sb("xn_sb", NT * E)
        xnT_sb = sb("xnT_sb", KT * T)
        X = x_sb[:, :].rearrange("p (t e) -> p t e", t=NT)
        XN = xn_sb[:, :].rearrange("p (t e) -> p t e", t=NT)
        XNT = xnT_sb[:, :].rearrange("p (k t) -> p k t", k=KT)
        ident = sb("ident", P)
        ones = sb("ones", P)
        upto = sb("upto", P)
        after = sb("after", P)
        slots = sb("slots", P)
        causal = sb("causal", P)
        ARENA = 46200
        arena = sb("arena", ARENA)
        psum = ctx.enter_context(nc.psum_tensor("psum", [P, 8 * BANK], F32))

        class Region:

            def __init__(self):
                self.at = 0

            def __call__(self, cols):
                self.at += cols
                assert self.at <= ARENA, self.at
                return arena[:, self.at - cols:self.at]

        def bank(b, n=1):
            return psum[:, b * BANK:(b + n) * BANK]

        def row(ap):
            return ap.rearrange("(a d) -> a d", a=1).to_broadcast([P, ap.shape[0]])

        def proj(pe, dst, lhs, rhs, n):
            for k in range(n):
                last = pe.matmul(dst, lhs(k), rhs(k), start=(k == 0), stop=(k == n - 1))
            return last

        def credit(g, spare, pairs):
            for i, (s, n) in enumerate(pairs):
                g.memset(spare[:, i:i + 1], 0.0).then_inc(s, n)

        LN = "stats aggr ve sd rstd xn tr xnT"

        def ln_region(take):
            return {"st": take(NT * 6).rearrange("p (t s) -> p t s", t=NT),
                    "mv": take(NT * 2).rearrange("p (t s) -> p t s", t=NT),
                    "ve": take(NT), "sd": take(NT), "rstd": take(NT)}

        def ln_dve(v, S, M, src, dst, eps, tiles=NT):
            for t in range(tiles):
                v.bn_stats(M["st"][:, t, :], src[:, t, :]).then_inc(S["stats"], 1)
            v.wait_ge(S["stats"], tiles)
            for t in range(tiles):
                v.bn_aggr(M["mv"][:, t, :], M["st"][:, t, :]).then_inc(S["aggr"], 1)
            v.wait_ge(S["aggr"], tiles)
            v.tensor_scalar(M["ve"], M["mv"][:, :, 1], eps, None, ALU.add).then_inc(S["ve"], 1)
            v.wait_ge(S["sd"], 1)
            v.reciprocal(M["rstd"], M["sd"]).then_inc(S["rstd"], 1)
            v.wait_ge(S["rstd"], 1)
            for t in range(tiles):
                v.tensor_scalar(dst[:, t, :], src[:, t, :], M["mv"][:, t, 0:1], M["rstd"][:, t:t + 1],
                                ALU.subtract, ALU.mult).then_inc(S["xn"], 1)

        def ln_sqrt(act, S, M):
            act.wait_ge(S["ve"], 1)
            nc.scalar.activation(M["sd"], M["ve"], ACT.Sqrt).then_inc(S["sd"], 1)

        def ln_pe(pe, S):
            for g in range(NT // 2):
                pe.wait_ge(S["xn"], 2 * g + 2)
                if g >= 2:
                    pe.wait_ge(S["xnT"], g - 1)
                for k in range(KT):
                    for h in range(2):
                        last = pe.transpose(bank(g % 2)[:, (2 * k + h) * P:(2 * k + h + 1) * P],
                                            XN[:, 2 * g + h, k * P:(k + 1) * P], ident[:, :])
                last.then_inc(S["tr"], 1)

        def ln_copy(act, S):
            for g in range(NT // 2):
                act.wait_ge(S["tr"], g + 1)
                nc.scalar.copy(XNT[:, :, 2 * g * P:(2 * g + 2) * P],
                               bank(g % 2).rearrange("p (k t) -> p k t", k=KT)).then_inc(S["xnT"], 1)

        def topk_ffn(name, first):
            take = Region()
            S = sems(name, LN + " w r x const wr lcol lb ltr lmax rank rk sel selT seltr selTev wexp wz zs z rz cw"
                     " g gc up hT dn ol sc res half prod")
            M = ln_region(take)
            w1 = take(KT * DFF).rearrange("p (k f) -> p k f", k=KT)
            w2 = take(FT * E).rearrange("p (k e) -> p k e", k=FT)
            b1 = take(FT)
            b2, wr, br = take(E), take(E), take(1)
            lcol, lbc = take(NT), take(T).rearrange("p (t q) -> p t q", t=NT)
            junk = take(T)
            parts = take(3 * NT).rearrange("p (a t) -> p a t", a=3)
            rank, rank2, mask = take(NT), take(NT), take(NT)
            sel = take(NT * TOPK).rearrange("p (t s) -> p t s", t=NT)
            selT = take(NT * TOPK).rearrange("p (t s) -> p t s", t=NT)
            nmax, wexp, wz, zz, rz, cw = take(1), take(NT), take(NT), take(1), take(1), take(NT)
            fxT = take(KT * TOPK).rearrange("p (k s) -> p k s", k=KT)
            hT = take(FT * TOPK).rearrange("p (k s) -> p k s", k=FT)
            outl = take(E)
            prod2 = take(E * NT)
            prod = prod2.rearrange("p (t e) -> p t e", t=NT)

            with nc.Block() as block:
                @block.sync
                def _(sp):
                    if first:
                        for t in range(NT):
                            sp.dma_start(X[:, t, :], A["x"][t * P:(t + 1) * P, :]).then_inc(S["x"], 16)
                    sp.dma_start(wr, row(A["Wr"])).then_inc(S["r"], 16)
                    sp.dma_start(br, row(A["br"])).then_inc(S["r"], 16)
                    sp.dma_start(b2, row(A["b2"])).then_inc(S["r"], 16)
                    sp.dma_start(b1, A["b1"]).then_inc(S["r"], 16)
                    sp.dma_start(w1, A["W1"].rearrange("(k p) f -> p k f", p=P)).then_inc(S["w"], 16)
                    sp.dma_start(w2, A["W2"].rearrange("(k p) e -> p k e", p=P)).then_inc(S["w"], 16)

                if first:
                    @block.gpsimd
                    def _(g):
                        g.memset(ones[:, :], 1.0).then_inc(S["const"], 1)
                        g.memset(causal[:, :], 0.0).then_inc(S["const"], 1)
                        g.iota(slots[:, :], pattern=[[1, P]], base=0, channel_multiplier=0,
                               allow_small_or_imprecise_dtypes=True).then_inc(S["const"], 1)
                        g.wait_ge(S["const"], 3)
                        g.affine_select(out=ident[:, :], in_=ones[:, :], compare_op=ALU.is_equal, fill=0.0, base=0,
                                        pattern=[[-1, P]], channel_multiplier=1).then_inc(S["const"], 1)
                        g.affine_select(out=upto[:, :], in_=ones[:, :], compare_op=ALU.is_ge, fill=0.0, base=0,
                                        pattern=[[1, P]], channel_multiplier=-1).then_inc(S["const"], 1)
                        g.affine_select(out=after[:, :], in_=ones[:, :], compare_op=ALU.is_gt, fill=0.0, base=0,
                                        pattern=[[-1, P]], channel_multiplier=1).then_inc(S["const"], 1)
                        g.affine_select(out=causal[:, :], in_=causal[:, :], compare_op=ALU.is_ge, fill=NEG, base=0,
                                        pattern=[[-1, P]], channel_multiplier=1).then_inc(S["const"], 1)

                @block.vector
                def _(v):
                    if first:
                        v.wait_ge(S["x"], 16 * NT)
                    ln_dve(v, S, M, X, XN, 1e-5)
                    v.wait_ge(S["r"], 64)
                    v.wait_ge(S["xn"], NT)
                    for t in range(NT):
                        v.tensor_tensor(prod[:, t, :], XN[:, t, :], wr, ALU.mult).then_inc(S["prod"], 1)
                    v.wait_ge(S["prod"], NT)
                    v.tensor_reduce(lcol, prod, AX.X, ALU.add).then_inc(S["wr"], 1)
                    v.wait_ge(S["wr"], 1)
                    v.tensor_scalar(lcol, lcol, br[:, 0:1], None, ALU.add).then_inc(S["lcol"], 1)
                    v.wait_ge(S["lcol"], 1)
                    v.tensor_copy(lbc, lcol.unsqueeze(2).to_broadcast([P, NT, P])).then_inc(S["lb"], 1)
                    v.wait_ge(S["ltr"], 1)
                    lrow = bank(2, 2)
                    v.tensor_reduce(nmax, lrow, AX.X, ALU.max, negate=True).then_inc(S["lmax"], 1)
                    v.memset(parts[:, 0, 0:1], 0.0).then_inc(S["rank"], 1)
                    for t in range(NT):
                        v.wait_ge(S["rank"], 3 * t if t else 1)
                        if t:
                            v.tensor_scalar(junk[:, 0:t * P], lrow[:, 0:t * P], lcol[:, t:t + 1], 0.0, ALU.is_ge,
                                            ALU.add, accum_out=parts[:, 0, t:t + 1]).then_inc(S["rank"], 1)
                        v.tensor_scalar(prod2[:, 0:T - t * P], lrow[:, t * P:T], lcol[:, t:t + 1], 0.0, ALU.is_gt,
                                        ALU.add, accum_out=parts[:, 1, t:t + 1]).then_inc(S["rank"], 1)
                        v.scalar_tensor_tensor(prod2[:, T:T + P], lrow[:, t * P:(t + 1) * P], lcol[:, t:t + 1],
                                               after[:, :], ALU.is_equal, ALU.mult,
                                               accum_out=parts[:, 2, t:t + 1]).then_inc(S["rank"], 1)
                    v.wait_ge(S["rank"], 3 * NT)
                    v.tensor_tensor(rank2, parts[:, 0, :], parts[:, 1, :], ALU.add).then_inc(S["rk"], 1)
                    v.wait_ge(S["rk"], 1)
                    v.tensor_tensor(rank, rank2, parts[:, 2, :], ALU.add).then_inc(S["rk"], 1)
                    v.wait_ge(S["rk"], 2)
                    for t in range(NT):
                        v.tensor_scalar(sel[:, t, :], slots[:, :], rank[:, t:t + 1], None,
                                        ALU.is_equal).then_inc(S["sel"], 1)
                    v.tensor_scalar(mask, rank, float(TOPK), None, ALU.is_lt).then_inc(S["rk"], 1)
                    v.wait_ge(S["wexp"], 1)
                    v.wait_ge(S["rk"], 3)
                    v.tensor_tensor(wz, wexp, mask, ALU.mult).then_inc(S["wz"], 1)
                    v.wait_ge(S["zs"], 1)
                    v.tensor_reduce(zz, bank(4)[:, 0:NT], AX.X, ALU.add).then_inc(S["z"], 1)
                    v.wait_ge(S["z"], 1)
                    v.reciprocal(rz, zz).then_inc(S["rz"], 1)
                    v.wait_ge(S["rz"], 1)
                    v.tensor_scalar(cw, wexp, rz[:, 0:1], 0.5, ALU.mult, ALU.mult).then_inc(S["cw"], 1)
                    v.wait_ge(S["g"], 1)
                    v.tensor_copy(fxT, bank(5)[:, 0:KT * TOPK].rearrange("p (k s) -> p k s", k=KT)).then_inc(S["gc"], 1)
                    for g in range(2):
                        v.wait_ge(S["seltr"], g + 1)
                        v.tensor_copy(selT[:, 4 * g:4 * g + 4, :],
                                      bank(6 + g).rearrange("p (t s) -> p t s", t=4)).then_inc(S["selTev"], 1)
                    for t in range(NT):
                        v.scalar_tensor_tensor(X[:, t, :], XN[:, t, :], 0.5, X[:, t, :], ALU.mult,
                                               ALU.add).then_inc(S["half"], 1)
                    v.wait_ge(S["dn"], 1)
                    v.tensor_tensor(outl, bank(2)[:, 0:E], b2, ALU.add).then_inc(S["ol"], 1)
                    v.wait_ge(S["half"], NT)
                    v.wait_ge(S["cw"], 1)
                    for t in range(NT):
                        v.wait_ge(S["sc"], t + 1)
                        v.scalar_tensor_tensor(X[:, t, :], bank(4 + t % 2)[:, 0:E], cw[:, t:t + 1], X[:, t, :],
                                               ALU.mult, ALU.add).then_inc(S["res"], 1)

                @block.scalar
                def _(act):
                    ln_sqrt(act, S, M)
                    act.wait_ge(S["lmax"], 1)
                    nc.scalar.activation(wexp, lcol, ACT.Exp, bias=nmax[:, 0:1]).then_inc(S["wexp"], 1)
                    for f in range(FT):
                        act.wait_ge(S["up"], f + 1)
                        nc.scalar.activation(hT[:, f, :], bank(2 + f % 2)[:, 0:TOPK], ACT.Gelu,
                                             bias=b1[:, f:f + 1]).then_inc(S["hT"], 1)

                @block.tensor
                def _(pe):
                    if first:
                        pe.wait_ge(S["const"], 7)
                    pe.wait_ge(S["lb"], 1)
                    for t in range(NT):
                        last = pe.transpose(bank(2, 2)[:, t * P:(t + 1) * P], lbc[:, t, :], ident[:, :])
                    last.then_inc(S["ltr"], 1)
                    pe.wait_ge(S["sel"], NT)
                    for k in range(KT):
                        last = proj(pe, bank(5)[:, k * TOPK:(k + 1) * TOPK],
                                    lambda t: XN[:, t, k * P:(k + 1) * P], lambda t: sel[:, t, :], NT)
                    last.then_inc(S["g"], 1)
                    for t in range(NT):
                        last = pe.transpose(bank(6 + t // 4)[:, t % 4 * P:(t % 4 + 1) * P], sel[:, t, :], ident[:, :])
                        if t % 4 == 3:
                            last.then_inc(S["seltr"], 1)
                    pe.wait_ge(S["wz"], 1)
                    pe.matmul(bank(4)[:, 0:NT], ones[:, :], wz, start=True, stop=True).then_inc(S["zs"], 1)
                    pe.wait_ge(S["gc"], 1)
                    pe.wait_ge(S["w"], 32)
                    pe.wait_ge(S["rank"], 3 * NT)
                    for f in range(FT):
                        if f >= 2:
                            pe.wait_ge(S["hT"], f - 1)
                        proj(pe, bank(2 + f % 2)[:, 0:TOPK], lambda k: w1[:, k, f * P:(f + 1) * P],
                             lambda k: fxT[:, k, :], KT).then_inc(S["up"], 1)
                    pe.wait_ge(S["hT"], FT)
                    proj(pe, bank(2)[:, 0:E], lambda k: hT[:, k, :], lambda k: w2[:, k, :], FT).then_inc(S["dn"], 1)
                    pe.wait_ge(S["selTev"], 2)
                    pe.wait_ge(S["ol"], 1)
                    pe.wait_ge(S["z"], 1)
                    for t in range(NT):
                        if t >= 2:
                            pe.wait_ge(S["res"], t - 1)
                        pe.matmul(bank(4 + t % 2)[:, 0:E], selT[:, t, :], outl, start=True, stop=True).then_inc(S["sc"], 1)

        def mamba():
            take = Region()
            BTOK = take(GM * T).rearrange("p (g c n) -> p g c n", g=GM, c=NT)
            CB = take(GM * T).rearrange("p (g t) -> p g t", g=GM)
            cwt = take((HM + 2 * GM + 1) * CW).rearrange("p (n w) -> p n w", w=CW)
            dt, dtend, etot = (take(HM * NT) for _ in range(3))
            cum = take((HM + 1) * NT)
            nw = take(HM)
            dskip = take(HM)
            spare = take(32)
            wx = take(2 * E).rearrange("p (b k c) -> p b k c", b=2, k=KT)
            raw = take(T + CONV - 1)
            xT = take(2 * T).rearrange("p (b t) -> p b t", b=2)
            CT = arena[:, take.at:take.at + (GM + 1) * T].rearrange("p (g t) -> p g t", g=GM + 1)
            take(GM * T)
            common = take.at
            take(T)
            bT = take(2 * T).rearrange("p (b t) -> p b t", b=2)
            raw2 = take(T + CONV - 1)

            def col(ap, i):
                return ap[:, bass.ds(i, 1)]

            def tap_of(tile, w):
                return cwt[:, bass.ds(tile, 1), w:w + 1].rearrange("p o w -> p (o w)")

            def one_tap(v, S, b, n, tile, raw, w, ahead=2):
                if w:
                    v.wait_ge(S["tap"], n * (CONV - 2) + w)
                else:
                    v.wait_ge(S["c"], n + ahead)
                v.scalar_tensor_tensor(xT[:, b, :], raw[:, w:w + T], tap_of(tile, w), xT[:, b, :], ALU.mult,
                                       ALU.add).then_inc(S["tap"] if w < CONV - 2 else S["conv"], 1)

            def conv_taps(v, S, b, n, tile, raw, ahead=2):
                for w in range(CONV - 1):
                    one_tap(v, S, b, n, tile, raw, w, ahead)

            def conv_newest(act, S, b, tile, raw, at=0):
                nc.scalar.copy(raw[:, CONV - 1:], bank(at, 2)).then_inc(S["raw"], 1)
                nc.scalar.activation(xT[:, b, :], bank(at, 2), ACT.Identity, bias=tap_of(tile, CONV),
                                     scale=tap_of(tile, CONV - 1)).then_inc(S["c"], 1)

            def channels(pe, w, at=0):
                for h in range(2):
                    last = proj(pe, bank(at + h), lambda k: w[:, k, :], lambda k: XNT[:, k, h * HALF:(h + 1) * HALF], KT)
                return last

            S2 = sems("mb", "w0 w1 pj raw c tap conv xt bt btok cbp cb")
            S3 = sems("mm", "wx0 wx1 wg0 wg1 cr0 cr1 wo px pg raw c tap conv xt tx xd xs ds rc st ec cs df lm mm"
                      " y yd sg u sqs ad vr vv sd rr wos op oc")

            take.at = common
            M = ln_region(take)
            wdt = take(KT * HM).rearrange("p (k h) -> p k h", k=KT)
            dtb, alog, aneg = take(HM), take(HM), take(HM)
            z, za, ze, zl, a, dend = (take(HM * NT) for _ in range(6))
            cumT = take(2 * P).rearrange("p (b l) -> p b l", b=2)
            S = sems("mp", LN + " r dtp z za ze zl dt alog a cs sfx tot cum dend etot ctr cT scr pad dte")
            with nc.Block() as block:
                @block.sync
                def _(sp):
                    sp.dma_start(wdt, A["w_dt"].rearrange("(k p) h -> p k h", p=P)).then_inc(S["r"], 16)
                    sp.dma_start(dtb, row(A["dt_bias"])).then_inc(S["r"], 16)
                    sp.dma_start(alog, row(A["A_log"])).then_inc(S["r"], 16)
                    sp.dma_start(cwt, A["conv"].rearrange("(n p) w -> p n w", p=P)).then_inc(S["r"], 16)
                    sp.dma_start(nw, A["norm_w"]).then_inc(S["r"], 16)
                    sp.dma_start(dskip, row(A["D"])).then_inc(S["r"], 16)
                    sp.wait_ge(S["cT"], 1)
                    for b in range(2):
                        sp.dma_start(A["cum_rows"][b * P:(b + 1) * P, :], cumT[:, b, :]).then_inc(S["scr"], 16)
                    sp.dma_start(A["cum_rows"][HM * NT:(HM + 1) * NT, :], cumT[0:NT, 0, :]).then_inc(S["scr"], 16)
                    sp.wait_ge(S["r"], 96)
                    sp.wait_ge(S["scr"], 48)

                @block.gpsimd
                def _(g):
                    g.memset(raw[:, 0:CONV - 1], 0.0).then_inc(S["pad"], 1)
                    g.memset(raw2[:, 0:CONV - 1], 0.0).then_inc(S["pad"], 1)
                    credit(g, spare, [(S2["pj"], 2), (S2["c"], 2), (S2["cbp"], 2), (S2["btok"], 1), (S2["cb"], 1)]
                           + [(S3[n], 1) for n in "c st y yd ds sg u ad vr vv op oc ec".split()]
                           + [(S3[n], 2) for n in "px pg".split()])

                @block.vector
                def _(v):
                    ln_dve(v, S, M, X, XN, 1e-5)
                    v.wait_ge(S["r"], 96)
                    v.wait_ge(S["dtp"], 1)
                    pd = bank(2)[:, 0:HM * NT].rearrange("p (c h) -> p c h", c=NT)
                    for t in range(NT):
                        v.tensor_tensor(z.rearrange("p (h c) -> p c h", c=NT)[:, t, :], pd[:, t, :], dtb,
                                        ALU.add).then_inc(S["z"], 1)
                    v.wait_ge(S["zl"], 1)
                    v.scalar_tensor_tensor(dt, z, 0.0, zl, ALU.max, ALU.add).then_inc(S["dt"], 1)
                    v.wait_ge(S["dt"], 1)
                    v.wait_ge(S["alog"], 1)
                    v.scalar_tensor_tensor(a.rearrange("p (h c) -> p h c", c=NT), dt.rearrange("p (h c) -> p h c", c=NT),
                                           -1.0, aneg.unsqueeze(2).to_broadcast([P, HM, NT]), ALU.mult,
                                           ALU.mult).then_inc(S["a"], 1)
                    v.wait_ge(S["cs"], 1)
                    v.tensor_copy(cum[:, 0:HM * NT], bank(3)[:, 0:HM * NT]).then_inc(S["cum"], 1)
                    v.tensor_copy(cum[:, HM * NT:], bank(3)[:, 0:NT]).then_inc(S["cum"], 1)
                    v.wait_ge(S["dend"], 1)
                    v.tensor_tensor(dtend, dt, dend, ALU.mult).then_inc(S["dte"], 1)
                    v.wait_ge(S["ctr"], 1)
                    v.tensor_copy(cumT, bank(6)[:, 0:2 * P].rearrange("p (b l) -> p b l", b=2)).then_inc(S["cT"], 1)

                @block.scalar
                def _(act):
                    ln_sqrt(act, S, M)
                    ln_copy(act, S)
                    act.wait_ge(S["r"], 96)
                    nc.scalar.activation(aneg, alog, ACT.Exp).then_inc(S["alog"], 1)
                    act.wait_ge(S["z"], NT)
                    nc.scalar.activation(za, z, ACT.Abs).then_inc(S["za"], 1)
                    act.wait_ge(S["za"], 1)
                    nc.scalar.activation(ze, za, ACT.Exp, scale=-1.0).then_inc(S["ze"], 1)
                    act.wait_ge(S["ze"], 1)
                    nc.scalar.activation(zl, ze, ACT.Ln, bias=1.0).then_inc(S["zl"], 1)
                    act.wait_ge(S["sfx"], 1)
                    nc.scalar.activation(dend, bank(4)[:, 0:HM * NT], ACT.Exp).then_inc(S["dend"], 1)
                    act.wait_ge(S["tot"], 1)
                    nc.scalar.activation(etot, bank(5)[:, 0:HM * NT], ACT.Exp).then_inc(S["etot"], 1)

                @block.tensor
                def _(pe):
                    ln_pe(pe, S)
                    pe.wait_ge(S["xnT"], NT // 2)
                    pe.wait_ge(S["r"], 96)
                    for t in range(NT):
                        last = proj(pe, bank(2)[:, t * HM:(t + 1) * HM], lambda k: XNT[:, k, t * P:(t + 1) * P],
                                    lambda k: wdt[:, k, :], KT)
                    last.then_inc(S["dtp"], 1)
                    pe.wait_ge(S["a"], 1)
                    pe.matmul(bank(3)[:, 0:HM * NT], upto[:, :], a, start=True, stop=True).then_inc(S["cs"], 1)
                    pe.matmul(bank(4)[:, 0:HM * NT], after[:, :], a, start=True, stop=True).then_inc(S["sfx"], 1)
                    pe.matmul(bank(5)[:, 0:HM * NT], ones[:, :], a, start=True, stop=True).then_inc(S["tot"], 1)
                    pe.wait_ge(S["cum"], 1)
                    for b in range(2):
                        last = pe.transpose(bank(6)[:, b * P:(b + 1) * P], cum[:, b * P:(b + 1) * P], ident[:, :])
                    last.then_inc(S["ctr"], 1)

            raws = [raw, raw2]
            S = S2
            first_tile = [BTILE, CTILE]

            def group_tile(g, i):
                return A["w_in"][bass.ds(g + first_tile[i], 1), :, :, :].rearrange("o p k c -> p (o k) c")

            with nc.Block() as block:
                @block.sync
                def _(sp):
                    for i in range(2):
                        sp.dma_start(wx[:, i, :, :], A["w_in"][first_tile[i]]).then_inc(S["w" + str(i)], 16)
                    with sp.Fori(0, GM) as g:
                        for i in range(2):
                            sp.wait_ge(S["pj"], g * 2 + i + 3)
                            sp.dma_start(wx[:, i, :, :], group_tile(g + 1, i)).then_inc(S["w" + str(i)], 16)

                def project(pe, g, i):
                    pe.wait_ge(S["w" + str(i)], g * 16 + 16)
                    pe.wait_ge(S["c"], g * 2 + i + 1)
                    channels(pe, wx[:, i, :, :], 2 * i).then_inc(S["pj"], 1)

                @block.tensor
                def _(pe):
                    for i in range(2):
                        project(pe, 0, i)
                    with pe.Fori(0, GM // 2) as it:
                        for j in range(2):
                            g = it * 2 + j
                            for i in range(2):
                                project(pe, g + 1, i)
                            pe.wait_ge(S["xt"], g * 2 + 1)
                            pe.wait_ge(S["btok"], g + 1)
                            for c in range(NT):
                                last = pe.transpose(bank(4, 2)[:, c * P:(c + 1) * P], bT[:, j, c * P:(c + 1) * P],
                                                    ident[:, :])
                            last.then_inc(S["bt"], 1)
                            pe.wait_ge(S["xt"], g * 2 + 2)
                            pe.wait_ge(S["cb"], g + 1)
                            for c in range(NT):
                                last = pe.matmul(bank(6, 2)[:, c * P:(c + 1) * P], bT[:, j, c * P:(c + 1) * P],
                                                 CT[:, bass.ds(g, 1), c * P:(c + 1) * P].rearrange("p o t -> p (o t)"),
                                                 start=True, stop=True)
                            last.then_inc(S["cbp"], 1)

                def newest(act, g, i):
                    act.wait_ge(S["pj"], g * 2 + i + 3)
                    conv_newest(act, S, i, g + (first_tile[i] - HM), raws[i], 2 * i)

                def silus(act, g, b):
                    act.wait_ge(S["conv"], g * 2 + 1)
                    act.wait_ge(S["cbp"], g + 1)
                    nc.scalar.activation(bT[:, b, :], xT[:, 0, :], ACT.Silu).then_inc(S["xt"], 1)
                    act.wait_ge(S["conv"], g * 2 + 2)
                    nc.scalar.activation(CT[:, bass.ds(g, 1), :].rearrange("p o t -> p (o t)"), xT[:, 1, :],
                                         ACT.Silu).then_inc(S["xt"], 1)

                @block.scalar
                def _(act):
                    for i in range(2):
                        newest(act, 0, i)
                    act.wait_ge(S["conv"], 1)
                    nc.scalar.activation(bT[:, 0, :], xT[:, 0, :], ACT.Silu).then_inc(S["xt"], 1)
                    act.wait_ge(S["conv"], 2)
                    nc.scalar.activation(CT[:, 0, :], xT[:, 1, :], ACT.Silu).then_inc(S["xt"], 1)
                    with act.Fori(0, GM // 2) as it:
                        for j in range(2):
                            g = it * 2 + j
                            for i in range(2):
                                act.wait_ge(S["xt"], g * 2 + i + 1)
                                newest(act, g + 1, i)
                            silus(act, g + 1, 1 - j)

                @block.vector
                def _(v):
                    for i in range(2):
                        conv_taps(v, S, i, i, first_tile[i] - HM, raws[i], 3)
                    with v.Fori(0, GM) as g:
                        for i in range(2):
                            conv_taps(v, S, i, g * 2 + (i + 2), g + (first_tile[i] - HM + 1), raws[i], 3)
                        v.wait_ge(S["bt"], g + 1)
                        v.tensor_copy(BTOK[:, bass.ds(g, 1), :, :].rearrange("p o c n -> p (o c n)"),
                                      bank(4, 2)).then_inc(S["btok"], 1)
                        v.wait_ge(S["cbp"], g + 3)
                        v.tensor_tensor(CB[:, bass.ds(g, 1), :].rearrange("p o (c l) -> p (o c) l", c=NT),
                                        bank(6, 2).rearrange("p (c l) -> p c l", c=NT),
                                        upto[:, :].unsqueeze(1).to_broadcast([P, NT, P]), ALU.mult).then_inc(S["cb"], 1)

            take.at = common
            wg = take(2 * E).rearrange("p (b k c) -> p b k c", b=2, k=KT)
            lam = take(2 * T).rearrange("p (b t) -> p b t", b=2)
            ecs = take(T)
            cumrow = take(2 * T).rearrange("p (b t) -> p b t", b=2)
            xdt, xst, states = take(T), take(T), take(T)
            U = take(4 * T).rearrange("p (j t) -> p j t", j=4)
            sumsq, sq = take(T), take(T)
            wo = take(4 * E).rearrange("p (j e) -> p j e", j=4)
            ve, sd, rr = take(NT), take(NT), take(NT)
            cum_rows = A["cum_rows"].rearrange("(h c) l -> h (c l)", c=NT)
            w_out = A["w_out"].rearrange("(n p) e -> p n e", p=P)
            S = S3
            OCT = GM
            PASSES = HM // OCT
            chunk3 = "p (c l) -> p c l"

            def w_tile(i):
                return A["w_in"][bass.ds(i, 1), :, :, :].rearrange("o p k c -> p (o k) c")

            with nc.Block() as block:
                @block.sync
                def _(sp):
                    sp.dma_start(wx[:, 0, :, :], A["w_in"][XTILE]).then_inc(S["wx0"], 16)
                    sp.dma_start(cumrow[:, 0, :], cum_rows[0:1, :].to_broadcast([P, T])).then_inc(S["cr0"], 16)
                    with sp.Fori(0, PASSES) as it:
                        for j in range(OCT):
                            K, b = it * OCT + j, j % 2
                            if j % 4 == 1:
                                G = it * 2 + j // 4
                                sp.wait_ge(S["op"], G * NT + 1)
                                sp.dma_start(wo, w_out[:, bass.ds(K - 1, 4), :]).then_inc(S["wo"], 16)
                            sp.wait_ge(S["px"], K + 2)
                            sp.dma_start(wx[:, 1 - b, :, :], w_tile(K + (XTILE + 1))).then_inc(S["wx" + str(1 - b)], 16)
                            sp.wait_ge(S["pg"], K + 1)
                            sp.dma_start(wg[:, b, :, :], w_tile(K)).then_inc(S["wg" + str(b)], 16)
                            sp.wait_ge(S["ec"], K + 1)
                            sp.dma_start(cumrow[:, 1 - b, :], cum_rows[bass.ds(K + 1, 1), :].to_broadcast([P, T]))\
                              .then_inc(S["cr" + str(1 - b)], 16)

                def out_proj(pe, G):
                    pe.wait_ge(S["ad"], G * 3 + 4)
                    pe.wait_ge(S["vv"], G + 1)
                    pe.wait_ge(S["oc"], G * NT + 1)
                    for t in range(NT):
                        last = pe.matmul(bank(6)[:, t:t + 1], sumsq[:, t * P:(t + 1) * P], ones[:, 0:1],
                                         start=True, stop=True)
                    last.then_inc(S["vr"], 1)
                    pe.wait_ge(S["wos"], G + 1)
                    for t in range(NT):
                        if t == 1:
                            pe.wait_ge(S["vv"], G + 2)
                        if t >= 2:
                            pe.wait_ge(S["oc"], G * NT + t)
                        proj(pe, bank(7 - t % 2)[:, 0:E], lambda i: U[:, i, t * P:(t + 1) * P],
                             lambda i: wo[:, i, :], 4).then_inc(S["op"], 1)

                @block.tensor
                def _(pe):
                    pe.wait_ge(S["wx0"], 16)
                    channels(pe, wx[:, 0, :, :]).then_inc(S["px"], 1)
                    with pe.Fori(0, PASSES) as it:
                        for j in range(OCT):
                            K, b, c0 = it * OCT + j, j % 2, it * (OCT // 2) + j // 2
                            pe.wait_ge(S["xt"], K + 1)
                            pe.wait_ge(S["st"], K + 1)
                            for c in range(NT):
                                last = pe.transpose(bank(2, 2)[:, c * P:(c + 1) * P], xT[:, b, c * P:(c + 1) * P],
                                                    ident[:, :])
                            last.then_inc(S["tx"], 1)
                            pe.wait_ge(S["wx" + str(1 - b)], (it * (OCT // 2) + (j + 1) // 2 + 1) * 16)
                            pe.wait_ge(S["sg"], K + 1)
                            channels(pe, wx[:, 1 - b, :, :]).then_inc(S["px"], 1)
                            pe.wait_ge(S["xs"], K + 1)
                            pe.wait_ge(S["xd"], K + 1)
                            for c in range(NT - 1):
                                last = pe.matmul(bank(2, 2)[:, c * P:(c + 1) * P], BTOK[:, j, c, :],
                                                 xst[:, c * P:(c + 1) * P], start=True, stop=True)
                            last.then_inc(S["ds"], 1)
                            if j == 4:
                                out_proj(pe, it * 2)
                            pe.wait_ge(S["wg" + str(b)], (c0 + 1) * 16)
                            pe.wait_ge(S["c"], K + 3)
                            channels(pe, wg[:, b, :, :]).then_inc(S["pg"], 1)
                            pe.wait_ge(S["mm"], K + 1)
                            pe.wait_ge(S["cs"], K + 1)
                            pe.wait_ge(S["st"], K + 2)
                            pe.wait_ge(S["yd"], K + 1)
                            for c in range(NT):
                                r = slice(c * P, (c + 1) * P)
                                last = pe.matmul(bank(4, 2)[:, r], xdt[:, r], lam[:, b, r], start=True, stop=(c == 0))
                                if c:
                                    last = pe.matmul(bank(4, 2)[:, r], states[:, (c - 1) * P:c * P], ecs[:, r],
                                                     start=False, stop=True)
                            last.then_inc(S["y"], 1)
                        out_proj(pe, it * 2 + 1)

                @block.scalar
                def _(act):
                    act.wait_ge(S["px"], 3)
                    conv_newest(act, S, 0, 0, raw)
                    act.wait_ge(S["conv"], 1)
                    nc.scalar.activation(xT[:, 0, :], xT[:, 0, :], ACT.Silu).then_inc(S["xt"], 1)
                    act.wait_ge(S["df"], 1)
                    nc.scalar.activation(lam[:, 0, :], lam[:, 0, :], ACT.Exp).then_inc(S["lm"], 1)

                    def root(G):
                        act.wait_ge(S["vv"], G + 2)
                        nc.scalar.activation(sd, ve, ACT.Sqrt).then_inc(S["sd"], 1)

                    with act.Fori(0, PASSES) as it:
                        for j in range(OCT):
                            K, b, G = it * OCT + j, j % 2, it * 2 + j // 4
                            act.wait_ge(S["cr" + str(b)], (it * (OCT // 2) + j // 2 + 1) * 16)
                            act.wait_ge(S["y"], K + 1)
                            nc.scalar.activation(ecs, cumrow[:, b, :], ACT.Exp).then_inc(S["ec"], 1)
                            act.wait_ge(S["px"], K + 4)
                            act.wait_ge(S["u"], K + 1)
                            conv_newest(act, S, 1 - b, K + 1, raw)
                            act.wait_ge(S["conv"], K + 2)
                            nc.scalar.activation(xT[:, 1 - b, :], xT[:, 1 - b, :], ACT.Silu).then_inc(S["xt"], 1)
                            if j == 4:
                                root(it * 2)
                            act.wait_ge(S["pg"], K + 3)
                            act.wait_ge(S["op"], G * NT + 1)
                            nc.scalar.activation(U[:, j % 4, :], bank(0, 2), ACT.Silu).then_inc(S["sg"], 1)
                            act.wait_ge(S["df"], K + 2)
                            nc.scalar.activation(lam[:, 1 - b, :], lam[:, 1 - b, :], ACT.Exp).then_inc(S["lm"], 1)
                            act.wait_ge(S["u"], K + 2)
                            if j % 4 == 0:
                                act.wait_ge(S["vr"], G + 1)
                                nc.scalar.activation(sumsq, U[:, 0, :], ACT.Square).then_inc(S["sqs"], 1)
                            else:
                                act.wait_ge(S["ad"], G * 3 + j % 4)
                                nc.scalar.activation(sq, U[:, j % 4, :], ACT.Square).then_inc(S["sqs"], 1)
                        root(it * 2 + 1)

                @block.gpsimd
                def _(g):
                    with g.Fori(0, PASSES) as it:
                        for j in range(OCT):
                            K, b, G = it * OCT + j, j % 2, it * 2 + j // 4
                            if j % 4 == 2:
                                g.wait_ge(S["wo"], G * 16 + 16)
                                g.tensor_tensor(wo, wo, nw[:, bass.ds(K - 2, 4)].unsqueeze(2).to_broadcast([P, 4, E]),
                                                ALU.mult).then_inc(S["wos"], 1)
                            g.wait_ge(S["ec"], K + 2)
                            g.tensor_tensor(ecs, ecs, CT[:, j, :], ALU.mult).then_inc(S["cs"], 1)
                            if j % 4:
                                g.wait_ge(S["sqs"], K + 1)
                                g.wait_ge(S["ad"], G * 3 + j % 4)
                                g.tensor_tensor(sumsq, sumsq, sq, ALU.add).then_inc(S["ad"], 1)

                @block.vector
                def _(v):
                    conv_taps(v, S, 0, 0, 0, raw)

                    def difference(K, b, c):
                        return v.tensor_scalar(lam[:, b, c * P:(c + 1) * P], cumrow[:, b, c * P:(c + 1) * P],
                                               col(cum, K * NT + c), 0.0, ALU.subtract, ALU.min)

                    v.wait_ge(S["cr0"], 16)
                    for c in range(NT):
                        last = difference(0, 0, c)
                    last.then_inc(S["df"], 1)

                    def normalise(G):
                        v.wait_ge(S["vr"], G + 2)
                        v.tensor_scalar(ve, bank(6)[:, 0:NT], 1.0 / (4 * P), 1e-6, ALU.mult, ALU.add).then_inc(S["vv"], 1)
                        v.wait_ge(S["sd"], G + 1)
                        v.reciprocal(rr, sd).then_inc(S["rr"], 1)
                        v.wait_ge(S["rr"], G + 1)
                        for t in range(NT):
                            v.wait_ge(S["op"], G * NT + (t + 2))
                            v.scalar_tensor_tensor(X[:, t, :], bank(7 - t % 2)[:, 0:E], rr[:, t:t + 1], X[:, t, :],
                                                   ALU.mult, ALU.add).then_inc(S["oc"], 1)

                    with v.Fori(0, PASSES) as it:
                        for j in range(OCT):
                            K, b = it * OCT + j, j % 2
                            v.wait_ge(S["tx"], K + 1)
                            v.wait_ge(S["ds"], K + 1)
                            v.tensor_tensor(xst.rearrange(chunk3, c=NT), bank(2, 2).rearrange(chunk3, c=NT),
                                            dtend[:, bass.ds(K * NT, NT)].unsqueeze(2).to_broadcast([P, NT, P]),
                                            ALU.mult).then_inc(S["xs"], 1)
                            v.wait_ge(S["y"], K + 1)
                            v.tensor_tensor(xdt.rearrange(chunk3, c=NT), bank(2, 2).rearrange(chunk3, c=NT),
                                            dt[:, bass.ds(K * NT, NT)].unsqueeze(2).to_broadcast([P, NT, P]),
                                            ALU.mult).then_inc(S["xd"], 1)
                            v.wait_ge(S["lm"], K + 1)
                            v.tensor_tensor(lam[:, b, :], lam[:, b, :], CB[:, j, :], ALU.mult).then_inc(S["mm"], 1)
                            v.wait_ge(S["ds"], K + 2)
                            v.tensor_copy(states[:, 0:P], bank(2, 2)[:, 0:P]).then_inc(S["rc"], 1)
                            v.wait_ge(S["cr" + str(1 - b)], (it * (OCT // 2) + (j + 1) // 2 + 1) * 16)
                            for c in range(1, NT - 1):
                                difference(K + 1, 1 - b, c - 1)
                                v.wait_ge(S["rc"], K * (NT - 2) + c)
                                v.scalar_tensor_tensor(states[:, c * P:(c + 1) * P], states[:, (c - 1) * P:c * P],
                                                       col(etot, K * NT + c), bank(2, 2)[:, c * P:(c + 1) * P],
                                                       ALU.mult, ALU.add).then_inc(S["rc"] if c < NT - 2 else S["st"], 1)
                            difference(K + 1, 1 - b, NT - 2)
                            difference(K + 1, 1 - b, NT - 1).then_inc(S["df"], 1)
                            conv_taps(v, S, 1 - b, K + 1, K + 1, raw)
                            if j == 4:
                                normalise(it * 2)
                            v.wait_ge(S["y"], K + 2)
                            v.scalar_tensor_tensor(xT[:, b, :], xT[:, b, :], col(dskip, K), bank(4, 2), ALU.mult,
                                                   ALU.add).then_inc(S["yd"], 1)
                            v.wait_ge(S["yd"], K + 2)
                            v.wait_ge(S["sg"], K + 2)
                            v.tensor_tensor(U[:, j % 4, :], U[:, j % 4, :], xT[:, b, :], ALU.mult).then_inc(S["u"], 1)
                        normalise(it * 2 + 1)

        def ponder_ffn(name, last_phase):
            take = Region()
            S = sems(name, LN + " w r c pad o_stats o_aggr o_ve o_sd o_rstd o_xn m d q vr ve2 sd2 rc n g t"
                     " ap th up hb h dn b1 bc bcr gp gs sg mul out og ob fin st")
            SO = {k: S["o_" + k] for k in "stats aggr ve sd rstd xn".split()}
            M, MO = ln_region(take), ln_region(take)
            cols = take(6 * KT).rearrange("p (n k) -> p n k", k=KT)
            in_g, in_b, agg_b, pn_g, pn_b, d2_b = (cols[:, i, :] for i in range(6))
            d1_b = take(FT)
            agg = take(KT * E).rearrange("p (k e) -> p k e", k=KT)
            bcw = take(KT * E).rearrange("p (k e) -> p k e", k=KT)
            gw = take(KT * E).rearrange("p (k e) -> p k e", k=KT)
            d1 = take(KT * DFF).rearrange("p (k f) -> p k f", k=KT)
            d2 = take(FT * E).rearrange("p (k e) -> p k e", k=FT)
            gb, bcb, out_g, out_b, bcrow = (take(E) for _ in range(5))
            mean_w, negmean_w = take(P), take(P)
            dev, dsq, tn, tt, th, th2 = (take(KT) for _ in range(6))
            hb, hh = take(FT), take(FT)
            var, vsd, vrs = take(1), take(1), take(1)
            SG = take(NT * E).rearrange("p (t e) -> p t e", t=NT)

            def wide(r):
                return r.unsqueeze(1).to_broadcast([P, NT, E])

            with nc.Block() as block:
                @block.sync
                def _(sp):
                    for dst, src in ((gb, "gate_b"), (bcb, "bc_b"), (out_g, "out_g"), (out_b, "out_b")):
                        sp.dma_start(dst, row(A[src])).then_inc(S["r"], 16)
                    sp.dma_start(cols, A["cols"]).then_inc(S["r"], 16)
                    sp.dma_start(d1_b, A["d1_b"]).then_inc(S["r"], 16)
                    for dst, src in ((agg, "agg_w"), (gw, "gate_w"), (d1, "d1_w"), (d2, "d2_w"), (bcw, "bc_w")):
                        sp.dma_start(dst, A[src].rearrange("(k p) f -> p k f", p=P)).then_inc(S["w"], 16)
                    if last_phase:
                        for t in range(NT):
                            sp.wait_ge(S["fin"], t + 1)
                            sp.dma_start(out[t * P:(t + 1) * P, :], X[:, t, :]).then_inc(S["st"], 16)
                        sp.wait_ge(S["st"], 16 * NT)

                @block.gpsimd
                def _(g):
                    g.memset(mean_w, 1.0 / E).then_inc(S["pad"], 1)
                    g.memset(negmean_w, -1.0 / E).then_inc(S["pad"], 1)

                def col_ln_dve(v, src, n, gamma, beta):
                    v.wait_ge(S["m"], n + 1)
                    v.tensor_scalar(dev, src, bank(2)[:, 0:1], None, ALU.add).then_inc(S["d"], 1)
                    v.wait_ge(S["d"], n + 1)
                    v.tensor_tensor(dsq, dev, dev, ALU.mult).then_inc(S["q"], 1)
                    v.wait_ge(S["vr"], n + 1)
                    v.tensor_scalar(var, bank(3)[:, 0:1], 1e-6, None, ALU.add).then_inc(S["ve2"], 1)
                    v.wait_ge(S["sd2"], n + 1)
                    v.reciprocal(vrs, vsd).then_inc(S["rc"], 1)
                    v.wait_ge(S["rc"], n + 1)
                    v.scalar_tensor_tensor(tn, dev, vrs[:, 0:1], gamma, ALU.mult, ALU.mult).then_inc(S["n"], 1)
                    v.wait_ge(S["n"], n + 1)
                    v.tensor_tensor(tt, tn, beta, ALU.add).then_inc(S["t"], 1)

                def col_ln_act(act, n):
                    act.wait_ge(S["ve2"], n + 1)
                    nc.scalar.activation(vsd, var, ACT.Sqrt).then_inc(S["sd2"], 1)

                def col_ln_pe(pe, src, n):
                    proj(pe, bank(2)[:, 0:1], lambda k: negmean_w, lambda k: src[:, k:k + 1], KT).then_inc(S["m"], 1)
                    pe.wait_ge(S["q"], n + 1)
                    proj(pe, bank(3)[:, 0:1], lambda k: mean_w, lambda k: dsq[:, k:k + 1], KT).then_inc(S["vr"], 1)

                newest = XNT[:, :, T - 1]

                @block.tensor
                def _(pe):
                    ln_pe(pe, S)
                    pe.wait_ge(S["xnT"], NT // 2)
                    pe.wait_ge(S["pad"], 2)
                    col_ln_pe(pe, newest, 0)
                    pe.wait_ge(S["w"], 16 * 5)
                    def gates(g):
                        if g >= 2:
                            pe.wait_ge(S["gs"], g - 1)
                        for h in range(2):
                            t = 2 * g + h
                            last = proj(pe, bank(6 + g % 2)[:, h * E:(h + 1) * E],
                                        lambda k: XNT[:, k, t * P:(t + 1) * P], lambda k: gw[:, k, :], KT)
                        last.then_inc(S["gp"], 1)
                    for g in range(NT // 2):
                        gates(g)
                    pe.wait_ge(S["t"], 1)
                    for m in range(KT):
                        last = proj(pe, bank(4)[:, m:m + 1], lambda k: agg[:, k, m * P:(m + 1) * P],
                                    lambda k: tt[:, k:k + 1], KT)
                    last.then_inc(S["ap"], 1)
                    with pe.Fori(0, 4) as i:
                        pe.wait_ge(S["th"], i + 1)
                        col_ln_pe(pe, th, i + 1)
                        pe.wait_ge(S["t"], i + 2)
                        for f in range(FT):
                            last = proj(pe, bank(5)[:, f:f + 1], lambda k: d1[:, k, f * P:(f + 1) * P],
                                        lambda k: tt[:, k:k + 1], KT)
                        last.then_inc(S["up"], 1)
                        pe.wait_ge(S["h"], i + 1)
                        for m in range(KT):
                            last = proj(pe, bank(4)[:, m:m + 1], lambda k: d2[:, k, m * P:(m + 1) * P],
                                        lambda k: hh[:, k:k + 1], FT)
                        last.then_inc(S["dn"], 1)
                    pe.wait_ge(S["th"], 5)
                    proj(pe, bank(3)[:, 0:E], lambda k: th[:, k:k + 1].to_broadcast([P, P]), lambda k: bcw[:, k, :],
                         KT).then_inc(S["bc"], 1)

                @block.scalar
                def _(act):
                    ln_sqrt(act, S, M)
                    ln_copy(act, S)
                    col_ln_act(act, 0)
                    act.wait_ge(S["gs"], NT // 2)
                    nc.scalar.activation(SG, SG, ACT.Sigmoid).then_inc(S["sg"], 1)
                    with act.Fori(0, 4) as i:
                        col_ln_act(act, i + 1)
                        act.wait_ge(S["hb"], i + 1)
                        nc.scalar.activation(hh, hb, ACT.Gelu).then_inc(S["h"], 1)
                    ln_sqrt(act, SO, MO)

                @block.vector
                def _(v):
                    ln_dve(v, S, M, X, XN, 1e-5)
                    v.wait_ge(S["r"], 16 * 6)
                    col_ln_dve(v, newest, 0, in_g, in_b)
                    for g in range(NT // 2):
                        v.wait_ge(S["gp"], g + 1)
                        v.tensor_tensor(SG[:, 2 * g:2 * g + 2, :], bank(6 + g % 2).rearrange("p (t e) -> p t e", t=2),
                                        gb.unsqueeze(1).to_broadcast([P, 2, E]), ALU.add).then_inc(S["gs"], 1)
                    v.wait_ge(S["ap"], 1)
                    v.tensor_tensor(th, bank(4)[:, 0:KT], agg_b, ALU.add).then_inc(S["th"], 1)
                    v.wait_ge(S["th"], 1)
                    with v.Fori(0, 4) as i:
                        v.tensor_tensor(th2, th, d2_b, ALU.add).then_inc(S["b1"], 1)
                        col_ln_dve(v, th, i + 1, pn_g, pn_b)
                        v.wait_ge(S["up"], i + 1)
                        v.tensor_tensor(hb, bank(5)[:, 0:FT], d1_b, ALU.add).then_inc(S["hb"], 1)
                        v.wait_ge(S["dn"], i + 1)
                        v.wait_ge(S["b1"], i + 1)
                        v.tensor_tensor(th, bank(4)[:, 0:KT], th2, ALU.add).then_inc(S["th"], 1)
                        v.wait_ge(S["th"], i + 2)
                    v.wait_ge(S["bc"], 1)
                    v.tensor_tensor(bcrow, bank(3)[:, 0:E], bcb, ALU.add).then_inc(S["bcr"], 1)
                    v.wait_ge(S["bcr"], 1)
                    v.wait_ge(S["sg"], 1)
                    v.tensor_tensor(SG, SG, wide(bcrow), ALU.mult).then_inc(S["mul"], 1)
                    v.wait_ge(S["mul"], 1)
                    v.tensor_tensor(SG, SG, XN, ALU.add).then_inc(S["out"], 1)
                    v.wait_ge(S["out"], 1)
                    ln_dve(v, SO, MO, SG, SG, 1e-6)
                    v.wait_ge(SO["xn"], NT)
                    v.tensor_tensor(SG, SG, wide(out_g), ALU.mult).then_inc(S["og"], 1)
                    v.wait_ge(S["og"], 1)
                    v.tensor_tensor(SG, SG, wide(out_b), ALU.add).then_inc(S["ob"], 1)
                    v.wait_ge(S["ob"], 1)
                    for t in range(NT):
                        v.scalar_tensor_tensor(X[:, t, :], SG[:, t, :], 0.5, X[:, t, :], ALU.mult,
                                               ALU.add).then_inc(S["fin"], 1)

        def attention():
            take = Region()
            V = take(NH * NT * P).rearrange("p (t n) -> p t n", t=NT)
            OT = take(NH * T).rearrange("p (h t) -> p h t", h=NH)
            common = take.at
            S = sems("av", LN + " w vp vc")
            SA = sems("ah", "w0 w1 tab pq t1 t2 rd sc msk mx nb ex rcp tr tev pv oe")
            SW = sems("ao", "w p a")
            M = ln_region(take)
            wv = take(KT * NH * P).rearrange("p (k n) -> p k n", k=KT)
            spare = take(8)
            NB = NH * P // BANK
            with nc.Block() as block:
                @block.sync
                def _(sp):
                    sp.dma_start(wv, A["wv"].rearrange("(k p) n -> p k n", p=P)).then_inc(S["w"], 16)

                @block.gpsimd
                def _(g):
                    credit(g, spare, [(SA[s], n) for s, n in (("pq", 1), ("t2", 2), ("rd", 2), ("ex", 2), ("tr", 1), ("tev", 1), ("pv", 2), ("oe", 2))])

                @block.vector
                def _(v):
                    ln_dve(v, S, M, X, XN, 1e-5)

                @block.scalar
                def _(act):
                    ln_sqrt(act, S, M)
                    ln_copy(act, S)
                    for n in range(NT * NB):
                        act.wait_ge(S["vp"], n + 1)
                        nc.scalar.copy(V[:, n // NB, n % NB * BANK:(n % NB + 1) * BANK], bank(4 + n % 4)).then_inc(S["vc"], 1)

                @block.tensor
                def _(pe):
                    ln_pe(pe, S)
                    pe.wait_ge(S["xnT"], NT // 2)
                    pe.wait_ge(S["w"], 16)
                    for n in range(NT * NB):
                        if n >= 4:
                            pe.wait_ge(S["vc"], n - 3)
                        t = n // NB
                        proj(pe, bank(4 + n % 4), lambda k: XNT[:, k, t * P:(t + 1) * P],
                             lambda k: wv[:, k, n % NB * BANK:(n % NB + 1) * BANK], KT).then_inc(S["vp"], 1)

            take.at = common
            S = SA
            cos_t, sin_t = take(T), take(T)
            wqk = take(4 * E).rearrange("p (b u k d) -> p b u k d", b=2, u=2, k=KT)
            qk = take(4 * T).rearrange("p (b u t) -> p b u t", b=2, u=2)
            turn = take(2 * HALF).rearrange("p (b t) -> p b t", b=2)
            pr = take(2 * T).rearrange("p (b t) -> p b t", b=2)
            PT = take(2 * T).rearrange("p (b t) -> p b t", b=2)
            oS = take(T)
            nmx, nb, rsum, rinv = take(2), take(2), take(2), take(2)
            NU = 4
            TG = 14
            groups, outs, m = {}, {}, 0
            for i in range(NT):
                groups[i] = [(m, 0, min(4, i + 1))]
                m += 1
                if i == 5:
                    outs[i] = (m, 0)
                    m += 1
                if i >= 4:
                    groups[i].append((m, 4, i + 1))
                    m += 1
            outs[NT] = (m, 4)
            m += 1
            assert m == TG
            HALFP = P // 2

            with nc.Block() as block:
                @block.sync
                def _(sp):
                    sp.dma_start(wqk[:, 0, :, :, :], A["w_qk"][0]).then_inc(S["w0"], 16)
                    sp.dma_start(cos_t, A["cos"]).then_inc(S["tab"], 16)
                    sp.dma_start(sin_t, A["sin"]).then_inc(S["tab"], 16)
                    with sp.Fori(0, NH // 2) as it:
                        for j in range(2):
                            h = it * 2 + j
                            sp.wait_ge(S["pq"], h * NU + 1)
                            sp.dma_start(wqk[:, 1 - j, :, :, :], A["w_qk"][bass.ds(h + 1, 1)]
                                         .rearrange("o p u k d -> p (o u) k d")).then_inc(S["w" + str(1 - j)], 16)

                def project(pe, f, b, u):
                    r = f * NU + u
                    pe.wait_ge(S["t2"], r + 1)
                    proj(pe, bank(u % 2), lambda k: wqk[:, b, u // 2, k, :],
                         lambda k: XNT[:, k, u % 2 * HALF:(u % 2 + 1) * HALF], KT).then_inc(S["pq"], 1)

                @block.tensor
                def _(pe):
                    pe.wait_ge(S["w0"], 16)
                    for u in range(NU):
                        project(pe, 0, 0, u)
                    with pe.Fori(0, NH // 2) as it:
                        for j in range(2):
                            h = it * 2 + j

                            def scores(i):
                                n = h * NT + i
                                pe.wait_ge(S["ex"], n + 1)
                                base = 2 + i % 2 * 2
                                for lo in range(0, (i + 1) * P, BANK):
                                    hi = min(lo + BANK, (i + 1) * P)
                                    last = pe.matmul(bank(base, 2)[:, lo:hi], qk[:, j, 0, i * P:(i + 1) * P],
                                                     qk[:, j, 1, lo:hi], start=True, stop=True)
                                last.then_inc(S["sc"], 1)

                            def transposed(i, q):
                                n = h * NT + i
                                m, lo, hi = groups[i][q]
                                pe.wait_ge(S["ex"], n + 3)
                                pe.wait_ge(S["tev"], h * TG + (m + 1))
                                for c in range(lo, hi):
                                    last = pe.transpose(bank(6)[:, (c - lo) * P:(c - lo + 1) * P],
                                                        pr[:, i % 2, c * P:(c + 1) * P], ident[:, :])
                                last.then_inc(S["tr"], 1)

                            def outputs(i, q):
                                n = h * NT + i
                                m, lo, hi = groups[i][q]
                                if q == 0:
                                    pe.wait_ge(S["oe"], n + 2)
                                pe.wait_ge(S["tev"], h * TG + (m + 2))
                                for c in range(lo, hi):
                                    last = pe.matmul(bank(7)[:, 0:P], PT[:, i % 2, c * P:(c + 1) * P],
                                                     V[:, c, bass.ds(h * P, P)], start=(c == 0), stop=(c == i))
                                if hi == i + 1:
                                    last.then_inc(S["pv"], 1)

                            def turned_outputs(m, lo):
                                pe.wait_ge(S["oe"], h * NT + (lo + 6))
                                pe.wait_ge(S["tev"], h * TG + (m + 1))
                                for c in range(lo, lo + 4):
                                    last = pe.transpose(bank(6)[:, (c - lo) * P:(c - lo + 1) * P],
                                                        oS[:, c * P:(c + 1) * P], ident[:, :])
                                last.then_inc(S["tr"], 1)

                            pe.wait_ge(S["rd"], (h + 1) * NU + 2)
                            scores(0)
                            pe.wait_ge(S["w" + str(1 - j)], (it + 1 if j == 0 else it + 2) * 16)
                            for i in range(NT):
                                if i + 1 < NT:
                                    scores(i + 1)
                                if i < NU:
                                    project(pe, h + 1, 1 - j, i)
                                if i:
                                    outputs(i - 1, 0)
                                transposed(i, 0)
                                if i and len(groups[i - 1]) > 1:
                                    outputs(i - 1, 1)
                                if i in outs:
                                    turned_outputs(*outs[i])
                                if len(groups[i]) > 1:
                                    transposed(i, 1)
                            for q in range(2):
                                outputs(NT - 1, q)
                            turned_outputs(*outs[NT])

                @block.scalar
                def _(act):
                    with act.Fori(0, NH // 2) as it:
                        for j in range(2):
                            h = it * 2 + j

                            def out_tile(i):
                                act.wait_ge(S["pv"], h * NT + (i + 3))
                                act.wait_ge(S["rcp"], h * NT + (i + 1))
                                nc.scalar.activation(oS[:, i * P:(i + 1) * P], bank(7)[:, 0:P], ACT.Copy,
                                                     scale=rinv[:, i % 2:i % 2 + 1]).then_inc(S["oe"], 1)

                            def out_rows(m, lo):
                                act.wait_ge(S["tr"], h * TG + (m + 2))
                                nc.scalar.copy(OT[:, bass.ds(h, 1), lo * P:(lo + 4) * P]
                                               .rearrange("p o t -> p (o t)"), bank(6)).then_inc(S["tev"], 1)

                            def turned(i, q):
                                m, lo, hi = groups[i][q]
                                act.wait_ge(S["tr"], h * TG + (m + 2))
                                nc.scalar.copy(PT[:, i % 2, lo * P:hi * P], bank(6)[:, 0:(hi - lo) * P])\
                                  .then_inc(S["tev"], 1)

                            for i in range(NT):
                                n, b = h * NT + i, i % 2
                                act.wait_ge(S["nb"], n + 1)
                                nc.scalar.activation(pr[:, b, 0:(i + 1) * P], bank(2 + 2 * b, 2)[:, 0:(i + 1) * P],
                                                     ACT.Exp, bias=nb[:, b:b + 1], scale=ATTN_SCALE,
                                                     accum_out=rsum[:, b:b + 1]).then_inc(S["ex"], 1)
                                turned(i, 0)
                                if i:
                                    out_tile(i - 1)
                                if i in outs:
                                    out_rows(*outs[i])
                                if len(groups[i]) > 1:
                                    turned(i, 1)
                            out_tile(NT - 1)
                            out_rows(*outs[NT])

                @block.gpsimd
                def _(g):
                    def add(f, b, u):
                        r = f * NU + u
                        g.wait_ge(S["t2"], r + 3)
                        dst = qk[:, b, u // 2, u % 2 * HALF:(u % 2 + 1) * HALF]
                        g.tensor_tensor(dst, dst, turn[:, u % 2, :], ALU.add).then_inc(S["rd"], 1)

                    for u in range(NU):
                        add(0, 0, u)
                    with g.Fori(0, NH // 2) as it:
                        for j in range(2):
                            for u in range(NU):
                                add(it * 2 + j + 1, 1 - j, u)

                @block.vector
                def _(v):
                    def rotate(f, b, u):
                        r = f * NU + u
                        cols_ = slice(u % 2 * HALF, (u % 2 + 1) * HALF)
                        v.wait_ge(S["pq"], r + 2)
                        v.tensor_tensor(qk[:, b, u // 2, cols_], bank(u % 2), cos_t[:, cols_], ALU.mult).then_inc(S["t1"], 1)
                        v.wait_ge(S["rd"], r + 1)
                        v.tensor_tensor(turn[0:HALFP, u % 2, :], bank(u % 2)[HALFP:P, :], sin_t[HALFP:P, cols_],
                                        ALU.mult).then_inc(S["t1"], 1)
                        v.tensor_tensor(turn[HALFP:P, u % 2, :], bank(u % 2)[0:HALFP, :], sin_t[0:HALFP, cols_],
                                        ALU.mult).then_inc(S["t2"], 1)

                    v.wait_ge(S["tab"], 32)
                    for u in range(NU):
                        rotate(0, 0, u)
                    with v.Fori(0, NH // 2) as it:
                        for j in range(2):
                            h = it * 2 + j
                            for i in range(NT):
                                n = h * NT + i
                                b = i % 2
                                s = bank(2 + 2 * b, 2)
                                v.wait_ge(S["sc"], n + 1)
                                v.tensor_tensor(s[:, i * P:(i + 1) * P], s[:, i * P:(i + 1) * P], causal[:, :],
                                                ALU.add).then_inc(S["msk"], 1)
                                v.wait_ge(S["msk"], n + 1)
                                v.tensor_reduce(nmx[:, b:b + 1], s[:, 0:(i + 1) * P], AX.X, ALU.max,
                                                negate=True).then_inc(S["mx"], 1)
                                v.wait_ge(S["mx"], n + 1)
                                v.tensor_scalar(nb[:, b:b + 1], nmx[:, b:b + 1], ATTN_SCALE, None,
                                                ALU.mult).then_inc(S["nb"], 1)
                                if i < NU:
                                    rotate(h + 1, 1 - j, i)
                                for q in ([i - 1] if i else []) + ([i] if i == NT - 1 else []):
                                    v.wait_ge(S["ex"], h * NT + (q + 3))
                                    v.wait_ge(S["oe"], h * NT + (q + 1))
                                    v.reciprocal(rinv[:, q % 2:q % 2 + 1], rsum[:, q % 2:q % 2 + 1])\
                                     .then_inc(S["rcp"], 1)

            take.at = common
            wo = take(NH * E).rearrange("p (h e) -> p h e", h=NH)
            S = SW
            with nc.Block() as block:
                @block.sync
                def _(sp):
                    sp.dma_start(wo, A["wo"].rearrange("(h p) e -> p h e", p=P)).then_inc(S["w"], 16)

                @block.tensor
                def _(pe):
                    pe.wait_ge(S["w"], 16)
                    for t in range(NT):
                        if t >= 2:
                            pe.wait_ge(S["a"], t - 1)
                        proj(pe, bank(t % 2)[:, 0:E], lambda h: OT[:, h, t * P:(t + 1) * P], lambda h: wo[:, h, :],
                             NH).then_inc(S["p"], 1)

                @block.vector
                def _(v):
                    for t in range(NT):
                        v.wait_ge(S["p"], t + 1)
                        v.tensor_tensor(X[:, t, :], X[:, t, :], bank(t % 2)[:, 0:E], ALU.add).then_inc(S["a"], 1)

        topk_ffn("fa", True)
        end_phase()
        mamba()
        end_phase()
        topk_ffn("fb", False)
        end_phase()
        ponder_ffn("pa", False)
        end_phase()
        attention()
        end_phase()
        ponder_ffn("pb", True)


def kernel(**inputs):
    import numpy as np
    import concourse.bacc as bacc
    from concourse.bass_utils import run_bass_kernel_spmd

    def f(name):
        return np.ascontiguousarray(inputs[name])

    def columns(name):
        return f(name).reshape(-1, P).T

    w_in = f("L0_attn_in_proj_w")
    tiles = w_in[:-HM].reshape(-1, P, KT, P).transpose(0, 3, 2, 1)
    wq, wk = (f(n).reshape(KT, P, NH, P).transpose(2, 1, 0, 3) for n in ("L1_attn_wq", "L1_attn_wk"))
    w_qk = np.stack([wq, wk], axis=2)
    conv = np.concatenate([f("L0_attn_conv_w")[:, 0, :], f("L0_attn_conv_b")[:, None]], axis=1)
    half = P // 2
    freqs = np.power(np.float32(10000.0), -np.arange(half, dtype=np.float32) / np.float32(half))
    rad = (np.arange(T, dtype=np.float32)[:, None] * freqs[None, :]).astype(np.float32).T
    cos, sin = np.cos(rad).astype(np.float32), np.sin(rad).astype(np.float32)
    arrays = {
        "x": f("L0_attn_x").reshape(T, E),
        "Wr": f("L0_ffn_Wr").reshape(E), "br": f("L0_ffn_br"), "W1": f("L0_ffn_W1"), "b1": columns("L0_ffn_b1"),
        "W2": f("L0_ffn_W2"), "b2": f("L0_ffn_b2"),
        "w_in": np.concatenate([tiles, tiles[:1]]), "w_dt": w_in[-HM:].T,
        "conv": np.concatenate([conv, conv[:P]]),
        "dt_bias": f("L0_attn_dt_bias"), "A_log": f("L0_attn_A_log"), "D": f("L0_attn_D"),
        "norm_w": columns("L0_attn_norm_w"), "w_out": f("L0_attn_out_proj_w").T,
        "w_qk": np.concatenate([w_qk, w_qk[:1]]),
        "wv": f("L1_attn_wv").reshape(E, NH * P), "wo": f("L1_attn_wo").reshape(NH * P, E),
        "cos": np.concatenate([cos, cos]), "sin": np.concatenate([sin, -sin]),
        "cols": np.stack([columns(n) for n in ("L1_ffn_in_gamma", "L1_ffn_in_beta", "L1_ffn_agg_b", "L1_ffn_pn_gamma",
                                               "L1_ffn_pn_beta", "L1_ffn_d2_b")], axis=1),
        "d1_b": columns("L1_ffn_d1_b"), "gate_b": f("L1_ffn_gate_b"), "bc_b": f("L1_ffn_bc_b"),
        "out_g": f("L1_ffn_out_gamma"), "out_b": f("L1_ffn_out_beta"),
        "agg_w": f("L1_ffn_agg_w"), "gate_w": f("L1_ffn_gate_w"), "d1_w": f("L1_ffn_d1_w"), "d2_w": f("L1_ffn_d2_w"),
        "bc_w": f("L1_ffn_bc_w"),
    }
    arrays = {n: np.ascontiguousarray(a) for n, a in arrays.items()}
    nc = bacc.Bacc("TRN2", target_bir_lowering=False, num_devices=1)
    A = {n: nc.dram_tensor("in_" + n, a.shape, mybir.dt.from_np(a.dtype), kind="ExternalInput").ap()
         for n, a in arrays.items()}
    A["cum_rows"] = nc.dram_tensor("cum_rows", ((HM + 1) * NT, P), F32, kind="Internal").ap()
    out = nc.dram_tensor("out_x", (T, E), F32, kind="ExternalOutput").ap()
    build(nc, A, out)
    r = run_bass_kernel_spmd(nc, [{"in_" + n: a for n, a in arrays.items()}], core_ids=[0])
    return r.results[0]["out_x"].reshape(1, T, E)
```

```python
from contextlib import ExitStack

import concourse.bass as bass
from concourse import mybir

F32 = mybir.dt.float32
ALU = mybir.AluOpType
ACT = mybir.ActivationFunctionType
AX = mybir.AxisListType

P = 128
T = 1024
E = 256
NT = T // P
KT = E // P
TOPK = P
DFF = 1024
FT = DFF // P
HM, GM = 32, 8
CONV = 4
XTILE, BTILE, CTILE = HM, 2 * HM, 2 * HM + GM
CW = CONV + 1
NH = 16
HALF = T // 2
BANK = 512
NEG = -1e30


def build(nc, A, out):
    with ExitStack() as ctx:
        open_sems = []

        def sems(phase, names):
            S = {n: nc.alloc_semaphore(phase + "_" + n) for n in names.split()}
            open_sems.extend(S.values())
            return S

        def end_phase():
            nc.clear_and_free_semaphores(list(open_sems))
            open_sems.clear()
            nc.all_engine_barrier()

        def sb(name, cols):
            return ctx.enter_context(nc.sbuf_tensor(name, [P, cols], F32))

        x_sb = sb("x_sb", NT * E)
        xn_sb = sb("xn_sb", NT * E)
        xnT_sb = sb("xnT_sb", KT * T)
        X = x_sb[:, :].rearrange("p (t e) -> p t e", t=NT)
        XN = xn_sb[:, :].rearrange("p (t e) -> p t e", t=NT)
        XNT = xnT_sb[:, :].rearrange("p (k t) -> p k t", k=KT)
        ident = sb("ident", P)
        ones = sb("ones", P)
        upto = sb("upto", P)
        after = sb("after", P)
        slots = sb("slots", P)
        causal = sb("causal", P)
        ARENA = 46200
        arena = sb("arena", ARENA)
        psum = ctx.enter_context(nc.psum_tensor("psum", [P, 8 * BANK], F32))

        class Region:

            def __init__(self):
                self.at = 0

            def __call__(self, cols):
                self.at += cols
                assert self.at <= ARENA, self.at
                return arena[:, self.at - cols:self.at]

        def bank(b, n=1):
            return psum[:, b * BANK:(b + n) * BANK]

        def row(ap):
            return ap.rearrange("(a d) -> a d", a=1).to_broadcast([P, ap.shape[0]])

        def proj(pe, dst, lhs, rhs, n):
            for k in range(n):
                last = pe.matmul(dst, lhs(k), rhs(k), start=(k == 0), stop=(k == n - 1))
            return last

        def credit(g, spare, pairs):
            for i, (s, n) in enumerate(pairs):
                g.memset(spare[:, i:i + 1], 0.0).then_inc(s, n)

        LN = "stats aggr ve sd rstd xn tr xnT"

        def ln_region(take):
            return {"st": take(NT * 6).rearrange("p (t s) -> p t s", t=NT),
                    "mv": take(NT * 2).rearrange("p (t s) -> p t s", t=NT),
                    "ve": take(NT), "sd": take(NT), "rstd": take(NT)}

        def ln_dve(v, S, M, src, dst, eps, tiles=NT):
            for t in range(tiles):
                v.bn_stats(M["st"][:, t, :], src[:, t, :]).then_inc(S["stats"], 1)
            v.wait_ge(S["stats"], tiles)
            for t in range(tiles):
                v.bn_aggr(M["mv"][:, t, :], M["st"][:, t, :]).then_inc(S["aggr"], 1)
            v.wait_ge(S["aggr"], tiles)
            v.tensor_scalar(M["ve"], M["mv"][:, :, 1], eps, None, ALU.add).then_inc(S["ve"], 1)
            v.wait_ge(S["sd"], 1)
            v.reciprocal(M["rstd"], M["sd"]).then_inc(S["rstd"], 1)
            v.wait_ge(S["rstd"], 1)
            for t in range(tiles):
                v.tensor_scalar(dst[:, t, :], src[:, t, :], M["mv"][:, t, 0:1], M["rstd"][:, t:t + 1],
                                ALU.subtract, ALU.mult).then_inc(S["xn"], 1)

        def ln_sqrt(act, S, M):
            act.wait_ge(S["ve"], 1)
            nc.scalar.activation(M["sd"], M["ve"], ACT.Sqrt).then_inc(S["sd"], 1)

        def ln_pe(pe, S):
            for g in range(NT // 2):
                pe.wait_ge(S["xn"], 2 * g + 2)
                if g >= 2:
                    pe.wait_ge(S["xnT"], g - 1)
                for k in range(KT):
                    for h in range(2):
                        last = pe.transpose(bank(g % 2)[:, (2 * k + h) * P:(2 * k + h + 1) * P],
                                            XN[:, 2 * g + h, k * P:(k + 1) * P], ident[:, :])
                last.then_inc(S["tr"], 1)

        def ln_copy(act, S):
            for g in range(NT // 2):
                act.wait_ge(S["tr"], g + 1)
                nc.scalar.copy(XNT[:, :, 2 * g * P:(2 * g + 2) * P],
                               bank(g % 2).rearrange("p (k t) -> p k t", k=KT)).then_inc(S["xnT"], 1)

        def topk_ffn(name, first):
            take = Region()
            S = sems(name, LN + " w r x const wr lcol lb ltr lmax rank rk sel selT seltr selTev wexp wz zs z rz cw"
                     " g gc up hT dn ol sc res half")
            M = ln_region(take)
            w1 = take(KT * DFF).rearrange("p (k f) -> p k f", k=KT)
            w2 = take(FT * E).rearrange("p (k e) -> p k e", k=FT)
            b1 = take(FT)
            b2, wr, br = take(E), take(E), take(1)
            lcol, lbc = take(NT), take(T).rearrange("p (t q) -> p t q", t=NT)
            junk = take(T)
            parts = take(3 * NT).rearrange("p (a t) -> p a t", a=3)
            rank, rank2, mask = take(NT), take(NT), take(NT)
            sel = take(NT * TOPK).rearrange("p (t s) -> p t s", t=NT)
            selT = take(NT * TOPK).rearrange("p (t s) -> p t s", t=NT)
            nmax, wexp, wz, zz, rz, cw = take(1), take(NT), take(NT), take(1), take(1), take(NT)
            fxT = take(KT * TOPK).rearrange("p (k s) -> p k s", k=KT)
            hT = take(FT * TOPK).rearrange("p (k s) -> p k s", k=FT)
            outl = take(E)
            prod2 = take(E * NT)
            prod = prod2.rearrange("p (t e) -> p t e", t=NT)

            with nc.Block() as block:
                @block.sync
                def _(sp):
                    if first:
                        for t in range(NT):
                            sp.dma_start(X[:, t, :], A["x"][t * P:(t + 1) * P, :]).then_inc(S["x"], 16)
                    sp.dma_start(wr, row(A["Wr"])).then_inc(S["r"], 16)
                    sp.dma_start(br, row(A["br"])).then_inc(S["r"], 16)
                    sp.dma_start(b2, row(A["b2"])).then_inc(S["r"], 16)
                    sp.dma_start(b1, A["b1"]).then_inc(S["r"], 16)
                    sp.dma_start(w1, A["W1"].rearrange("(k p) f -> p k f", p=P)).then_inc(S["w"], 16)
                    sp.dma_start(w2, A["W2"].rearrange("(k p) e -> p k e", p=P)).then_inc(S["w"], 16)

                if first:
                    @block.gpsimd
                    def _(g):
                        g.memset(ones[:, :], 1.0).then_inc(S["const"], 1)
                        g.memset(causal[:, :], 0.0).then_inc(S["const"], 1)
                        g.iota(slots[:, :], pattern=[[1, P]], base=0, channel_multiplier=0,
                               allow_small_or_imprecise_dtypes=True).then_inc(S["const"], 1)
                        g.wait_ge(S["const"], 3)
                        g.affine_select(out=ident[:, :], in_=ones[:, :], compare_op=ALU.is_equal, fill=0.0, base=0,
                                        pattern=[[-1, P]], channel_multiplier=1).then_inc(S["const"], 1)
                        g.affine_select(out=upto[:, :], in_=ones[:, :], compare_op=ALU.is_ge, fill=0.0, base=0,
                                        pattern=[[1, P]], channel_multiplier=-1).then_inc(S["const"], 1)
                        g.affine_select(out=after[:, :], in_=ones[:, :], compare_op=ALU.is_gt, fill=0.0, base=0,
                                        pattern=[[-1, P]], channel_multiplier=1).then_inc(S["const"], 1)
                        g.affine_select(out=causal[:, :], in_=causal[:, :], compare_op=ALU.is_ge, fill=NEG, base=0,
                                        pattern=[[-1, P]], channel_multiplier=1).then_inc(S["const"], 1)

                @block.vector
                def _(v):
                    if first:
                        v.wait_ge(S["x"], 16 * NT)
                    ln_dve(v, S, M, X, XN, 1e-5)
                    v.wait_ge(S["r"], 64)
                    v.wait_ge(S["xn"], NT)
                    for t in range(NT):
                        v.scalar_tensor_tensor(prod[:, t, :], XN[:, t, :], 1.0, wr, ALU.mult, ALU.mult,
                                               accum_out=lcol[:, t:t + 1]).then_inc(S["wr"], 1)
                    v.wait_ge(S["wr"], NT)
                    v.tensor_scalar(lcol, lcol, br[:, 0:1], None, ALU.add).then_inc(S["lcol"], 1)
                    v.wait_ge(S["lcol"], 1)
                    v.tensor_copy(lbc, lcol.unsqueeze(2).to_broadcast([P, NT, P])).then_inc(S["lb"], 1)
                    v.wait_ge(S["ltr"], 1)
                    lrow = bank(2, 2)
                    v.tensor_reduce(nmax, lrow, AX.X, ALU.max, negate=True).then_inc(S["lmax"], 1)
                    v.memset(parts[:, 0, 0:1], 0.0).then_inc(S["rank"], 1)
                    for t in range(NT):
                        v.wait_ge(S["rank"], 3 * t if t else 1)
                        if t:
                            v.tensor_scalar(junk[:, 0:t * P], lrow[:, 0:t * P], lcol[:, t:t + 1], 0.0, ALU.is_ge,
                                            ALU.add, accum_out=parts[:, 0, t:t + 1]).then_inc(S["rank"], 1)
                        v.tensor_scalar(prod2[:, 0:T - t * P], lrow[:, t * P:T], lcol[:, t:t + 1], 0.0, ALU.is_gt,
                                        ALU.add, accum_out=parts[:, 1, t:t + 1]).then_inc(S["rank"], 1)
                        v.scalar_tensor_tensor(prod2[:, T:T + P], lrow[:, t * P:(t + 1) * P], lcol[:, t:t + 1],
                                               after[:, :], ALU.is_equal, ALU.mult,
                                               accum_out=parts[:, 2, t:t + 1]).then_inc(S["rank"], 1)
                    v.wait_ge(S["rank"], 3 * NT)
                    v.tensor_tensor(rank2, parts[:, 0, :], parts[:, 1, :], ALU.add).then_inc(S["rk"], 1)
                    v.wait_ge(S["rk"], 1)
                    v.tensor_tensor(rank, rank2, parts[:, 2, :], ALU.add).then_inc(S["rk"], 1)
                    v.wait_ge(S["rk"], 2)
                    for t in range(NT):
                        v.tensor_scalar(sel[:, t, :], slots[:, :], rank[:, t:t + 1], None,
                                        ALU.is_equal).then_inc(S["sel"], 1)
                    v.tensor_scalar(mask, rank, float(TOPK), None, ALU.is_lt).then_inc(S["rk"], 1)
                    v.wait_ge(S["wexp"], 1)
                    v.wait_ge(S["rk"], 3)
                    v.tensor_tensor(wz, wexp, mask, ALU.mult).then_inc(S["wz"], 1)
                    v.wait_ge(S["g"], 1)
                    v.tensor_copy(fxT, bank(5)[:, 0:KT * TOPK].rearrange("p (k s) -> p k s", k=KT)).then_inc(S["gc"], 1)
                    for g in range(2):
                        v.wait_ge(S["seltr"], g + 1)
                        v.tensor_copy(selT[:, 4 * g:4 * g + 4, :],
                                      bank(6 + g).rearrange("p (t s) -> p t s", t=4)).then_inc(S["selTev"], 1)
                    for t in range(NT):
                        v.scalar_tensor_tensor(X[:, t, :], XN[:, t, :], 0.5, X[:, t, :], ALU.mult,
                                               ALU.add).then_inc(S["half"], 1)
                    v.wait_ge(S["zs"], 1)
                    v.tensor_reduce(zz, bank(4)[:, 0:NT], AX.X, ALU.add).then_inc(S["z"], 1)
                    v.wait_ge(S["z"], 1)
                    v.reciprocal(rz, zz).then_inc(S["rz"], 1)
                    v.wait_ge(S["rz"], 1)
                    v.tensor_scalar(cw, wexp, rz[:, 0:1], 0.5, ALU.mult, ALU.mult).then_inc(S["cw"], 1)
                    v.wait_ge(S["dn"], 1)
                    v.tensor_tensor(outl, bank(2)[:, 0:E], b2, ALU.add).then_inc(S["ol"], 1)
                    v.wait_ge(S["half"], NT)
                    v.wait_ge(S["cw"], 1)
                    for t in range(NT):
                        v.wait_ge(S["sc"], t + 1)
                        v.scalar_tensor_tensor(X[:, t, :], bank(4 + t % 4)[:, 0:E], cw[:, t:t + 1], X[:, t, :],
                                               ALU.mult, ALU.add).then_inc(S["res"], 1)

                @block.scalar
                def _(act):
                    ln_sqrt(act, S, M)
                    act.wait_ge(S["lmax"], 1)
                    nc.scalar.activation(wexp, lcol, ACT.Exp, bias=nmax[:, 0:1]).then_inc(S["wexp"], 1)
                    for f in range(FT):
                        act.wait_ge(S["up"], f + 1)
                        nc.scalar.activation(hT[:, f, :], bank(2 + f % 2)[:, 0:TOPK], ACT.Gelu,
                                             bias=b1[:, f:f + 1]).then_inc(S["hT"], 1)

                @block.tensor
                def _(pe):
                    if first:
                        pe.wait_ge(S["const"], 7)
                    pe.wait_ge(S["lb"], 1)
                    for t in range(NT):
                        last = pe.transpose(bank(2, 2)[:, t * P:(t + 1) * P], lbc[:, t, :], ident[:, :])
                    last.then_inc(S["ltr"], 1)
                    pe.wait_ge(S["sel"], NT)
                    for k in range(KT):
                        last = proj(pe, bank(5)[:, k * TOPK:(k + 1) * TOPK],
                                    lambda t: XN[:, t, k * P:(k + 1) * P], lambda t: sel[:, t, :], NT)
                    last.then_inc(S["g"], 1)
                    for t in range(NT):
                        last = pe.transpose(bank(6 + t // 4)[:, t % 4 * P:(t % 4 + 1) * P], sel[:, t, :], ident[:, :])
                        if t % 4 == 3:
                            last.then_inc(S["seltr"], 1)
                    pe.wait_ge(S["gc"], 1)
                    pe.wait_ge(S["w"], 32)
                    pe.wait_ge(S["rank"], 3 * NT)
                    for f in range(FT):
                        if f >= 2:
                            pe.wait_ge(S["hT"], f - 1)
                        proj(pe, bank(2 + f % 2)[:, 0:TOPK], lambda k: w1[:, k, f * P:(f + 1) * P],
                             lambda k: fxT[:, k, :], KT).then_inc(S["up"], 1)
                    pe.wait_ge(S["wz"], 1)
                    pe.matmul(bank(4)[:, 0:NT], ones[:, :], wz, start=True, stop=True).then_inc(S["zs"], 1)
                    pe.wait_ge(S["hT"], FT)
                    proj(pe, bank(2)[:, 0:E], lambda k: hT[:, k, :], lambda k: w2[:, k, :], FT).then_inc(S["dn"], 1)
                    pe.wait_ge(S["selTev"], 2)
                    pe.wait_ge(S["ol"], 1)
                    pe.wait_ge(S["z"], 1)
                    for t in range(NT):
                        if t >= 4:
                            pe.wait_ge(S["res"], t - 3)
                        pe.matmul(bank(4 + t % 4)[:, 0:E], selT[:, t, :], outl, start=True, stop=True).then_inc(S["sc"], 1)

        def mamba():
            take = Region()
            BTOK = take(GM * T).rearrange("p (g c n) -> p g c n", g=GM, c=NT)
            CB = take(GM * T).rearrange("p (g t) -> p g t", g=GM)
            cwt = take((HM + 2 * GM + 1) * CW).rearrange("p (n w) -> p n w", w=CW)
            dt, dend, etot = (take(HM * NT) for _ in range(3))
            cum = take(HM * NT)
            nw = take(HM)
            dskip = take(HM)
            spare = take(32)
            wx = take(2 * E).rearrange("p (b k c) -> p b k c", b=2, k=KT)
            raw = take(T + CONV - 1)
            xT = take(2 * T).rearrange("p (b t) -> p b t", b=2)
            CT = arena[:, take.at:take.at + (GM + 1) * T].rearrange("p (g t) -> p g t", g=GM + 1)
            take(GM * T)
            common = take.at
            take(T)
            bT = take(2 * T).rearrange("p (b t) -> p b t", b=2)
            raw2 = take(T + CONV - 1)

            def col(ap, i):
                return ap[:, bass.ds(i, 1)]

            def tap_of(tile, w):
                return cwt[:, bass.ds(tile, 1), w:w + 1].rearrange("p o w -> p (o w)")

            def one_tap(v, S, b, n, tile, raw, w, ahead=2):
                if w:
                    v.wait_ge(S["tap"], n * (CONV - 2) + w)
                else:
                    v.wait_ge(S["c"], n + ahead)
                v.scalar_tensor_tensor(xT[:, b, :], raw[:, w:w + T], tap_of(tile, w), xT[:, b, :], ALU.mult,
                                       ALU.add).then_inc(S["tap"] if w < CONV - 2 else S["conv"], 1)

            def conv_taps(v, S, b, n, tile, raw, ahead=2):
                for w in range(CONV - 1):
                    one_tap(v, S, b, n, tile, raw, w, ahead)

            def conv_newest(act, S, b, tile, raw, at=0):
                nc.scalar.copy(raw[:, CONV - 1:], bank(at, 2)).then_inc(S["raw"], 1)
                nc.scalar.activation(xT[:, b, :], bank(at, 2), ACT.Identity, bias=tap_of(tile, CONV),
                                     scale=tap_of(tile, CONV - 1)).then_inc(S["c"], 1)

            def channels(pe, w, at=0):
                for h in range(2):
                    last = proj(pe, bank(at + h), lambda k: w[:, k, :], lambda k: XNT[:, k, h * HALF:(h + 1) * HALF], KT)
                return last

            S2 = sems("mb", "w0 w1 pj raw c tap conv xt bt btok cbp cb")
            S3 = sems("mm", "wx0 wx1 wg0 wg1 cr0 cr1 wo px pg raw c tap conv xt tx xd xs ds rc st ec cs df rl lm mm"
                      " y yd sg u sqs ad vr vv sd rr wos op oc")

            take.at = common
            M = ln_region(take)
            wdt = take(KT * HM).rearrange("p (k h) -> p k h", k=KT)
            dtb, alog, aneg = take(HM), take(HM), take(HM)
            z, za, ze, zl, a = (take(HM * NT) for _ in range(5))
            cumT = take(2 * P).rearrange("p (b l) -> p b l", b=2)
            S = sems("mp", LN + " r dtp z za ze zl dt alog a cs sfx tot cum dend etot ctr cT scr pad")
            with nc.Block() as block:
                @block.sync
                def _(sp):
                    sp.dma_start(wdt, A["w_dt"].rearrange("(k p) h -> p k h", p=P)).then_inc(S["r"], 16)
                    sp.dma_start(dtb, row(A["dt_bias"])).then_inc(S["r"], 16)
                    sp.dma_start(alog, row(A["A_log"])).then_inc(S["r"], 16)
                    sp.dma_start(cwt, A["conv"].rearrange("(n p) w -> p n w", p=P)).then_inc(S["r"], 16)
                    sp.dma_start(nw, A["norm_w"]).then_inc(S["r"], 16)
                    sp.dma_start(dskip, row(A["D"])).then_inc(S["r"], 16)
                    sp.wait_ge(S["cT"], 1)
                    for b in range(2):
                        sp.dma_start(A["cum_rows"][b * P:(b + 1) * P, :], cumT[:, b, :]).then_inc(S["scr"], 16)
                    sp.wait_ge(S["r"], 96)
                    sp.wait_ge(S["scr"], 32)

                @block.gpsimd
                def _(g):
                    g.memset(raw[:, 0:CONV - 1], 0.0).then_inc(S["pad"], 1)
                    g.memset(raw2[:, 0:CONV - 1], 0.0).then_inc(S["pad"], 1)
                    credit(g, spare, [(S2["pj"], 2), (S2["c"], 2), (S2["cbp"], 2), (S2["btok"], 1), (S2["cb"], 1)]
                           + [(S3[n], 1) for n in "c st y yd ds sg u ad vr op ec".split()]
                           + [(S3[n], 2) for n in "px pg".split()])

                @block.vector
                def _(v):
                    ln_dve(v, S, M, X, XN, 1e-5)
                    v.wait_ge(S["r"], 96)
                    v.wait_ge(S["dtp"], 1)
                    pd = bank(2)[:, 0:HM * NT].rearrange("p (c h) -> p c h", c=NT)
                    for t in range(NT):
                        v.tensor_tensor(z.rearrange("p (h c) -> p c h", c=NT)[:, t, :], pd[:, t, :], dtb,
                                        ALU.add).then_inc(S["z"], 1)
                    v.wait_ge(S["zl"], 1)
                    v.scalar_tensor_tensor(dt, z, 0.0, zl, ALU.max, ALU.add).then_inc(S["dt"], 1)
                    v.wait_ge(S["dt"], 1)
                    v.wait_ge(S["alog"], 1)
                    v.scalar_tensor_tensor(a.rearrange("p (h c) -> p h c", c=NT), dt.rearrange("p (h c) -> p h c", c=NT),
                                           -1.0, aneg.unsqueeze(2).to_broadcast([P, HM, NT]), ALU.mult,
                                           ALU.mult).then_inc(S["a"], 1)
                    v.wait_ge(S["cs"], 1)
                    v.tensor_copy(cum[:, 0:HM * NT], bank(3)[:, 0:HM * NT]).then_inc(S["cum"], 1)
                    v.wait_ge(S["ctr"], 1)
                    v.tensor_copy(cumT, bank(6)[:, 0:2 * P].rearrange("p (b l) -> p b l", b=2)).then_inc(S["cT"], 1)

                @block.scalar
                def _(act):
                    ln_sqrt(act, S, M)
                    ln_copy(act, S)
                    act.wait_ge(S["r"], 96)
                    nc.scalar.activation(aneg, alog, ACT.Exp).then_inc(S["alog"], 1)
                    act.wait_ge(S["z"], NT)
                    nc.scalar.activation(za, z, ACT.Abs).then_inc(S["za"], 1)
                    act.wait_ge(S["za"], 1)
                    nc.scalar.activation(ze, za, ACT.Exp, scale=-1.0).then_inc(S["ze"], 1)
                    act.wait_ge(S["ze"], 1)
                    nc.scalar.activation(zl, ze, ACT.Ln, bias=1.0).then_inc(S["zl"], 1)
                    act.wait_ge(S["sfx"], 1)
                    nc.scalar.activation(dend, bank(4)[:, 0:HM * NT], ACT.Exp).then_inc(S["dend"], 1)
                    act.wait_ge(S["tot"], 1)
                    nc.scalar.activation(etot, bank(5)[:, 0:HM * NT], ACT.Exp).then_inc(S["etot"], 1)

                @block.tensor
                def _(pe):
                    ln_pe(pe, S)
                    pe.wait_ge(S["xnT"], NT // 2)
                    pe.wait_ge(S["r"], 96)
                    for t in range(NT):
                        last = proj(pe, bank(2)[:, t * HM:(t + 1) * HM], lambda k: XNT[:, k, t * P:(t + 1) * P],
                                    lambda k: wdt[:, k, :], KT)
                    last.then_inc(S["dtp"], 1)
                    pe.wait_ge(S["a"], 1)
                    pe.matmul(bank(3)[:, 0:HM * NT], upto[:, :], a, start=True, stop=True).then_inc(S["cs"], 1)
                    pe.matmul(bank(4)[:, 0:HM * NT], after[:, :], a, start=True, stop=True).then_inc(S["sfx"], 1)
                    pe.matmul(bank(5)[:, 0:HM * NT], ones[:, :], a, start=True, stop=True).then_inc(S["tot"], 1)
                    pe.wait_ge(S["cum"], 1)
                    for b in range(2):
                        last = pe.transpose(bank(6)[:, b * P:(b + 1) * P], cum[:, b * P:(b + 1) * P], ident[:, :])
                    last.then_inc(S["ctr"], 1)

            raws = [raw, raw2]
            S = S2
            first_tile = [BTILE, CTILE]

            def group_tile(g, i):
                return A["w_in"][bass.ds(g + first_tile[i], 1), :, :, :].rearrange("o p k c -> p (o k) c")

            with nc.Block() as block:
                @block.sync
                def _(sp):
                    for i in range(2):
                        sp.dma_start(wx[:, i, :, :], A["w_in"][first_tile[i]]).then_inc(S["w" + str(i)], 16)
                    with sp.Fori(0, GM) as g:
                        for i in range(2):
                            sp.wait_ge(S["pj"], g * 2 + i + 3)
                            sp.dma_start(wx[:, i, :, :], group_tile(g + 1, i)).then_inc(S["w" + str(i)], 16)

                def project(pe, g, i):
                    pe.wait_ge(S["w" + str(i)], g * 16 + 16)
                    pe.wait_ge(S["c"], g * 2 + i + 1)
                    channels(pe, wx[:, i, :, :], 2 * i).then_inc(S["pj"], 1)

                @block.tensor
                def _(pe):
                    for i in range(2):
                        project(pe, 0, i)
                    with pe.Fori(0, GM // 2) as it:
                        for j in range(2):
                            g = it * 2 + j
                            for i in range(2):
                                project(pe, g + 1, i)
                            pe.wait_ge(S["xt"], g * 2 + 1)
                            pe.wait_ge(S["btok"], g + 1)
                            for c in range(NT):
                                last = pe.transpose(bank(4, 2)[:, c * P:(c + 1) * P], bT[:, j, c * P:(c + 1) * P],
                                                    ident[:, :])
                            last.then_inc(S["bt"], 1)
                            pe.wait_ge(S["xt"], g * 2 + 2)
                            pe.wait_ge(S["cb"], g + 1)
                            for c in range(NT):
                                last = pe.matmul(bank(6, 2)[:, c * P:(c + 1) * P], bT[:, j, c * P:(c + 1) * P],
                                                 CT[:, bass.ds(g, 1), c * P:(c + 1) * P].rearrange("p o t -> p (o t)"),
                                                 start=True, stop=True)
                            last.then_inc(S["cbp"], 1)

                def newest(act, g, i):
                    act.wait_ge(S["pj"], g * 2 + i + 3)
                    conv_newest(act, S, i, g + (first_tile[i] - HM), raws[i], 2 * i)

                def silus(act, g, b):
                    act.wait_ge(S["conv"], g * 2 + 1)
                    act.wait_ge(S["cbp"], g + 1)
                    nc.scalar.activation(bT[:, b, :], xT[:, 0, :], ACT.Silu).then_inc(S["xt"], 1)
                    act.wait_ge(S["conv"], g * 2 + 2)
                    nc.scalar.activation(CT[:, bass.ds(g, 1), :].rearrange("p o t -> p (o t)"), xT[:, 1, :],
                                         ACT.Silu).then_inc(S["xt"], 1)

                @block.scalar
                def _(act):
                    for i in range(2):
                        newest(act, 0, i)
                    act.wait_ge(S["conv"], 1)
                    nc.scalar.activation(bT[:, 0, :], xT[:, 0, :], ACT.Silu).then_inc(S["xt"], 1)
                    act.wait_ge(S["conv"], 2)
                    nc.scalar.activation(CT[:, 0, :], xT[:, 1, :], ACT.Silu).then_inc(S["xt"], 1)
                    with act.Fori(0, GM // 2) as it:
                        for j in range(2):
                            g = it * 2 + j
                            for i in range(2):
                                act.wait_ge(S["xt"], g * 2 + i + 1)
                                newest(act, g + 1, i)
                            silus(act, g + 1, 1 - j)

                @block.vector
                def _(v):
                    for i in range(2):
                        conv_taps(v, S, i, i, first_tile[i] - HM, raws[i], 3)
                    with v.Fori(0, GM) as g:
                        for i in range(2):
                            conv_taps(v, S, i, g * 2 + (i + 2), g + (first_tile[i] - HM + 1), raws[i], 3)
                        v.wait_ge(S["bt"], g + 1)
                        v.tensor_copy(BTOK[:, bass.ds(g, 1), :, :].rearrange("p o c n -> p (o c n)"),
                                      bank(4, 2)).then_inc(S["btok"], 1)
                        v.wait_ge(S["cbp"], g + 3)
                        v.tensor_tensor(CB[:, bass.ds(g, 1), :].rearrange("p o (c l) -> p (o c) l", c=NT),
                                        bank(6, 2).rearrange("p (c l) -> p c l", c=NT),
                                        upto[:, :].unsqueeze(1).to_broadcast([P, NT, P]), ALU.mult).then_inc(S["cb"], 1)

            take.at = common
            wg = take(2 * E).rearrange("p (b k c) -> p b k c", b=2, k=KT)
            lam = take(2 * T).rearrange("p (b t) -> p b t", b=2)
            ecs = take(T)
            cumrow = take(2 * T).rearrange("p (b t) -> p b t", b=2)
            xdt, xst, states = take(T), take(T), take(T)
            U = take(4 * T).rearrange("p (j t) -> p j t", j=4)
            sumsq, sq = take(T), take(T)
            wo = take(4 * E).rearrange("p (j e) -> p j e", j=4)
            ve, sd, rr = take(NT), take(NT), take(NT)
            cum_rows = A["cum_rows"].rearrange("(h c) l -> h (c l)", c=NT)
            w_out = A["w_out"].rearrange("(n p) e -> p n e", p=P)
            S = S3
            OCT = GM
            PASSES = HM // OCT
            chunk3 = "p (c l) -> p c l"

            def w_tile(i):
                return A["w_in"][bass.ds(i, 1), :, :, :].rearrange("o p k c -> p (o k) c")

            LAST = OCT - 1
            PAIRS = NT // 2
            PAIR_BANK = (6, 7, 0, 1)

            def all_heads(engine, step):
                step(0, 0)
                with engine.Fori(0, PASSES - 1) as it:
                    for j in range(1, OCT + 1):
                        step(it, j)
                for j in range(1, OCT):
                    step(PASSES - 1, j)

            def place(it, j):
                K = it * OCT + j
                fixed = isinstance(K, int)
                return K, j % 2, it * 2 + j // 4, fixed and K == 0, not (fixed and K == HM - 1)

            def loads(it, j):
                return (it * (OCT // 2) + j // 2 + 1) * 16

            with nc.Block() as block:
                @block.sync
                def _(sp):
                    sp.dma_start(wx[:, 0, :, :], A["w_in"][XTILE]).then_inc(S["wx0"], 16)
                    sp.dma_start(cumrow[:, 0, :], cum_rows[0:1, :].to_broadcast([P, T])).then_inc(S["cr0"], 16)

                    def step(it, j):
                        K, b, G, first, more = place(it, j)
                        if j % 4 == 1:
                            sp.wait_ge(S["op"], G * PAIRS + 1)
                            sp.dma_start(wo, w_out[:, bass.ds(K - 1, 4), :]).then_inc(S["wo"], 16)
                        if more:
                            sp.wait_ge(S["px"], K + 2)
                            sp.dma_start(wx[:, 1 - b, :, :], w_tile(K + (XTILE + 1))).then_inc(S["wx" + str(1 - b)], 16)
                        sp.wait_ge(S["pg"], K + 1)
                        sp.dma_start(wg[:, b, :, :], w_tile(K)).then_inc(S["wg" + str(b)], 16)
                        if more:
                            sp.wait_ge(S["ec"], K + 1)
                            sp.dma_start(cumrow[:, 1 - b, :], cum_rows[bass.ds(K + 1, 1), :].to_broadcast([P, T]))\
                              .then_inc(S["cr" + str(1 - b)], 16)

                    all_heads(sp, step)

                def out_pair(pe, G, p):
                    for t in range(2 * p, 2 * p + 2):
                        last = proj(pe, bank(PAIR_BANK[p])[:, t % 2 * E:(t % 2 + 1) * E],
                                    lambda i: U[:, i, t * P:(t + 1) * P], lambda i: wo[:, i, :], 4)
                    last.then_inc(S["op"], 1)

                def out_first(pe, K, G, states):
                    pe.wait_ge(S["u"], K + 1)
                    pe.wait_ge(S["wos"], G)
                    pe.wait_ge(S["sg"], K + 1)
                    out_pair(pe, G, 0)
                    out_pair(pe, G, 1)
                    pe.wait_ge(S["st"], states)
                    pe.wait_ge(S["ad"], G * 3 + 1)
                    for t in range(NT):
                        last = pe.matmul(bank(3)[:, 3 * P + t:3 * P + t + 1], sumsq[:, t * P:(t + 1) * P], ones[:, 0:1],
                                         start=True, stop=True)
                    last.then_inc(S["vr"], 1)

                def out_second(pe, G, convolved):
                    pe.wait_ge(S["c"], convolved)
                    out_pair(pe, G, 2)
                    out_pair(pe, G, 3)

                @block.tensor
                def _(pe):
                    pe.wait_ge(S["wx0"], 16)
                    channels(pe, wx[:, 0, :, :]).then_inc(S["px"], 1)

                    def gate(it, j):
                        K, b, G, first, more = place(it, j)
                        pe.wait_ge(S["wg" + str(b)], loads(it, j))
                        pe.wait_ge(S["sg"], K + 1)
                        channels(pe, wg[:, b, :, :], 6).then_inc(S["pg"], 1)

                    def step(it, j):
                        K, b, G, first, more = place(it, j)
                        group_end = j % 4 == 0 and not first
                        pe.wait_ge(S["xt"], K + 1)
                        pe.wait_ge(S["st"], K + 1)
                        for c in range(NT):
                            last = pe.transpose(bank(2, 2)[:, c * P:(c + 1) * P], xT[:, b, c * P:(c + 1) * P],
                                                ident[:, :])
                        last.then_inc(S["tx"], 1)
                        if more:
                            pe.wait_ge(S["wx" + str(1 - b)], loads(it, j + 1))
                            pe.wait_ge(S["c"], K + 2)
                            if j % 4 == 1 and not (isinstance(K, int) and K == 1):
                                pe.wait_ge(S["oc"], G * PAIRS)
                            channels(pe, wx[:, 1 - b, :, :]).then_inc(S["px"], 1)
                        pe.wait_ge(S["xd"], K + 1)
                        pe.wait_ge(S["xs"], K + 1)
                        for c in range(NT - 1):
                            last = pe.matmul(bank(2, 2)[:, c * P:(c + 1) * P], BTOK[:, j % OCT, c, :],
                                             xst[:, c * P:(c + 1) * P], start=True, stop=True)
                        last.then_inc(S["ds"], 1)
                        if group_end:
                            out_first(pe, K, G, K + 2)
                        else:
                            gate(it, j)
                        pe.wait_ge(S["mm"], K + 1)
                        pe.wait_ge(S["cs"], K + 1)
                        pe.wait_ge(S["st"], K + 2)
                        pe.wait_ge(S["yd"], K + 1)
                        for c in range(NT):
                            r = slice(c * P, (c + 1) * P)
                            last = pe.matmul(bank(4, 2)[:, r], xdt[:, r], lam[:, b, r], start=True, stop=(c == 0))
                            if c:
                                last = pe.matmul(bank(4, 2)[:, r], states[:, (c - 1) * P:c * P], ecs[:, r],
                                                 start=False, stop=True)
                        last.then_inc(S["y"], 1)
                        if group_end:
                            out_second(pe, G, K + 3)
                            pe.wait_ge(S["oc"], G * PAIRS - 2)
                            gate(it, j)

                    all_heads(pe, step)
                    out_first(pe, HM, HM // 4, HM + 1)
                    out_second(pe, HM // 4, HM + 1)

                @block.scalar
                def _(act):
                    act.wait_ge(S["px"], 3)
                    conv_newest(act, S, 0, 0, raw)
                    act.wait_ge(S["conv"], 1)
                    nc.scalar.activation(xT[:, 0, :], xT[:, 0, :], ACT.Silu).then_inc(S["xt"], 1)

                    def decays(n, b, loaded):
                        act.wait_ge(S["df"], n + 1)
                        nc.scalar.activation(lam[:, b, :], lam[:, b, :], ACT.Relu, scale=-1.0).then_inc(S["rl"], 1)
                        act.wait_ge(S["rl"], n + 1)
                        nc.scalar.activation(lam[:, b, :], lam[:, b, :], ACT.Exp, scale=-1.0).then_inc(S["lm"], 1)
                        act.wait_ge(S["cr" + str(b)], loaded)
                        act.wait_ge(S["y"], n + 1)
                        nc.scalar.activation(ecs, cumrow[:, b, :], ACT.Exp).then_inc(S["ec"], 1)

                    def squares(K, j, G):
                        act.wait_ge(S["u"], K + 2)
                        if j % 4 == 0:
                            act.wait_ge(S["vr"], G + 1)
                            nc.scalar.activation(sumsq, U[:, 0, :], ACT.Square).then_inc(S["sqs"], 1)
                        else:
                            act.wait_ge(S["ad"], G * 3 + j % 4)
                            nc.scalar.activation(sq, U[:, j % 4, :], ACT.Square).then_inc(S["sqs"], 1)

                    def root(G):
                        act.wait_ge(S["vv"], G)
                        nc.scalar.activation(sd, ve, ACT.Sqrt).then_inc(S["sd"], 1)

                    decays(0, 0, 16)

                    def step(it, j):
                        K, b, G, first, more = place(it, j)
                        group_end = j % 4 == 0 and not first
                        if more:
                            act.wait_ge(S["px"], K + 4)
                            nc.scalar.copy(raw[:, CONV - 1:], bank(0, 2)).then_inc(S["raw"], 1)
                        if more:
                            act.wait_ge(S["u"], K + 1)
                            nc.scalar.activation(xT[:, 1 - b, :], bank(0, 2), ACT.Identity, bias=tap_of(K + 1, CONV),
                                                 scale=tap_of(K + 1, CONV - 1)).then_inc(S["c"], 1)
                        if not first:
                            squares(K - 1, j - 1, it * 2 + (j - 1) // 4)

                        def gate():
                            act.wait_ge(S["pg"], K + 3)
                            act.wait_ge(S["op"], G * PAIRS + 1)
                            nc.scalar.activation(U[:, j % 4, :], bank(6, 2), ACT.Silu).then_inc(S["sg"], 1)

                        if not group_end:
                            gate()
                        if more:
                            act.wait_ge(S["conv"], K + 2)
                            nc.scalar.activation(xT[:, 1 - b, :], xT[:, 1 - b, :], ACT.Silu).then_inc(S["xt"], 1)
                        if group_end:
                            root(G)
                        if more:
                            decays(K + 1, 1 - b, loads(it, j + 1))
                        if group_end:
                            gate()

                    all_heads(act, step)
                    squares(HM - 1, LAST, HM // 4 - 1)
                    root(HM // 4)

                @block.gpsimd
                def _(g):
                    def difference(n, b, loaded):
                        g.wait_ge(S["cr" + str(b)], loaded)
                        g.wait_ge(S["y"], n if not isinstance(n, int) or n else 1)
                        g.tensor_tensor(lam[:, b, :].rearrange(chunk3, c=NT), cumrow[:, b, :].rearrange(chunk3, c=NT),
                                        cum[:, bass.ds(n * NT, NT)].unsqueeze(2).to_broadcast([P, NT, P]),
                                        ALU.subtract).then_inc(S["df"], 1)

                    def add_squares(K, j, G):
                        g.wait_ge(S["sqs"], K + 1)
                        g.wait_ge(S["ad"], G * 3 + j % 4)
                        g.tensor_tensor(sumsq, sumsq, sq, ALU.add).then_inc(S["ad"], 1)

                    difference(0, 0, 16)

                    def step(it, j):
                        K, b, G, first, more = place(it, j)
                        g.wait_ge(S["xd"], K + 1)
                        g.wait_ge(S["ds"], K + 1)
                        g.tensor_tensor(xst.rearrange(chunk3, c=NT), xdt.rearrange(chunk3, c=NT),
                                        dend[:, bass.ds(K * NT, NT)].unsqueeze(2).to_broadcast([P, NT, P]),
                                        ALU.mult).then_inc(S["xs"], 1)
                        g.wait_ge(S["ec"], K + 2)
                        g.tensor_tensor(ecs, ecs, CT[:, j % OCT, :], ALU.mult).then_inc(S["cs"], 1)
                        if (j - 1) % 4 and not first:
                            add_squares(K - 1, j - 1, it * 2 + (j - 1) // 4)
                        if more:
                            difference(K + 1, 1 - b, loads(it, j + 1))
                        if j % 4 == 2:
                            g.wait_ge(S["wo"], G * 16 + 16)
                            g.tensor_tensor(wo, wo, nw[:, bass.ds(K - 2, 4)].unsqueeze(2).to_broadcast([P, 4, E]),
                                            ALU.mult).then_inc(S["wos"], 1)

                    all_heads(g, step)
                    add_squares(HM - 1, LAST, HM // 4 - 1)

                @block.vector
                def _(v):
                    QUARTERS = 4
                    QT = T // QUARTERS

                    def tap_part(n, b, w, q):
                        if w:
                            v.wait_ge(S["tap"], n * ((CONV - 2) * QUARTERS) + ((w - 1) * QUARTERS + q + 1))
                        else:
                            v.wait_ge(S["c"], n + 2)
                        xq = xT[:, b, q * QT:(q + 1) * QT]
                        last = v.scalar_tensor_tensor(xq, raw[:, w + q * QT:w + (q + 1) * QT], tap_of(n, w), xq,
                                                      ALU.mult, ALU.add)
                        if w < CONV - 2:
                            last.then_inc(S["tap"], 1)
                        elif q == QUARTERS - 1:
                            last.then_inc(S["conv"], 1)

                    for w in range(CONV - 1):
                        for q in range(QUARTERS):
                            tap_part(0, 0, w, q)

                    def normalise(G):
                        v.wait_ge(S["vr"], G + 1)
                        v.tensor_scalar(ve, bank(3)[:, 3 * P:3 * P + NT], 1.0 / (4 * P), 1e-6, ALU.mult,
                                        ALU.add).then_inc(S["vv"], 1)
                        v.wait_ge(S["sd"], G)
                        v.reciprocal(rr, sd).then_inc(S["rr"], 1)
                        v.wait_ge(S["rr"], G)
                        for p in range(PAIRS):
                            v.wait_ge(S["op"], G * PAIRS + (p + 2 - PAIRS))
                            for t in range(2 * p, 2 * p + 2):
                                last = v.scalar_tensor_tensor(X[:, t, :], bank(PAIR_BANK[p])[:, t % 2 * E:(t % 2 + 1) * E],
                                                              rr[:, t:t + 1], X[:, t, :], ALU.mult, ALU.add)
                            last.then_inc(S["oc"], 1)

                    def skip_added(K, b):
                        v.wait_ge(S["y"], K + 2)
                        v.scalar_tensor_tensor(xT[:, b, :], xT[:, b, :], col(dskip, K), bank(4, 2), ALU.mult,
                                               ALU.add).then_inc(S["yd"], 1)

                    def gated(K, b, j):
                        v.wait_ge(S["yd"], K + 2)
                        v.wait_ge(S["sg"], K + 2)
                        v.tensor_tensor(U[:, j % 4, :], U[:, j % 4, :], xT[:, b, :], ALU.mult).then_inc(S["u"], 1)

                    def step(it, j):
                        K, b, G, first, more = place(it, j)
                        if not first:
                            skip_added(K - 1, 1 - b)
                        v.wait_ge(S["tx"], K + 1)
                        v.wait_ge(S["y"], K + 1)
                        v.tensor_tensor(xdt.rearrange(chunk3, c=NT), bank(2, 2).rearrange(chunk3, c=NT),
                                        dt[:, bass.ds(K * NT, NT)].unsqueeze(2).to_broadcast([P, NT, P]),
                                        ALU.mult).then_inc(S["xd"], 1)
                        if not first:
                            gated(K - 1, 1 - b, j - 1)
                        v.wait_ge(S["lm"], K + 1)
                        v.tensor_tensor(lam[:, b, :], lam[:, b, :], CB[:, j % OCT, :], ALU.mult).then_inc(S["mm"], 1)
                        v.wait_ge(S["ds"], K + 2)
                        taps = [(w, q) for w in range(CONV - 1) for q in range(QUARTERS)] if more else []
                        v.tensor_copy(states[:, 0:P], bank(2, 2)[:, 0:P]).then_inc(S["rc"], 1)
                        for c in range(1, NT - 1):
                            if taps and c > 1:
                                tap_part(K + 1, 1 - b, *taps.pop(0))
                            v.wait_ge(S["rc"], K * (NT - 2) + c)
                            v.scalar_tensor_tensor(states[:, c * P:(c + 1) * P], states[:, (c - 1) * P:c * P],
                                                   col(etot, K * NT + c), bank(2, 2)[:, c * P:(c + 1) * P],
                                                   ALU.mult, ALU.add).then_inc(S["rc"] if c < NT - 2 else S["st"], 1)
                        for w, q in taps:
                            tap_part(K + 1, 1 - b, w, q)
                        if j % 4 == 0 and not first:
                            normalise(G)

                    all_heads(v, step)
                    skip_added(HM - 1, 1)
                    gated(HM - 1, 1, LAST)
                    normalise(HM // 4)

        def ponder_ffn(name, last_phase):
            take = Region()
            S = sems(name, LN + " w r c pad o_stats o_aggr o_ve o_sd o_rstd o_xn m d q vr ve2 sd2 rc n g t"
                     " bs ba nt tc up hr ht ap th hb h dn b1 bc bcr gp gs sg mul out og ob fin st")
            SO = {k: S["o_" + k] for k in "stats aggr ve sd rstd xn".split()}
            M, MO = ln_region(take), ln_region(take)
            cols = take(4 * KT).rearrange("p (n k) -> p n k", k=KT)
            in_g, in_b, pn_g, pn_b = (cols[:, i, :] for i in range(4))
            d1_b = take(FT)
            agg = take(KT * E).rearrange("p (k e) -> p k e", k=KT)
            bcw = take(KT * E).rearrange("p (k e) -> p k e", k=KT)
            gw = take(KT * E).rearrange("p (k e) -> p k e", k=KT)
            d1 = take(KT * DFF).rearrange("p (k f) -> p k f", k=KT)
            d2 = take(FT * E).rearrange("p (k e) -> p k e", k=FT)
            gb, bcb, out_g, out_b, bcrow = (take(E) for _ in range(5))
            mean_w, negmean_w = take(P), take(P)
            dev, dsq, tn, tt, thc = (take(KT) for _ in range(5))
            hb, hh = take(FT), take(FT)
            agg_b, d2_b, th, th2, tr = (take(E)[0:1, :] for _ in range(5))
            hrow = take(DFF)[0:1, :]
            rst, rmv = take(6)[0:1, :], take(2)[0:1, :]
            var, vsd, vrs = take(1), take(1), take(1)
            SG = take(NT * E).rearrange("p (t e) -> p t e", t=NT)

            def wide(r):
                return r.unsqueeze(1).to_broadcast([P, NT, E])

            with nc.Block() as block:
                @block.sync
                def _(sp):
                    for dst, src in ((gb, "gate_b"), (bcb, "bc_b"), (out_g, "out_g"), (out_b, "out_b")):
                        sp.dma_start(dst, row(A[src])).then_inc(S["r"], 16)
                    sp.dma_start(cols, A["cols"]).then_inc(S["r"], 16)
                    sp.dma_start(d1_b, A["d1_b"]).then_inc(S["r"], 16)
                    for dst, src in ((agg_b, "agg_b"), (d2_b, "d2_b")):
                        sp.dma_start(dst, A[src].rearrange("(a d) -> a d", a=1)).then_inc(S["r"], 16)
                    for dst, src in ((agg, "agg_w"), (gw, "gate_w"), (d1, "d1_w"), (d2, "d2_w"), (bcw, "bc_w")):
                        sp.dma_start(dst, A[src].rearrange("(k p) f -> p k f", p=P)).then_inc(S["w"], 16)
                    if last_phase:
                        for t in range(NT):
                            sp.wait_ge(S["fin"], t + 1)
                            sp.dma_start(out[t * P:(t + 1) * P, :], X[:, t, :]).then_inc(S["st"], 16)
                        sp.wait_ge(S["st"], 16 * NT)

                @block.gpsimd
                def _(g):
                    g.memset(mean_w, 1.0 / E).then_inc(S["pad"], 1)
                    g.memset(negmean_w, -1.0 / E).then_inc(S["pad"], 1)

                def col_ln_dve(v, src, gamma, beta):
                    v.wait_ge(S["m"], 1)
                    v.tensor_scalar(dev, src, bank(2)[:, 0:1], None, ALU.add).then_inc(S["d"], 1)
                    v.wait_ge(S["d"], 1)
                    v.tensor_tensor(dsq, dev, dev, ALU.mult).then_inc(S["q"], 1)
                    v.wait_ge(S["vr"], 1)
                    v.tensor_scalar(var, bank(3)[:, 0:1], 1e-6, None, ALU.add).then_inc(S["ve2"], 1)
                    v.wait_ge(S["sd2"], 1)
                    v.reciprocal(vrs, vsd).then_inc(S["rc"], 1)
                    v.wait_ge(S["rc"], 1)
                    v.scalar_tensor_tensor(tn, dev, vrs[:, 0:1], gamma, ALU.mult, ALU.mult).then_inc(S["n"], 1)
                    v.wait_ge(S["n"], 1)
                    v.tensor_tensor(tt, tn, beta, ALU.add).then_inc(S["t"], 1)

                def col_ln_pe(pe, src):
                    proj(pe, bank(2)[:, 0:1], lambda k: negmean_w, lambda k: src[:, k:k + 1], KT).then_inc(S["m"], 1)
                    pe.wait_ge(S["q"], 1)
                    proj(pe, bank(3)[:, 0:1], lambda k: mean_w, lambda k: dsq[:, k:k + 1], KT).then_inc(S["vr"], 1)

                def to_column(pe, dst, src):
                    return pe.matmul(dst, src, ones[0:1, 0:1], start=True, stop=True)

                newest = XNT[:, :, T - 1]

                @block.tensor
                def _(pe):
                    ln_pe(pe, S)
                    pe.wait_ge(S["xnT"], NT // 2)
                    pe.wait_ge(S["pad"], 2)
                    col_ln_pe(pe, newest)
                    pe.wait_ge(S["w"], 16 * 5)
                    def gates(g):
                        if g >= 2:
                            pe.wait_ge(S["gs"], g - 1)
                        for h in range(2):
                            t = 2 * g + h
                            last = proj(pe, bank(6 + g % 2)[:, h * E:(h + 1) * E],
                                        lambda k: XNT[:, k, t * P:(t + 1) * P], lambda k: gw[:, k, :], KT)
                        last.then_inc(S["gp"], 1)
                    for g in range(NT // 2):
                        gates(g)
                    pe.wait_ge(S["t"], 1)
                    proj(pe, bank(2)[0:1, 0:E], lambda k: tt[:, k:k + 1], lambda k: agg[:, k, :], KT).then_inc(S["ap"], 1)
                    with pe.Fori(0, 4) as i:
                        pe.wait_ge(S["nt"], i + 1)
                        for k in range(KT):
                            last = to_column(pe, bank(1)[:, k:k + 1], tr[:, k * P:(k + 1) * P])
                        last.then_inc(S["tc"], 1)
                        pe.wait_ge(S["t"], i + 2)
                        for h in range(2):
                            proj(pe, bank(4 + h)[0:1, :], lambda k: tt[:, k:k + 1],
                                 lambda k: d1[:, k, h * BANK:(h + 1) * BANK], KT).then_inc(S["up"], 1)
                        for h in range(2):
                            pe.wait_ge(S["hr"], i * 2 + (h + 1))
                            for f in range(h * FT // 2, (h + 1) * FT // 2):
                                last = to_column(pe, bank(0)[:, f:f + 1], hrow[:, f * P:(f + 1) * P])
                        last.then_inc(S["ht"], 1)
                        pe.wait_ge(S["h"], i + 1)
                        proj(pe, bank(2)[0:1, 0:E], lambda k: hh[:, k:k + 1], lambda k: d2[:, k, :], FT)\
                            .then_inc(S["dn"], 1)
                    pe.wait_ge(S["th"], 5)
                    for k in range(KT):
                        last = to_column(pe, bank(1)[:, k:k + 1], th[:, k * P:(k + 1) * P])
                    last.then_inc(S["tc"], 1)
                    pe.wait_ge(S["t"], 6)
                    proj(pe, bank(3)[:, 0:E], lambda k: thc[:, k:k + 1].to_broadcast([P, P]), lambda k: bcw[:, k, :],
                         KT).then_inc(S["bc"], 1)

                @block.scalar
                def _(act):
                    ln_sqrt(act, S, M)
                    ln_copy(act, S)
                    act.wait_ge(S["ve2"], 1)
                    nc.scalar.activation(vsd, var, ACT.Sqrt).then_inc(S["sd2"], 1)
                    act.wait_ge(S["gs"], NT // 2)
                    nc.scalar.activation(SG, SG, ACT.Sigmoid).then_inc(S["sg"], 1)
                    with act.Fori(0, 4) as i:
                        act.wait_ge(S["ve2"], i + 2)
                        nc.scalar.activation(vsd[0:1, :], var[0:1, :], ACT.Sqrt).then_inc(S["sd2"], 1)
                        act.wait_ge(S["up"], i * 2 + 1)
                        nc.scalar.copy(hrow[:, 0:BANK], bank(4)[0:1, :]).then_inc(S["hr"], 1)
                        act.wait_ge(S["hb"], i + 1)
                        nc.scalar.activation(hh, hb, ACT.Gelu).then_inc(S["h"], 1)
                    ln_sqrt(act, SO, MO)

                @block.vector
                def _(v):
                    ln_dve(v, S, M, X, XN, 1e-5)
                    v.wait_ge(S["r"], 16 * 8)
                    col_ln_dve(v, newest, in_g, in_b)
                    for g in range(NT // 2):
                        v.wait_ge(S["gp"], g + 1)
                        v.tensor_tensor(SG[:, 2 * g:2 * g + 2, :], bank(6 + g % 2).rearrange("p (t e) -> p t e", t=2),
                                        gb.unsqueeze(1).to_broadcast([P, 2, E]), ALU.add).then_inc(S["gs"], 1)
                        for t in range(2 * g, 2 * g + 2):
                            v.scalar_tensor_tensor(X[:, t, :], out_b, 0.5, X[:, t, :], ALU.mult,
                                                   ALU.add).then_inc(S["ob"], 1)
                    v.wait_ge(S["ap"], 1)
                    v.tensor_tensor(th, bank(2)[0:1, 0:E], agg_b, ALU.add).then_inc(S["th"], 1)
                    v.wait_ge(S["th"], 1)
                    with v.Fori(0, 4) as i:
                        v.bn_stats(rst, th).then_inc(S["bs"], 1)
                        v.wait_ge(S["bs"], i + 1)
                        v.tensor_tensor(th2, th, d2_b, ALU.add).then_inc(S["b1"], 1)
                        v.bn_aggr(rmv, rst).then_inc(S["ba"], 1)
                        v.wait_ge(S["ba"], i + 1)
                        v.tensor_scalar(var[0:1, :], rmv[:, 1:2], 1e-6, None, ALU.add).then_inc(S["ve2"], 1)
                        v.wait_ge(S["sd2"], i + 2)
                        v.reciprocal(vrs[0:1, :], vsd[0:1, :]).then_inc(S["rc"], 1)
                        v.wait_ge(S["rc"], i + 2)
                        v.tensor_scalar(tr, th, rmv[:, 0:1], vrs[0:1, 0:1], ALU.subtract, ALU.mult).then_inc(S["nt"], 1)
                        v.wait_ge(S["tc"], i + 1)
                        v.tensor_tensor(tn, bank(1)[:, 0:KT], pn_g, ALU.mult).then_inc(S["n"], 1)
                        v.wait_ge(S["n"], i + 2)
                        v.tensor_tensor(tt, tn, pn_b, ALU.add).then_inc(S["t"], 1)
                        v.wait_ge(S["up"], i * 2 + 2)
                        v.wait_ge(S["hr"], i * 2 + 1)
                        v.tensor_copy(hrow[:, BANK:], bank(5)[0:1, :]).then_inc(S["hr"], 1)
                        v.wait_ge(S["ht"], i + 1)
                        v.tensor_tensor(hb, bank(0)[:, 0:FT], d1_b, ALU.add).then_inc(S["hb"], 1)
                        v.wait_ge(S["dn"], i + 1)
                        v.wait_ge(S["b1"], i + 1)
                        v.tensor_tensor(th, bank(2)[0:1, 0:E], th2, ALU.add).then_inc(S["th"], 1)
                        v.wait_ge(S["th"], i + 2)
                    v.wait_ge(S["tc"], 5)
                    v.tensor_copy(thc, bank(1)[:, 0:KT]).then_inc(S["t"], 1)
                    v.wait_ge(S["bc"], 1)
                    v.tensor_tensor(bcrow, bank(3)[:, 0:E], bcb, ALU.add).then_inc(S["bcr"], 1)
                    v.wait_ge(S["bcr"], 1)
                    v.wait_ge(S["sg"], 1)
                    v.tensor_tensor(SG, SG, wide(bcrow), ALU.mult).then_inc(S["mul"], 1)
                    v.wait_ge(S["mul"], 1)
                    v.tensor_tensor(SG, SG, XN, ALU.add).then_inc(S["out"], 1)
                    v.wait_ge(S["out"], 1)
                    ln_dve(v, SO, MO, SG, SG, 1e-6)
                    v.wait_ge(SO["xn"], NT)
                    v.tensor_tensor(SG, SG, wide(out_g), ALU.mult).then_inc(S["og"], 1)
                    v.wait_ge(S["og"], 1)
                    v.wait_ge(S["ob"], NT)
                    for t in range(NT):
                        v.scalar_tensor_tensor(X[:, t, :], SG[:, t, :], 0.5, X[:, t, :], ALU.mult,
                                               ALU.add).then_inc(S["fin"], 1)

        def attention():
            take = Region()
            S = sems("ah", LN + " w0 w1 wo tab pq t1 t2 rd vp vc sc msk mx ex rcp no tr2 ta tw tv pv oe op oa")
            M = ln_region(take)
            spare = take(16)
            OT = take(NH * T).rearrange("p (h t) -> p h t", h=NH)
            wo = take(NH * E).rearrange("p (h e) -> p h e", h=NH)
            cos_t, sin_t = take(T), take(T)
            wqkv = take(6 * E).rearrange("p (b u k d) -> p b u k d", b=2, u=3, k=KT)
            qk = take(4 * T).rearrange("p (b u t) -> p b u t", b=2, u=2)
            V = take(2 * T).rearrange("p (b t d) -> p b t d", b=2, t=NT)
            turn = take(2 * HALF).rearrange("p (b t) -> p b t", b=2)
            pr = take(2 * T).rearrange("p (b t) -> p b t", b=2)
            PT = take(2 * T).rearrange("p (b t) -> p b t", b=2)
            nmx, rsum, rinv = take(2), take(2), take(2)
            NU = 4
            FOUR = BANK // P
            LATE = NT - FOUR
            HALFP = P // 2

            w_o = A["wo"].rearrange("(h p) e -> p h e", p=P)
            with nc.Block() as block:
                @block.sync
                def _(sp):
                    sp.dma_start(wqkv[:, 0, :, :, :], A["w_qkv"][0]).then_inc(S["w0"], 16)
                    sp.dma_start(cos_t, A["cos"]).then_inc(S["tab"], 16)
                    sp.dma_start(sin_t, A["sin"]).then_inc(S["tab"], 16)
                    sp.dma_start(wqkv[:, 1, :, :, :], A["w_qkv"][1]).then_inc(S["w1"], 16)
                    with sp.Fori(0, NH // 2 - 1) as it:
                        for j in range(2):
                            h = it * 2 + j
                            sp.wait_ge(S["vp"], (h + 1) * NU)
                            sp.dma_start(wqkv[:, j, :, :, :], A["w_qkv"][bass.ds(h + 2, 1)]
                                         .rearrange("o p u k d -> p (o u) k d")).then_inc(S["w" + str(j)], 16)
                            if j == 0:
                                sp.dma_start(wo[:, bass.ds(h, 2), :], w_o[:, bass.ds(h, 2), :]).then_inc(S["wo"], 16)
                    sp.dma_start(wo[:, NH - 2:, :], w_o[:, NH - 2:, :]).then_inc(S["wo"], 16)

                def project(pe, f, b, u, loads):
                    if u == 0:
                        pe.wait_ge(S["w" + str(b)], loads * 16)
                    pe.wait_ge(S["t2"], f * NU + (u + 1))
                    if u < 2 and not (isinstance(f, int) and f == 0):
                        pe.wait_ge(S["tv"], f * FOUR + (u - 3))
                    proj(pe, bank(u % 2), lambda k: wqkv[:, b, u // 2, k, :],
                         lambda k: XNT[:, k, u % 2 * HALF:(u % 2 + 1) * HALF], KT).then_inc(S["pq"], 1)

                def project_v(pe, f, b, u):
                    pe.wait_ge(S["vc"], f * NU + (u + 1))
                    if not (isinstance(f, int) and f == 0):
                        pe.wait_ge(S["oe"], f * NT + (u - LATE + 1))
                    for t in range(2):
                        last = proj(pe, bank(7)[:, (2 + t) * P:(3 + t) * P],
                                    lambda k: XNT[:, k, (2 * u + t) * P:(2 * u + t + 1) * P],
                                    lambda k: wqkv[:, b, 2, k, :], KT)
                    last.then_inc(S["vp"], 1)

                def heads(engine, first, step, last):
                    first()
                    with engine.Fori(0, NH // 2 - 1) as it:
                        for j in range(2):
                            for i in range(1, NT):
                                step(it * 2 + j, j, i, True, None)
                            step(it * 2 + (j + 1), 1 - j, 0, True, it + 2)
                    for j in range(2):
                        for i in range(1, NT):
                            step(NH - 2 + j, j, i, j == 0, None)
                        if j == 0:
                            step(NH - 1, 1, 0, False, None)
                    last()

                @block.tensor
                def _(pe):
                    def scores(h, j, i):
                        n = h * NT + i
                        if i == 0:
                            pe.wait_ge(S["rd"], (h + 1) * NU + 2)
                        pe.wait_ge(S["ex"], n + 1)
                        for lo in range(0, (i + 1) * P, BANK):
                            hi = min(lo + BANK, (i + 1) * P)
                            last = pe.matmul(bank(2 + i % 2 * 2, 2)[:, lo:hi], qk[:, j, 0, i * P:(i + 1) * P],
                                             qk[:, j, 1, lo:hi], start=True, stop=True)
                        last.then_inc(S["sc"], 1)

                    def transposed(h, i, rotations):
                        n = h * NT + i
                        pe.wait_ge(S["no"], n + 1)
                        pe.wait_ge(S["ta"], n + 1)
                        for c in range(0, min(FOUR, i + 1)):
                            last = pe.transpose(bank(6)[:, c * P:(c + 1) * P], pr[:, i % 2, c * P:(c + 1) * P],
                                                ident[:, :])
                        last.then_inc(S["tr2"], 1)
                        if i >= LATE:
                            if i < LATE + 2:
                                pe.wait_ge(S["t2"], rotations)
                            pe.wait_ge(S["tv"], h * FOUR + (i - LATE + 1))
                            for c in range(FOUR, i + 1):
                                last = pe.transpose(bank(i % 2)[:, (c - FOUR) * P:(c - FOUR + 1) * P],
                                                    pr[:, i % 2, c * P:(c + 1) * P], ident[:, :])
                            last.then_inc(S["tw"], 1)

                    def outputs(h, j, i, more=False):
                        if more and i >= LATE:
                            pe.wait_ge(S["vc"], (h + 1) * NU + (i - LATE + 2))
                        elif i == 0:
                            pe.wait_ge(S["vc"], (h + 1) * NU + 1)
                        n = h * NT + i
                        pe.wait_ge(S["oe"], n + 1)
                        pe.wait_ge(S["ta"], n + 2)
                        for c in range(i + 1):
                            if c == FOUR:
                                pe.wait_ge(S["tv"], h * FOUR + (i - LATE + 3))
                            last = pe.matmul(bank(7)[:, 0:P], V[:, j, c, :],
                                             PT[:, i % 2, c * P:(c + 1) * P], start=(c == 0), stop=(c == i))
                        last.then_inc(S["pv"], 1)

                    def step(h, j, i, more, loads):
                        if i + 1 < NT:
                            scores(h, j, i + 1)
                        elif more:
                            scores(h + 1, 1 - j, 0)
                        if more and i < NU:
                            project(pe, h + 1, 1 - j, i, loads)
                        if i:
                            outputs(h, j, i - 1, more)
                        elif not (isinstance(h, int) and h == 0):
                            outputs(h - 1, 1 - j, NT - 1, True)
                        transposed(h, i, (h + 2 if more else h + 1) * NU + 2)
                        if more and i >= LATE:
                            project_v(pe, h + 1, 1 - j, i - LATE)

                    def first():
                        ln_pe(pe, S)
                        pe.wait_ge(S["xnT"], NT // 2)
                        for u in range(NU):
                            project(pe, 0, 0, u, 1)
                        for u in range(NU):
                            project_v(pe, 0, 0, u)
                        scores(0, 0, 0)
                        step(0, 0, 0, True, 1)

                    def last_step():
                        outputs(NH - 1, 1, NT - 1)
                        pe.wait_ge(S["wo"], NH // 2 * 16)
                        pe.wait_ge(S["oe"], NH * NT + 1)
                        for t in range(NT):
                            if t >= 2:
                                pe.wait_ge(S["oa"], t - 1)
                            proj(pe, bank(2 + t % 2)[:, 0:E], lambda h: OT[:, h, t * P:(t + 1) * P],
                                 lambda h: wo[:, h, :], NH).then_inc(S["op"], 1)

                    heads(pe, first, step, last_step)

                @block.scalar
                def _(act):
                    def exponentials(h, i):
                        n, b = h * NT + i, i % 2
                        act.wait_ge(S["mx"], n + 1)
                        act.wait_ge(S["tr2"], n + 1)
                        if i >= LATE + 2 or i < 2:
                            act.wait_ge(S["tw"], h * FOUR + (i - LATE + 1 if i >= 2 else i + 1))
                        nc.scalar.activation(pr[:, b, 0:(i + 1) * P], bank(2 + 2 * b, 2)[:, 0:(i + 1) * P],
                                             ACT.Exp, bias=nmx[:, b:b + 1], accum_out=rsum[:, b:b + 1])\
                          .then_inc(S["ex"], 1)

                    def turned(h, i):
                        n = h * NT + i
                        act.wait_ge(S["tr2"], n + 3)
                        act.wait_ge(S["pv"], n + 1)
                        w = min(FOUR, i + 1) * P
                        nc.scalar.copy(PT[:, i % 2, 0:w], bank(6)[:, 0:w]).then_inc(S["ta"], 1)

                    def output(h, i):
                        act.wait_ge(S["pv"], h * NT + (i + 3))
                        nc.scalar.copy(OT[:, bass.ds(h, 1), i * P:(i + 1) * P].rearrange("p o t -> p (o t)"),
                                       bank(7)[:, 0:P]).then_inc(S["oe"], 1)

                    def values(f, b, u):
                        act.wait_ge(S["vp"], f * NU + (u + 1))
                        nc.scalar.copy(V[:, b, 2 * u:2 * u + 2, :],
                                       bank(7)[:, 2 * P:4 * P].rearrange("p (t d) -> p t d", t=2)).then_inc(S["vc"], 1)

                    def step(h, j, i, more, loads):
                        def ahead():
                            if i + 1 < NT:
                                exponentials(h, i + 1)
                            elif more:
                                exponentials(h + 1, 0)
                        if i < LATE:
                            ahead()
                        if i:
                            output(h, i - 1)
                        elif not (isinstance(h, int) and h == 0):
                            output(h - 1, NT - 1)
                        turned(h, i)
                        if i >= LATE:
                            ahead()
                        if more and i >= LATE:
                            values(h + 1, 1 - j, i - LATE)

                    def first():
                        ln_sqrt(act, S, M)
                        ln_copy(act, S)
                        for u in range(NU):
                            values(0, 0, u)
                        exponentials(0, 0)
                        step(0, 0, 0, True, 1)

                    heads(act, first, step, lambda: output(NH - 1, NT - 1))

                @block.gpsimd
                def _(g):
                    def add(f, b, u):
                        g.wait_ge(S["t2"], f * NU + (u + 3))
                        dst = qk[:, b, u // 2, u % 2 * HALF:(u % 2 + 1) * HALF]
                        g.tensor_tensor(dst, dst, turn[:, u % 2, :], ALU.add).then_inc(S["rd"], 1)

                    def step(h, j, i, more, loads):
                        if more and i < NU:
                            add(h + 1, 1 - j, i)

                    def first():
                        credit(g, spare, [(S[s], n) for s, n in (("t2", 2), ("rd", 2), ("vc", 1), ("ex", 2), ("tr2", 2),
                                                                 ("ta", 1), ("tw", 2), ("tv", 2), ("pv", 2), ("oe", 1))])
                        for u in range(NU):
                            add(0, 0, u)
                        step(0, 0, 0, True, 1)

                    heads(g, first, step, lambda: None)

                @block.vector
                def _(v):
                    def rotate(f, b, u):
                        r = f * NU + u
                        cols_ = slice(u % 2 * HALF, (u % 2 + 1) * HALF)
                        v.wait_ge(S["pq"], r + 1)
                        v.tensor_tensor(qk[:, b, u // 2, cols_], bank(u % 2), cos_t[:, cols_], ALU.mult).then_inc(S["t1"], 1)
                        v.wait_ge(S["rd"], r + 1)
                        v.tensor_tensor(turn[0:HALFP, u % 2, :], bank(u % 2)[HALFP:P, :], sin_t[HALFP:P, cols_],
                                        ALU.mult).then_inc(S["t1"], 1)
                        v.tensor_tensor(turn[HALFP:P, u % 2, :], bank(u % 2)[0:HALFP, :], sin_t[0:HALFP, cols_],
                                        ALU.mult).then_inc(S["t2"], 1)

                    def maximum(h, i):
                        n, b = h * NT + i, i % 2
                        s = bank(2 + 2 * b, 2)
                        v.wait_ge(S["sc"], n + 1)
                        v.tensor_tensor(s[:, i * P:(i + 1) * P], s[:, i * P:(i + 1) * P], causal[:, :],
                                        ALU.add).then_inc(S["msk"], 1)
                        v.wait_ge(S["msk"], n + 1)
                        v.tensor_reduce(nmx[:, b:b + 1], s[:, 0:(i + 1) * P], AX.X, ALU.max,
                                        negate=True).then_inc(S["mx"], 1)

                    def normalise(h, i):
                        n, b = h * NT + i, i % 2
                        v.wait_ge(S["ex"], n + 3)
                        v.reciprocal(rinv[:, b:b + 1], rsum[:, b:b + 1]).then_inc(S["rcp"], 1)
                        v.wait_ge(S["rcp"], n + 1)
                        v.tensor_scalar(pr[:, b, 0:(i + 1) * P], pr[:, b, 0:(i + 1) * P], rinv[:, b:b + 1], None,
                                        ALU.mult).then_inc(S["no"], 1)

                    def turned(h, i):
                        v.wait_ge(S["tw"], h * FOUR + (i - LATE + 3))
                        v.wait_ge(S["pv"], h * NT + (i + 1))
                        w = (i + 1 - FOUR) * P
                        v.tensor_copy(PT[:, i % 2, FOUR * P:(i + 1) * P], bank(i % 2)[:, 0:w]).then_inc(S["tv"], 1)

                    def step(h, j, i, more, loads):
                        normalise(h, i)
                        if i + 1 < NT:
                            maximum(h, i + 1)
                        elif more:
                            maximum(h + 1, 0)
                        if more and i < NU:
                            rotate(h + 1, 1 - j, i)
                        if i >= LATE:
                            turned(h, i)

                    def first():
                        ln_dve(v, S, M, X, XN, 1e-5)
                        v.wait_ge(S["tab"], 32)
                        for u in range(NU):
                            rotate(0, 0, u)
                        maximum(0, 0)
                        step(0, 0, 0, True, 1)

                    def last_step():
                        for t in range(NT):
                            v.wait_ge(S["op"], t + 1)
                            v.tensor_tensor(X[:, t, :], X[:, t, :], bank(2 + t % 2)[:, 0:E], ALU.add).then_inc(S["oa"], 1)

                    heads(v, first, step, last_step)

        topk_ffn("fa", True)
        end_phase()
        mamba()
        end_phase()
        topk_ffn("fb", False)
        end_phase()
        ponder_ffn("pa", False)
        end_phase()
        attention()
        end_phase()
        ponder_ffn("pb", True)


def kernel(**inputs):
    import numpy as np
    import concourse.bacc as bacc
    from concourse.bass_utils import run_bass_kernel_spmd

    def f(name):
        return np.ascontiguousarray(inputs[name])

    def columns(name):
        return f(name).reshape(-1, P).T

    w_in = f("L0_attn_in_proj_w")
    tiles = w_in[:-HM].reshape(-1, P, KT, P).transpose(0, 3, 2, 1)
    w_qkv = np.stack([f("L1_attn_" + n).reshape(KT, P, NH, P).transpose(2, 1, 0, 3) for n in ("wq", "wk", "wv")], axis=2)
    conv = np.concatenate([f("L0_attn_conv_w")[:, 0, :], f("L0_attn_conv_b")[:, None]], axis=1)
    half = P // 2
    freqs = np.power(np.float32(10000.0), -np.arange(half, dtype=np.float32) / np.float32(half))
    rad = (np.arange(T, dtype=np.float32)[:, None] * freqs[None, :]).astype(np.float32).T
    mult = np.sqrt(np.float32(1.0 / 128.0))
    cos, sin = np.cos(rad).astype(np.float32) * mult, np.sin(rad).astype(np.float32) * mult
    arrays = {
        "x": f("L0_attn_x").reshape(T, E),
        "Wr": f("L0_ffn_Wr").reshape(E), "br": f("L0_ffn_br"), "W1": f("L0_ffn_W1"), "b1": columns("L0_ffn_b1"),
        "W2": f("L0_ffn_W2"), "b2": f("L0_ffn_b2"),
        "w_in": np.concatenate([tiles, tiles[:1]]), "w_dt": w_in[-HM:].T,
        "conv": np.concatenate([conv, conv[:P]]),
        "dt_bias": f("L0_attn_dt_bias"), "A_log": f("L0_attn_A_log"), "D": f("L0_attn_D"),
        "norm_w": columns("L0_attn_norm_w"), "w_out": f("L0_attn_out_proj_w").T,
        "w_qkv": w_qkv, "wo": f("L1_attn_wo").reshape(NH * P, E),
        "cos": np.concatenate([cos, cos]), "sin": np.concatenate([sin, -sin]),
        "cols": np.stack([columns(n) for n in ("L1_ffn_in_gamma", "L1_ffn_in_beta", "L1_ffn_pn_gamma",
                                               "L1_ffn_pn_beta")], axis=1),
        "agg_b": f("L1_ffn_agg_b"), "d2_b": f("L1_ffn_d2_b"),
        "d1_b": columns("L1_ffn_d1_b"), "gate_b": f("L1_ffn_gate_b"), "bc_b": f("L1_ffn_bc_b"),
        "out_g": f("L1_ffn_out_gamma"), "out_b": f("L1_ffn_out_beta"),
        "agg_w": f("L1_ffn_agg_w"), "gate_w": f("L1_ffn_gate_w"), "d1_w": f("L1_ffn_d1_w"), "d2_w": f("L1_ffn_d2_w"),
        "bc_w": f("L1_ffn_bc_w"),
    }
    arrays = {n: np.ascontiguousarray(a) for n, a in arrays.items()}
    nc = bacc.Bacc("TRN2", target_bir_lowering=False, num_devices=1)
    A = {n: nc.dram_tensor("in_" + n, a.shape, mybir.dt.from_np(a.dtype), kind="ExternalInput").ap()
         for n, a in arrays.items()}
    A["cum_rows"] = nc.dram_tensor("cum_rows", (HM * NT, P), F32, kind="Internal").ap()
    out = nc.dram_tensor("out_x", (T, E), F32, kind="ExternalOutput").ap()
    build(nc, A, out)
    r = run_bass_kernel_spmd(nc, [{"in_" + n: a for n, a in arrays.items()}], core_ids=[0])
    return r.results[0]["out_x"].reshape(1, T, E)
```
